# Optimizing a Trainium2 kernel written in Bass

```python
import numpy as np
import jax
import jax.numpy as jnp

def _softmax(x, axis=-1):
    return jax.nn.softmax(x, axis=axis)

def _gelu(x):
    return jax.nn.gelu(x, approximate=True)

def _silu(x):
    return jax.nn.silu(x)

def _sigmoid(x):
    return jax.nn.sigmoid(x)

def _layernorm(x, axis=-1, eps=1e-05):
    m = jnp.mean(x, axis=axis, keepdims=True)
    v = jnp.var(x, axis=axis, keepdims=True)
    return (x - m) / jnp.sqrt(v + eps)

def _scatter_add(tgt, idx, src, axis=0):
    return tgt.at[idx].add(src)

def _segment_sum(src, seg, n):
    return jax.ops.segment_sum(src, seg, n)
kernel_name = 'mk_pixart_seq_d4_seqx_r8_dd9f9b'

def setup_inputs(seed: int=0):
    np.random.seed(seed)
    _w = jnp.asarray

    def _rec_inputs():
        import jax
        import jax.numpy as jnp
        _rk = jax.random.key(seed)
        x = -0.0002928 + 1 * jax.random.normal(jax.random.fold_in(_rk, 1), (8, 128, 128), jnp.float32)
        _lenS = 128 - jax.random.randint(jax.random.fold_in(_rk, 7), (8,), 0, max(1, 128 // 4) + 1, jnp.int32)
        _lenS2 = 77 - jax.random.randint(jax.random.fold_in(_rk, 8), (8,), 0, max(1, 77 // 4) + 1, jnp.int32)
        cond_1024 = 0.0061147 + 1.02565 * jax.random.normal(jax.random.fold_in(_rk, 11), (8, 128), jnp.float32)
        _ctx_1024P = jax.random.normal(jax.random.fold_in(_rk, 12), (8, 16, 128), jnp.float32)
        _ctx_1024c = jax.random.dirichlet(jax.random.fold_in(_rk, 512), 0.3 * jnp.ones((16,), jnp.float32), (8, 77))
        _ctx_1024t = jnp.einsum('bsk,bkd->bsd', _ctx_1024c, _ctx_1024P)
        _ctx_1024t = _ctx_1024t * jax.lax.rsqrt(jnp.mean(jnp.square(_ctx_1024t)) + 1e-12) * 0.953939
        ctx_1024 = -0.00265004 + 0.998804 * (_ctx_1024t + 0.3 * jax.random.normal(jax.random.fold_in(_rk, 612), (8, 77, 128), jnp.float32))
        _validS = jnp.arange(128)[None, :] < _lenS[:, None]
        _validS2 = jnp.arange(77)[None, :] < _lenS2[:, None]
        _causal = jnp.tril(jnp.ones((128, 128), dtype=bool))
        mask_BxS2_bf0 = jnp.logical_not(jnp.ones((8, 77), dtype=bool))
        mask_BxS2_bf1 = jnp.ones((8, 77), dtype=bool)
        mask_SxS_bk0 = jnp.logical_not(jnp.broadcast_to(_validS[0:1, :], (128, 128)))
        return (x, cond_1024, ctx_1024, mask_BxS2_bf0, mask_BxS2_bf1, mask_SxS_bk0)
    x, cond_1024, ctx_1024, mask_BxS2_bf0, mask_BxS2_bf1, mask_SxS_bk0 = _rec_inputs()

    def _L0_xcond_setup():
        import jax, jax.numpy as jnp
        import numpy as np
        D, H, B, N, S = (128, 16, 4, 128, 77)
        HD = D // H
        DF = 4 * D
        EPS = 1e-06
        SCALE = HD ** (-0.5)

        def _ln(x):
            m = jnp.mean(x, axis=-1, keepdims=True)
            v = jnp.mean((x - m) ** 2, axis=-1, keepdims=True)
            return (x - m) / jnp.sqrt(v + EPS)
        key = jax.random.key(seed)
        ks = jax.random.split(key, 24)
        s = 0.02
        inp = {'x': jax.random.normal(ks[0], (B, N, D), jnp.float32), 't_emb': jax.random.normal(ks[1], (B, D), jnp.float32), 'context': jax.random.normal(ks[2], (B, S, D), jnp.float32), 'context_mask': jnp.zeros((B, S), jnp.bool_), 'ada_w': jax.random.normal(ks[3], (D, 6 * D), jnp.float32) * s, 'ada_b': jnp.zeros((6 * D,), jnp.float32), 'qkv_w': jax.random.normal(ks[4], (D, 3 * D), jnp.float32) * s, 'qkv_b': jnp.zeros((3 * D,), jnp.float32), 'sa_proj_w': jax.random.normal(ks[5], (D, D), jnp.float32) * s, 'sa_proj_b': jnp.zeros((D,), jnp.float32), 'q_w': jax.random.normal(ks[6], (D, D), jnp.float32) * s, 'q_b': jnp.zeros((D,), jnp.float32), 'kv_w': jax.random.normal(ks[7], (D, 2 * D), jnp.float32) * s, 'kv_b': jnp.zeros((2 * D,), jnp.float32), 'ca_proj_w': jax.random.normal(ks[8], (D, D), jnp.float32) * s, 'ca_proj_b': jnp.zeros((D,), jnp.float32), 'fc1_w': jax.random.normal(ks[9], (D, DF), jnp.float32) * s, 'fc1_b': jnp.zeros((DF,), jnp.float32), 'fc2_w': jax.random.normal(ks[10], (DF, D), jnp.float32) * s, 'fc2_b': jnp.zeros((D,), jnp.float32)}
        return inp
    _L0_xcond_all = _L0_xcond_setup()
    _L0_xcond_in = {k: v for k, v in _L0_xcond_all.items() if k in ('ada_w', 'ada_b', 'qkv_w', 'qkv_b', 'sa_proj_w', 'sa_proj_b', 'q_w', 'q_b', 'kv_w', 'kv_b', 'ca_proj_w', 'ca_proj_b', 'fc1_w', 'fc1_b', 'fc2_w', 'fc2_b')}
    del _L0_xcond_all

    def _L1_xcond_setup():
        import jax, jax.numpy as jnp
        import numpy as np
        C = 128
        H = 16
        D = C // H
        WIN = 64
        SHIFT = 32
        TOPK = 16
        HID = 512
        EPS = 1e-06

        def _ln(x):
            x32 = x.astype(jnp.float32)
            m = x32.mean(-1, keepdims=True)
            v = jnp.mean((x32 - m) ** 2, axis=-1, keepdims=True)
            return ((x32 - m) * jax.lax.rsqrt(v + EPS)).astype(x.dtype)

        def _self_attn(h, w_qkv, b_qkv, w_so, b_so):
            B, L, _ = h.shape
            qkv = h @ w_qkv + b_qkv
            qkv = jnp.roll(qkv, -SHIFT, axis=1)
            nw = L // WIN
            qkv = qkv.reshape(B, nw, WIN, 3, H, D)
            q, k, v = (qkv[:, :, :, 0], qkv[:, :, :, 1], qkv[:, :, :, 2])
            scores = jnp.einsum('bnqhd,bnkhd->bnhqk', q, k) / jnp.sqrt(jnp.float32(D)).astype(h.dtype)
            attn = jax.nn.softmax(scores, axis=-1)
            o = jnp.einsum('bnhqk,bnkhd->bnqhd', attn, v).reshape(B, L, C)
            o = jnp.roll(o, SHIFT, axis=1)
            return o @ w_so + b_so

        def _topk_cross_attn(h, ctx, w_q, b_q, w_kv, b_kv, w_co, b_co):
            B, L, _ = h.shape
            Lc = ctx.shape[1]
            q = (h @ w_q + b_q).reshape(B, L, H, D)
            kv = (ctx @ w_kv + b_kv).reshape(B, Lc, 2, H, D)
            k, v = (kv[:, :, 0], kv[:, :, 1])
            scores = jnp.einsum('bqhd,bkhd->bhqk', q, k) / jnp.sqrt(jnp.float32(D)).astype(h.dtype)
            top_s, top_i = jax.lax.top_k(scores, TOPK)
            attn = jax.nn.softmax(top_s, axis=-1)
            v_bh = jnp.transpose(v, (0, 2, 1, 3))
            vg = jnp.take_along_axis(v_bh[:, :, None, :, :], top_i[..., None], axis=3)
            o = jnp.einsum('bhqk,bhqkd->bqhd', attn, vg).reshape(B, L, C)
            return o @ w_co + b_co

        def _swiglu(h, w_m1, b_m1, w_m2, b_m2):
            u = h @ w_m1 + b_m1
            a, b = (u[..., :HID], u[..., HID:])
            return jax.nn.silu(a) * b @ w_m2 + b_m2
        key = jax.random.key(seed)
        ks = jax.random.split(key, 24)
        s = 0.02
        inp = {'x': jax.random.normal(ks[0], (2, 512, C), jnp.float32), 'mod': jax.random.normal(ks[1], (2, C), jnp.float32), 'context': jax.random.normal(ks[2], (2, 128, C), jnp.float32), 'w_ada': jax.random.normal(ks[3], (C, 9 * C), jnp.float32) * s, 'b_ada': jnp.zeros((9 * C,), jnp.float32), 'w_qkv': jax.random.normal(ks[4], (C, 3 * C), jnp.float32) * s, 'b_qkv': jnp.zeros((3 * C,), jnp.float32), 'w_so': jax.random.normal(ks[5], (C, C), jnp.float32) * s, 'b_so': jnp.zeros((C,), jnp.float32), 'w_q': jax.random.normal(ks[6], (C, C), jnp.float32) * s, 'b_q': jnp.zeros((C,), jnp.float32), 'w_kv': jax.random.normal(ks[7], (C, 2 * C), jnp.float32) * s, 'b_kv': jnp.zeros((2 * C,), jnp.float32), 'w_co': jax.random.normal(ks[8], (C, C), jnp.float32) * s, 'b_co': jnp.zeros((C,), jnp.float32), 'w_m1': jax.random.normal(ks[9], (C, 2 * HID), jnp.float32) * s, 'b_m1': jnp.zeros((2 * HID,), jnp.float32), 'w_m2': jax.random.normal(ks[10], (HID, C), jnp.float32) * s, 'b_m2': jnp.zeros((C,), jnp.float32)}
        return inp
    _L1_xcond_all = _L1_xcond_setup()
    _L1_xcond_in = {k: v for k, v in _L1_xcond_all.items() if k in ('w_ada', 'b_ada', 'w_qkv', 'b_qkv', 'w_so', 'b_so', 'w_q', 'b_q', 'w_kv', 'b_kv', 'w_co', 'b_co', 'w_m1', 'b_m1', 'w_m2', 'b_m2')}
    del _L1_xcond_all

    def _L2_xcond_setup():
        import jax, jax.numpy as jnp
        import numpy as np
        B, N, D, H, LC = (2, 128, 128, 16, 77)
        HD = D // H
        BLOCK = 16
        ROPE_BASE = 10000.0
        EPS = 1e-05

        def _block_diff_mask(n, block_size):
            idx = np.arange(2 * n)
            q = idx[:, None]
            kv = idx[None, :]
            fq = q >= n
            fkv = kv >= n
            bq = np.where(fq, (q - n) // block_size, q // block_size)
            bkv = np.where(fkv, (kv - n) // block_size, kv // block_size)
            block_diagonal = (bq == bkv) & (fq == fkv)
            offset_block_causal = (bq > bkv) & fkv & ~fq
            block_causal = (bq >= bkv) & fq & fkv
            return jnp.asarray(block_diagonal | offset_block_causal | block_causal)

        def _rope_tables(n):
            inv_freq = 1.0 / ROPE_BASE ** (np.arange(0, HD, 2, dtype=np.float32) / HD)
            freqs = np.outer(np.arange(n, dtype=np.float32), inv_freq)
            emb = np.concatenate([freqs, freqs], axis=-1)
            cos = jnp.asarray(np.cos(emb), jnp.float32)[None, :, None, :]
            sin = jnp.asarray(np.sin(emb), jnp.float32)[None, :, None, :]
            return (cos, sin)

        def _ln(x, w):
            xf = x.astype(jnp.float32)
            mu = jnp.mean(xf, axis=-1, keepdims=True)
            var = jnp.mean(jnp.square(xf - mu), axis=-1, keepdims=True)
            y = (xf - mu) * jax.lax.rsqrt(var + EPS)
            return y * w[None, None, :]

        def _apply_rope(t, cos, sin):
            t1, t2 = jnp.split(t, 2, axis=-1)
            rot = jnp.concatenate([-t2, t1], axis=-1)
            return t * cos + rot * sin

        def _attn(q, k, v, mask):
            scale = 1.0 / np.sqrt(HD)
            s = jnp.einsum('bqhd,bkhd->bhqk', q, k) * scale
            s = jnp.where(mask, s, jnp.finfo(s.dtype).min)
            a = jax.nn.softmax(s, axis=-1)
            return jnp.einsum('bhqk,bkhd->bqhd', a, v)
        key = jax.random.key(seed)
        ks = jax.random.split(key, 16)
        w = lambda k, shp: jax.random.normal(k, shp, jnp.float32) * 0.02
        inp = {'x': jax.random.normal(ks[0], (B, 2 * N, D), jnp.float32), 'cond_global': jax.random.normal(ks[1], (B, D), jnp.float32), 'cond_tokens': jax.random.normal(ks[2], (B, LC, D), jnp.float32), 'adaLN_W': w(ks[3], (D, 9 * D)), 'adaLN_b': w(ks[4], (9 * D,)), 'norm1_w': jnp.ones((D,), jnp.float32), 'qkv_W': w(ks[5], (D, 3 * D)), 'attn_out_W': w(ks[6], (D, D)), 'normc_w': jnp.ones((D,), jnp.float32), 'cq_W': w(ks[7], (D, D)), 'ck_W': w(ks[8], (D, D)), 'cv_W': w(ks[9], (D, D)), 'co_W': w(ks[10], (D, D)), 'norm2_w': jnp.ones((D,), jnp.float32), 'mlp_W1': w(ks[11], (D, 4 * D)), 'mlp_b1': w(ks[12], (4 * D,)), 'mlp_W2': w(ks[13], (4 * D, D)), 'mlp_b2': w(ks[14], (D,)), 'cond_kv_mask': jnp.ones((B, LC), bool), 'attn_mask': _block_diff_mask(N, BLOCK)}
        return inp
    _L2_xcond_all = _L2_xcond_setup()
    _L2_xcond_in = {k: v for k, v in _L2_xcond_all.items() if k in ('adaLN_W', 'adaLN_b', 'norm1_w', 'qkv_W', 'attn_out_W', 'normc_w', 'cq_W', 'ck_W', 'cv_W', 'co_W', 'norm2_w', 'mlp_W1', 'mlp_b1', 'mlp_W2', 'mlp_b2')}
    del _L2_xcond_all

    def _L3_xcond_setup():
        import jax, jax.numpy as jnp
        import numpy as np
        H = 128
        RH = 2 * H
        E = 3
        B, T, P = (8, 256, 64)
        LN_EPS = 1e-05

        def _layer_norm(x, gamma, beta):
            mu = jnp.mean(x, axis=-1, keepdims=True)
            var = jnp.mean(jnp.square(x - mu), axis=-1, keepdims=True)
            return (x - mu) * jax.lax.rsqrt(var + LN_EPS) * gamma + beta
        key = jax.random.key(seed)
        ks = jax.random.split(key, 24)
        s = lambda fan_in: 1.0 / np.sqrt(fan_in)
        inp = {'mix_hidden_states': jax.random.normal(ks[0], (B, T, H), jnp.float32), 'global_anchor': jax.random.normal(ks[1], (B, H), jnp.float32), 'prototype_bank': jax.random.normal(ks[2], (B, P, H), jnp.float32), 'ln_gamma': jnp.ones((H,), jnp.float32), 'ln_beta': jnp.zeros((H,), jnp.float32), 'Wq': jax.random.normal(ks[3], (H, H), jnp.float32) * s(H), 'Wk': jax.random.normal(ks[4], (H, H), jnp.float32) * s(H), 'Wv': jax.random.normal(ks[5], (H, H), jnp.float32) * s(H), 'router_W': jax.random.normal(ks[6], (3 * H, E), jnp.float32) * s(3 * H), 'router_b': jnp.zeros((E,), jnp.float32), 'e_w1': jax.random.normal(ks[7], (E, 3 * H, RH), jnp.float32) * s(3 * H), 'e_b1': jnp.zeros((E, RH), jnp.float32), 'e_w2': jax.random.normal(ks[8], (E, RH, H), jnp.float32) * s(RH), 'e_b2': jnp.zeros((E, H), jnp.float32), 'gate_w1': jax.random.normal(ks[9], (3 * H, H), jnp.float32) * s(3 * H), 'gate_b1': jnp.zeros((H,), jnp.float32), 'gate_w2': jax.random.normal(ks[10], (H, H), jnp.float32) * s(H), 'gate_b2': jnp.zeros((H,), jnp.float32), 'out_w': jax.random.normal(ks[11], (H, H), jnp.float32) * s(H), 'out_b': jnp.zeros((H,), jnp.float32)}
        return inp
    _L3_xcond_all = _L3_xcond_setup()
    _L3_xcond_in = {k: v for k, v in _L3_xcond_all.items() if k in ('ln_gamma', 'ln_beta', 'Wq', 'Wk', 'Wv', 'router_W', 'router_b', 'e_w1', 'e_b1', 'e_w2', 'e_b2', 'gate_w1', 'gate_b1', 'gate_w2', 'gate_b2', 'out_w', 'out_b')}
    del _L3_xcond_all
    return {'x': x, 'cond_1024': cond_1024, 'ctx_1024': ctx_1024, 'mask_BxS2_bf0': mask_BxS2_bf0, 'mask_BxS2_bf1': mask_BxS2_bf1, 'mask_SxS_bk0': mask_SxS_bk0, 'L0_xcond_ada_w': _L0_xcond_in['ada_w'], 'L0_xcond_ada_b': _L0_xcond_in['ada_b'], 'L0_xcond_qkv_w': _L0_xcond_in['qkv_w'], 'L0_xcond_qkv_b': _L0_xcond_in['qkv_b'], 'L0_xcond_sa_proj_w': _L0_xcond_in['sa_proj_w'], 'L0_xcond_sa_proj_b': _L0_xcond_in['sa_proj_b'], 'L0_xcond_q_w': _L0_xcond_in['q_w'], 'L0_xcond_q_b': _L0_xcond_in['q_b'], 'L0_xcond_kv_w': _L0_xcond_in['kv_w'], 'L0_xcond_kv_b': _L0_xcond_in['kv_b'], 'L0_xcond_ca_proj_w': _L0_xcond_in['ca_proj_w'], 'L0_xcond_ca_proj_b': _L0_xcond_in['ca_proj_b'], 'L0_xcond_fc1_w': _L0_xcond_in['fc1_w'], 'L0_xcond_fc1_b': _L0_xcond_in['fc1_b'], 'L0_xcond_fc2_w': _L0_xcond_in['fc2_w'], 'L0_xcond_fc2_b': _L0_xcond_in['fc2_b'], 'L1_xcond_w_ada': _L1_xcond_in['w_ada'], 'L1_xcond_b_ada': _L1_xcond_in['b_ada'], 'L1_xcond_w_qkv': _L1_xcond_in['w_qkv'], 'L1_xcond_b_qkv': _L1_xcond_in['b_qkv'], 'L1_xcond_w_so': _L1_xcond_in['w_so'], 'L1_xcond_b_so': _L1_xcond_in['b_so'], 'L1_xcond_w_q': _L1_xcond_in['w_q'], 'L1_xcond_b_q': _L1_xcond_in['b_q'], 'L1_xcond_w_kv': _L1_xcond_in['w_kv'], 'L1_xcond_b_kv': _L1_xcond_in['b_kv'], 'L1_xcond_w_co': _L1_xcond_in['w_co'], 'L1_xcond_b_co': _L1_xcond_in['b_co'], 'L1_xcond_w_m1': _L1_xcond_in['w_m1'], 'L1_xcond_b_m1': _L1_xcond_in['b_m1'], 'L1_xcond_w_m2': _L1_xcond_in['w_m2'], 'L1_xcond_b_m2': _L1_xcond_in['b_m2'], 'L2_xcond_adaLN_W': _L2_xcond_in['adaLN_W'], 'L2_xcond_adaLN_b': _L2_xcond_in['adaLN_b'], 'L2_xcond_norm1_w': _L2_xcond_in['norm1_w'], 'L2_xcond_qkv_W': _L2_xcond_in['qkv_W'], 'L2_xcond_attn_out_W': _L2_xcond_in['attn_out_W'], 'L2_xcond_normc_w': _L2_xcond_in['normc_w'], 'L2_xcond_cq_W': _L2_xcond_in['cq_W'], 'L2_xcond_ck_W': _L2_xcond_in['ck_W'], 'L2_xcond_cv_W': _L2_xcond_in['cv_W'], 'L2_xcond_co_W': _L2_xcond_in['co_W'], 'L2_xcond_norm2_w': _L2_xcond_in['norm2_w'], 'L2_xcond_mlp_W1': _L2_xcond_in['mlp_W1'], 'L2_xcond_mlp_b1': _L2_xcond_in['mlp_b1'], 'L2_xcond_mlp_W2': _L2_xcond_in['mlp_W2'], 'L2_xcond_mlp_b2': _L2_xcond_in['mlp_b2'], 'L3_xcond_ln_gamma': _L3_xcond_in['ln_gamma'], 'L3_xcond_ln_beta': _L3_xcond_in['ln_beta'], 'L3_xcond_Wq': _L3_xcond_in['Wq'], 'L3_xcond_Wk': _L3_xcond_in['Wk'], 'L3_xcond_Wv': _L3_xcond_in['Wv'], 'L3_xcond_router_W': _L3_xcond_in['router_W'], 'L3_xcond_router_b': _L3_xcond_in['router_b'], 'L3_xcond_e_w1': _L3_xcond_in['e_w1'], 'L3_xcond_e_b1': _L3_xcond_in['e_b1'], 'L3_xcond_e_w2': _L3_xcond_in['e_w2'], 'L3_xcond_e_b2': _L3_xcond_in['e_b2'], 'L3_xcond_gate_w1': _L3_xcond_in['gate_w1'], 'L3_xcond_gate_b1': _L3_xcond_in['gate_b1'], 'L3_xcond_gate_w2': _L3_xcond_in['gate_w2'], 'L3_xcond_gate_b2': _L3_xcond_in['gate_b2'], 'L3_xcond_out_w': _L3_xcond_in['out_w'], 'L3_xcond_out_b': _L3_xcond_in['out_b']}

def reference(x, cond_1024, ctx_1024, mask_BxS2_bf0, mask_BxS2_bf1, mask_SxS_bk0, L0_xcond_ada_w, L0_xcond_ada_b, L0_xcond_qkv_w, L0_xcond_qkv_b, L0_xcond_sa_proj_w, L0_xcond_sa_proj_b, L0_xcond_q_w, L0_xcond_q_b, L0_xcond_kv_w, L0_xcond_kv_b, L0_xcond_ca_proj_w, L0_xcond_ca_proj_b, L0_xcond_fc1_w, L0_xcond_fc1_b, L0_xcond_fc2_w, L0_xcond_fc2_b, L1_xcond_w_ada, L1_xcond_b_ada, L1_xcond_w_qkv, L1_xcond_b_qkv, L1_xcond_w_so, L1_xcond_b_so, L1_xcond_w_q, L1_xcond_b_q, L1_xcond_w_kv, L1_xcond_b_kv, L1_xcond_w_co, L1_xcond_b_co, L1_xcond_w_m1, L1_xcond_b_m1, L1_xcond_w_m2, L1_xcond_b_m2, L2_xcond_adaLN_W, L2_xcond_adaLN_b, L2_xcond_norm1_w, L2_xcond_qkv_W, L2_xcond_attn_out_W, L2_xcond_normc_w, L2_xcond_cq_W, L2_xcond_ck_W, L2_xcond_cv_W, L2_xcond_co_W, L2_xcond_norm2_w, L2_xcond_mlp_W1, L2_xcond_mlp_b1, L2_xcond_mlp_W2, L2_xcond_mlp_b2, L3_xcond_ln_gamma, L3_xcond_ln_beta, L3_xcond_Wq, L3_xcond_Wk, L3_xcond_Wv, L3_xcond_router_W, L3_xcond_router_b, L3_xcond_e_w1, L3_xcond_e_b1, L3_xcond_e_w2, L3_xcond_e_b2, L3_xcond_gate_w1, L3_xcond_gate_b1, L3_xcond_gate_w2, L3_xcond_gate_b2, L3_xcond_out_w, L3_xcond_out_b):
    import jax
    import jax.numpy as jnp

    def _L0_xcond_ref(x, t_emb, context, context_mask, ada_w, ada_b, qkv_w, qkv_b, sa_proj_w, sa_proj_b, q_w, q_b, kv_w, kv_b, ca_proj_w, ca_proj_b, fc1_w, fc1_b, fc2_w, fc2_b):
        import jax, jax.numpy as jnp
        import numpy as np
        D, H, B, N, S = (128, 16, 4, 128, 77)
        HD = D // H
        DF = 4 * D
        EPS = 1e-06
        SCALE = HD ** (-0.5)

        def _ln(x):
            m = jnp.mean(x, axis=-1, keepdims=True)
            v = jnp.mean((x - m) ** 2, axis=-1, keepdims=True)
            return (x - m) / jnp.sqrt(v + EPS)
        Bx, Nx, C = x.shape
        Sx = context.shape[1]
        mod = jax.nn.silu(t_emb) @ ada_w + ada_b
        shift_sa, scale_sa, gate_sa, shift_ff, scale_ff, gate_ff = [m[:, None, :] for m in jnp.split(mod, 6, axis=-1)]
        xm1 = _ln(x) * (1 + scale_sa) + shift_sa
        qkv = (xm1 @ qkv_w + qkv_b).reshape(Bx, Nx, 3, H, HD)
        q, k, v = (qkv[:, :, 0], qkv[:, :, 1], qkv[:, :, 2])
        attn = jnp.einsum('bnhd,bmhd->bhnm', q, k) * SCALE
        attn = jax.nn.softmax(attn, axis=-1)
        sa = jnp.einsum('bhnm,bmhd->bnhd', attn, v).reshape(Bx, Nx, C)
        sa = sa @ sa_proj_w + sa_proj_b
        x = x + gate_sa * sa
        xn2 = _ln(x)
        qc = (xn2 @ q_w + q_b).reshape(Bx, Nx, H, HD)
        kvc = (context @ kv_w + kv_b).reshape(Bx, Sx, 2, H, HD)
        kc, vc = (kvc[:, :, 0], kvc[:, :, 1])
        attn_c = jnp.einsum('bnhd,bshd->bhns', qc, kc) * SCALE
        attn_c = jnp.where(context_mask[:, None, None, :], -jnp.inf, attn_c)
        attn_c = jax.nn.softmax(attn_c, axis=-1)
        ca = jnp.einsum('bhns,bshd->bnhd', attn_c, vc).reshape(Bx, Nx, C)
        ca = ca @ ca_proj_w + ca_proj_b
        x = x + ca
        xm3 = _ln(x) * (1 + scale_ff) + shift_ff
        h = jax.nn.gelu(xm3 @ fc1_w + fc1_b, approximate=False)
        ff = h @ fc2_w + fc2_b
        x = x + gate_ff * ff
        return x

    def _L1_xcond_ref(x, mod, context, w_ada, b_ada, w_qkv, b_qkv, w_so, b_so, w_q, b_q, w_kv, b_kv, w_co, b_co, w_m1, b_m1, w_m2, b_m2):
        import jax, jax.numpy as jnp
        import numpy as np
        C = 128
        H = 16
        D = C // H
        WIN = 64
        SHIFT = 32
        TOPK = 16
        HID = 512
        EPS = 1e-06

        def _ln(x):
            x32 = x.astype(jnp.float32)
            m = x32.mean(-1, keepdims=True)
            v = jnp.mean((x32 - m) ** 2, axis=-1, keepdims=True)
            return ((x32 - m) * jax.lax.rsqrt(v + EPS)).astype(x.dtype)

        def _self_attn(h, w_qkv, b_qkv, w_so, b_so):
            B, L, _ = h.shape
            qkv = h @ w_qkv + b_qkv
            qkv = jnp.roll(qkv, -SHIFT, axis=1)
            nw = L // WIN
            qkv = qkv.reshape(B, nw, WIN, 3, H, D)
            q, k, v = (qkv[:, :, :, 0], qkv[:, :, :, 1], qkv[:, :, :, 2])
            scores = jnp.einsum('bnqhd,bnkhd->bnhqk', q, k) / jnp.sqrt(jnp.float32(D)).astype(h.dtype)
            attn = jax.nn.softmax(scores, axis=-1)
            o = jnp.einsum('bnhqk,bnkhd->bnqhd', attn, v).reshape(B, L, C)
            o = jnp.roll(o, SHIFT, axis=1)
            return o @ w_so + b_so

        def _topk_cross_attn(h, ctx, w_q, b_q, w_kv, b_kv, w_co, b_co):
            B, L, _ = h.shape
            Lc = ctx.shape[1]
            q = (h @ w_q + b_q).reshape(B, L, H, D)
            kv = (ctx @ w_kv + b_kv).reshape(B, Lc, 2, H, D)
            k, v = (kv[:, :, 0], kv[:, :, 1])
            scores = jnp.einsum('bqhd,bkhd->bhqk', q, k) / jnp.sqrt(jnp.float32(D)).astype(h.dtype)
            top_s, top_i = jax.lax.top_k(scores, TOPK)
            attn = jax.nn.softmax(top_s, axis=-1)
            v_bh = jnp.transpose(v, (0, 2, 1, 3))
            vg = jnp.take_along_axis(v_bh[:, :, None, :, :], top_i[..., None], axis=3)
            o = jnp.einsum('bhqk,bhqkd->bqhd', attn, vg).reshape(B, L, C)
            return o @ w_co + b_co

        def _swiglu(h, w_m1, b_m1, w_m2, b_m2):
            u = h @ w_m1 + b_m1
            a, b = (u[..., :HID], u[..., HID:])
            return jax.nn.silu(a) * b @ w_m2 + b_m2
        m = jax.nn.silu(mod) @ w_ada + b_ada
        sh_msa, sc_msa, g_msa, sh_mca, sc_mca, g_mca, sh_mlp, sc_mlp, g_mlp = [m[:, i * C:(i + 1) * C][:, None, :] for i in range(9)]
        h = _ln(x) * (1 + sc_msa) + sh_msa
        h = _self_attn(h, w_qkv, b_qkv, w_so, b_so)
        x = x + h * g_msa
        h = _ln(x) * (1 + sc_mca) + sh_mca
        h = _topk_cross_attn(h, context, w_q, b_q, w_kv, b_kv, w_co, b_co)
        x = x + h * g_mca
        h = _ln(x) * (1 + sc_mlp) + sh_mlp
        h = _swiglu(h, w_m1, b_m1, w_m2, b_m2)
        x = x + h * g_mlp
        return x

    def _L2_xcond_ref(x, cond_global, cond_tokens, adaLN_W, adaLN_b, norm1_w, qkv_W, attn_out_W, normc_w, cq_W, ck_W, cv_W, co_W, norm2_w, mlp_W1, mlp_b1, mlp_W2, mlp_b2, cond_kv_mask, attn_mask):
        import jax, jax.numpy as jnp
        import numpy as np
        B, N, D, H, LC = (2, 128, 128, 16, 77)
        HD = D // H
        BLOCK = 16
        ROPE_BASE = 10000.0
        EPS = 1e-05

        def _block_diff_mask(n, block_size):
            idx = np.arange(2 * n)
            q = idx[:, None]
            kv = idx[None, :]
            fq = q >= n
            fkv = kv >= n
            bq = np.where(fq, (q - n) // block_size, q // block_size)
            bkv = np.where(fkv, (kv - n) // block_size, kv // block_size)
            block_diagonal = (bq == bkv) & (fq == fkv)
            offset_block_causal = (bq > bkv) & fkv & ~fq
            block_causal = (bq >= bkv) & fq & fkv
            return jnp.asarray(block_diagonal | offset_block_causal | block_causal)

        def _rope_tables(n):
            inv_freq = 1.0 / ROPE_BASE ** (np.arange(0, HD, 2, dtype=np.float32) / HD)
            freqs = np.outer(np.arange(n, dtype=np.float32), inv_freq)
            emb = np.concatenate([freqs, freqs], axis=-1)
            cos = jnp.asarray(np.cos(emb), jnp.float32)[None, :, None, :]
            sin = jnp.asarray(np.sin(emb), jnp.float32)[None, :, None, :]
            return (cos, sin)

        def _ln(x, w):
            xf = x.astype(jnp.float32)
            mu = jnp.mean(xf, axis=-1, keepdims=True)
            var = jnp.mean(jnp.square(xf - mu), axis=-1, keepdims=True)
            y = (xf - mu) * jax.lax.rsqrt(var + EPS)
            return y * w[None, None, :]

        def _apply_rope(t, cos, sin):
            t1, t2 = jnp.split(t, 2, axis=-1)
            rot = jnp.concatenate([-t2, t1], axis=-1)
            return t * cos + rot * sin

        def _attn(q, k, v, mask):
            scale = 1.0 / np.sqrt(HD)
            s = jnp.einsum('bqhd,bkhd->bhqk', q, k) * scale
            s = jnp.where(mask, s, jnp.finfo(s.dtype).min)
            a = jax.nn.softmax(s, axis=-1)
            return jnp.einsum('bhqk,bkhd->bqhd', a, v)
        b, s, d = x.shape
        n = s // 2
        mod = (cond_global @ adaLN_W + adaLN_b)[:, None, :]
        sh_msa, sc_msa, g_msa, sh_x, sc_x, g_x, sh_mlp, sc_mlp, g_mlp = jnp.split(mod, 9, axis=-1)
        x_norm = _ln(x, norm1_w) * (1 + sc_msa) + sh_msa
        cos, sin = _rope_tables(n)

        def qkv(h):
            t = (h @ qkv_W).reshape(b, n, 3, H, HD)
            q, k, v = (t[:, :, 0], t[:, :, 1], t[:, :, 2])
            return (_apply_rope(q, cos, sin), _apply_rope(k, cos, sin), v)
        q1, k1, v1 = qkv(x_norm[:, :n])
        q2, k2, v2 = qkv(x_norm[:, n:])
        q = jnp.concatenate([q1, q2], axis=1)
        k = jnp.concatenate([k1, k2], axis=1)
        v = jnp.concatenate([v1, v2], axis=1)
        self_out = _attn(q, k, v, attn_mask[None, None]).reshape(b, s, d) @ attn_out_W
        x = x + g_msa * self_out
        xc = _ln(x, normc_w) * (1 + sc_x) + sh_x
        qc = (xc @ cq_W).reshape(b, s, H, HD)
        kc = (cond_tokens @ ck_W).reshape(b, LC, H, HD)
        vc = (cond_tokens @ cv_W).reshape(b, LC, H, HD)
        cross = _attn(qc, kc, vc, cond_kv_mask[:, None, None, :]).reshape(b, s, d) @ co_W
        x = x + g_x * cross
        xm = _ln(x, norm2_w) * (1 + sc_mlp) + sh_mlp
        h = jax.nn.gelu(xm @ mlp_W1 + mlp_b1, approximate=True)
        mlp_out = h @ mlp_W2 + mlp_b2
        return x + g_mlp * mlp_out

    def _L3_xcond_ref(mix_hidden_states, global_anchor, prototype_bank, ln_gamma, ln_beta, Wq, Wk, Wv, router_W, router_b, e_w1, e_b1, e_w2, e_b2, gate_w1, gate_b1, gate_w2, gate_b2, out_w, out_b):
        import jax, jax.numpy as jnp
        import numpy as np
        H = 128
        RH = 2 * H
        E = 3
        B, T, P = (8, 256, 64)
        LN_EPS = 1e-05

        def _layer_norm(x, gamma, beta):
            mu = jnp.mean(x, axis=-1, keepdims=True)
            var = jnp.mean(jnp.square(x - mu), axis=-1, keepdims=True)
            return (x - mu) * jax.lax.rsqrt(var + LN_EPS) * gamma + beta
        x = mix_hidden_states
        nx = _layer_norm(x, ln_gamma, ln_beta)
        q = nx @ Wq
        k = prototype_bank @ Wk
        v = prototype_bank @ Wv
        scores = jnp.einsum('bth,bph->btp', q, k) * H ** (-0.5)
        weights = jax.nn.softmax(scores, axis=-1)
        evidence = jnp.einsum('btp,bph->bth', weights, v)
        anchor = jnp.broadcast_to(global_anchor[:, None, :], nx.shape)
        combined = jnp.concatenate([nx, evidence, anchor], axis=-1)
        router_logits = combined @ router_W + router_b
        router_probs = jax.nn.softmax(router_logits, axis=-1)
        h = jax.nn.silu(jnp.einsum('btc,ecr->bter', combined, e_w1) + e_b1)
        expert_out = jnp.einsum('bter,erh->bteh', h, e_w2) + e_b2
        routed = jnp.sum(expert_out * router_probs[..., None], axis=-2)
        g = jax.nn.sigmoid(jax.nn.silu(combined @ gate_w1 + gate_b1) @ gate_w2 + gate_b2)
        refined_delta = g * (routed @ out_w + out_b)
        return x + refined_delta
    x = _L0_xcond_ref(x, cond_1024, ctx_1024, mask_BxS2_bf0, L0_xcond_ada_w, L0_xcond_ada_b, L0_xcond_qkv_w, L0_xcond_qkv_b, L0_xcond_sa_proj_w, L0_xcond_sa_proj_b, L0_xcond_q_w, L0_xcond_q_b, L0_xcond_kv_w, L0_xcond_kv_b, L0_xcond_ca_proj_w, L0_xcond_ca_proj_b, L0_xcond_fc1_w, L0_xcond_fc1_b, L0_xcond_fc2_w, L0_xcond_fc2_b)
    x = _L1_xcond_ref(x, cond_1024, ctx_1024, L1_xcond_w_ada, L1_xcond_b_ada, L1_xcond_w_qkv, L1_xcond_b_qkv, L1_xcond_w_so, L1_xcond_b_so, L1_xcond_w_q, L1_xcond_b_q, L1_xcond_w_kv, L1_xcond_b_kv, L1_xcond_w_co, L1_xcond_b_co, L1_xcond_w_m1, L1_xcond_b_m1, L1_xcond_w_m2, L1_xcond_b_m2)
    x = _L2_xcond_ref(x, cond_1024, ctx_1024, L2_xcond_adaLN_W, L2_xcond_adaLN_b, L2_xcond_norm1_w, L2_xcond_qkv_W, L2_xcond_attn_out_W, L2_xcond_normc_w, L2_xcond_cq_W, L2_xcond_ck_W, L2_xcond_cv_W, L2_xcond_co_W, L2_xcond_norm2_w, L2_xcond_mlp_W1, L2_xcond_mlp_b1, L2_xcond_mlp_W2, L2_xcond_mlp_b2, mask_BxS2_bf1, mask_SxS_bk0)
    x = _L3_xcond_ref(x, cond_1024, ctx_1024, L3_xcond_ln_gamma, L3_xcond_ln_beta, L3_xcond_Wq, L3_xcond_Wk, L3_xcond_Wv, L3_xcond_router_W, L3_xcond_router_b, L3_xcond_e_w1, L3_xcond_e_b1, L3_xcond_e_w2, L3_xcond_e_b2, L3_xcond_gate_w1, L3_xcond_gate_b1, L3_xcond_gate_w2, L3_xcond_gate_b2, L3_xcond_out_w, L3_xcond_out_b)
    return x

_drawn_inputs = setup_inputs


def setup_inputs(seed=0):
    import zlib

    import numpy as np

    out = dict(_drawn_inputs(seed))
    spreads = {'L0_xcond_ada_b': (0.0, 0.46),
     'L0_xcond_qkv_b': (0.0, 0.8),
     'L0_xcond_sa_proj_b': (0.0, 0.411),
     'L0_xcond_q_b': (0.0, 2.0),
     'L0_xcond_kv_b': (0.0, 0.361),
     'L0_xcond_ca_proj_b': (0.0, 0.1),
     'L0_xcond_fc1_b': (0.0, 0.8),
     'L0_xcond_fc2_b': (0.0, 0.516),
     'L1_xcond_b_ada': (0.0, 0.572),
     'L1_xcond_b_qkv': (0.0, 0.8),
     'L1_xcond_b_so': (0.0, 0.527),
     'L1_xcond_b_q': (0.0, 0.8),
     'L1_xcond_b_kv': (0.0, 0.8),
     'L1_xcond_b_co': (0.0, 0.505),
     'L1_xcond_b_m1': (0.0, 0.8),
     'L1_xcond_b_m2': (0.0, 1.612),
     'L2_xcond_norm1_w': (1.0, 0.6),
     'L2_xcond_normc_w': (1.0, 0.6),
     'L2_xcond_norm2_w': (1.0, 0.6),
     'L3_xcond_ln_gamma': (1.0, 0.6),
     'L3_xcond_ln_beta': (0.0, 2.0),
     'L3_xcond_router_b': (0.0, 2.0),
     'L3_xcond_e_b1': (0.0, 2.0),
     'L3_xcond_e_b2': (0.0, 0.8),
     'L3_xcond_gate_b1': (0.0, 2.0),
     'L3_xcond_gate_b2': (0.0, 2.0),
     'L3_xcond_out_b': (0.0, 0.8)}
    factors = {'L0_xcond_qkv_w': 8.0,
     'L0_xcond_sa_proj_w': 8.0,
     'L0_xcond_q_w': 64.0,
     'L0_xcond_fc1_w': 6.339,
     'L0_xcond_fc2_w': 5.739,
     'L1_xcond_w_qkv': 8.0,
     'L1_xcond_w_so': 8.0,
     'L1_xcond_w_q': 8.0,
     'L1_xcond_w_kv': 8.0,
     'L1_xcond_w_co': 8.0,
     'L1_xcond_w_m1': 8.0,
     'L1_xcond_w_m2': 8.0,
     'L2_xcond_adaLN_W': 3.311,
     'L2_xcond_adaLN_b': 8.0,
     'L2_xcond_qkv_W': 6.065,
     'L2_xcond_attn_out_W': 6.382,
     'L2_xcond_cq_W': 8.0,
     'L2_xcond_ck_W': 8.0,
     'L2_xcond_cv_W': 8.0,
     'L2_xcond_co_W': 8.0,
     'L2_xcond_mlp_W1': 4.398,
     'L2_xcond_mlp_b1': 30.368,
     'L2_xcond_mlp_W2': 4.26,
     'L2_xcond_mlp_b2': 44.33,
     'L0_xcond_kv_w': 2.838,
     'L3_xcond_Wq': 8.0,
     'L3_xcond_Wk': 8.0,
     'L3_xcond_Wv': 6.364,
     'L3_xcond_router_W': 4.411,
     'L3_xcond_e_w1': 2.793,
     'L3_xcond_gate_w1': 8.0,
     'L3_xcond_gate_w2': 8.0}
    for name, (base, spread) in spreads.items():
        noise = np.random.default_rng([zlib.crc32(name.encode()), seed]).standard_normal(out[name].shape)
        drawn = base * np.exp(spread * noise) if base else spread * noise
        out[name] = jnp.asarray(drawn.astype(out[name].dtype))
    for name, factor in factors.items():
        out[name] = (out[name] * factor).astype(out[name].dtype)
    return out
```

```python
from contextlib import ExitStack

import numpy as np

import concourse.bass as bass
from concourse import mybir

P = 128
NB = 8
H, HD = 16, 8
NC = 77
CH = 4
NCH = H // CH
TOPK = 16
HID = 4
NE = 3
NEG = -float(2 ** 100)
REPLACED = -3.0e38
SCALE = float(HD) ** -0.5
SCALE3 = float(P) ** -0.5

SELF, CROSS, TOP, ROPE, GELU, GLU, GELUT, PROTO, EXPERTS = (
    "self", "cross", "top", "rope", "gelu", "glu", "gelut", "proto", "experts")
PHASES = [SELF, CROSS, GELU, SELF, TOP, GLU, ROPE, CROSS, GELUT, PROTO, EXPERTS]
LAYER = [0, 0, 0, 1, 1, 1, 2, 2, 2, 3, 3]
HEADS = (SELF, CROSS, TOP, ROPE)
MLPS = (GELU, GLU, GELUT)
CTX = (CROSS, TOP, PROTO)
EPS = [1e-6, 1e-6, 1e-5, 1e-5]

WEIGHTS = [
    [("ada", 768), ("qkv", 384), ("so", 128), ("q", 128), ("kv", 256), ("co", 128), ("m1", 512), ("m2", 512)],
    [("ada", 1152), ("qkv", 384), ("so", 128), ("q", 128), ("kv", 256), ("co", 128), ("m1", 1024), ("m2", 512)],
    [("ada", 1152), ("qkv", 384), ("so", 128), ("q", 128), ("kv", 256), ("co", 128), ("m1", 512), ("m2", 512)],
    [("q", 128), ("kv", 256), ("router", 9), ("gate1", 384), ("e1", 2304), ("e2", 768), ("gate2", 128),
     ("out", 128)],
]
WCOL, WSIZE = [], []
for _l in WEIGHTS:
    _at, _d = 0, {}
    for _n, _c in _l:
        _d[_n] = _at
        _at += _c
    WCOL.append(_d)
    WSIZE.append(_at)

VECTORS = [("ada", 0, 6), ("qkv", 0, 3), ("so", 0, 1), ("q", 0, 1), ("kv", 0, 2), ("co", 0, 1), ("m1", 0, 4),
           ("m2", 0, 1),
           ("ada", 1, 9), ("qkv", 1, 3), ("so", 1, 1), ("q", 1, 1), ("kv", 1, 2), ("co", 1, 1), ("m1", 1, 8),
           ("m2", 1, 1),
           ("ada", 2, 9), ("norm", 2, 3), ("m1", 2, 4), ("m2", 2, 1),
           ("gamma", 3, 1), ("beta", 3, 1), ("e1", 3, 6), ("gate1", 3, 1), ("router", 3, 1)]
VCOL, _at = {}, 0
for _n, _l, _c in VECTORS:
    VCOL[_l, _n] = _at
    _at += _c
NVEC = _at

C_ID, C_HEAD, C_COS, C_SIN, C_WIN, NCONST = 0, 128, 144, 272, 400, 528


def kinds(**rates):
    out = {}
    for names, rate in rates.items():
        for k in {"heads": HEADS, "mlps": MLPS, "ctx": CTX}.get(names, (names,)):
            out[k] = out.get(k, 0) + rate
    return out


class Event:

    def __init__(self, sem, rates, first=0):
        self.sem, self.rates, self.base = sem, rates, [first]
        for kind in PHASES:
            self.base.append(self.base[-1] + NB * rates.get(kind, 0))

    def count(self, p, b, k):
        return self.base[p] + self.rates[PHASES[p]] * b + k

    def all_of(self, p):
        return self.base[p + 1]


def wait(eng, event, count):
    if isinstance(count, int) and count <= 0:
        return
    eng.wait_ge(event.sem, count)


def wait_apart(eng, event, count, passed):
    if isinstance(count, int):
        wait(eng, event, count)
    else:
        eng.wait_ge(event.sem, count)
        eng.sem_inc(passed, 1)


def build(nc, x, ctx_t, cond_t, vec, consts, rows, key_mask0, key_mask2, self_mask, w_dram, out):
    fp32, bf16, u8 = mybir.dt.float32, mybir.dt.bfloat16, mybir.dt.uint8
    ALU, ACT, AX = mybir.AluOpType, mybir.ActivationFunctionType, mybir.AxisListType

    ctx = ExitStack()
    with ctx:
        def sb(name, shape, dt=fp32):
            return ctx.enter_context(nc.sbuf_tensor(name, shape, dt))

        def sem(name):
            return ctx.enter_context(nc.semaphore(name))

        def event(name, **rates):
            return Event(sem(name), kinds(**rates))

        def open_event(name, **rates):
            return Event(sem(name), kinds(**rates), 1)

        X = sb("X", [P, NB, P])
        CT = sb("CT", [P, NB, NC])
        condT = sb("condT", [P, NB])
        silu_cond = sb("silu_cond", [P, NB])
        VEC = sb("VEC", [P, NVEC])
        CONST = sb("CONST", [P, NCONST])
        W = [sb(f"W{l}", [P, WSIZE[l]]) for l in range(4)]
        rope_w = sb("rope_w", [P, 2, P])
        ident_b = sb("ident_b", [P, P], bf16)
        window_b = sb("window_b", [P, P], bf16)
        self_mask_u = sb("self_mask_u", [P, P], u8)
        self_mask_b = sb("self_mask_b", [P, P], bf16)
        key_mask_u = sb("key_mask_u", [1, 2, NB * NC], u8)
        key_mask_b = sb("key_mask_b", [1, 2, NB * NC], bf16)
        ones_b = sb("ones_b", [1, P], bf16)
        PRM = sb("PRM", [P, 10, 4, NB])
        eff_bias = sb("eff_bias", [P, 4])
        minus_half = sb("minus_half", [P, 1])
        expert_bias = sb("expert_bias", [P, 7, NB])
        router_bias = sb("router_bias", [NE, NB])
        rows_bc = sb("rows_bc", [P, 5 * P])

        stats = sb("stats", [P, 2, 6])
        mean_var = sb("mean_var", [P, 2, 2])
        var_eps = sb("var_eps", [P, 2])
        rstd = sb("rstd", [P, 2])
        XN = sb("XN", [P, 2, P])
        HT = sb("HT", [P, 2, P])
        CS = sb("CS", [P, 2, NC])
        QK = sb("QK", [P, 2, 2, P])
        rope_prod = sb("rope_prod", [P, 2, 2, P])
        V = sb("V", [P, 2, H, 32])
        KM = sb("KM", [P, 2, H, P])
        MX = sb("MX", [P, 2, CH])
        D = sb("D", [P, 2, CH, P])
        E = sb("E", [P, 2, CH, P])
        PT = sb("PT", [P, 2, CH, P])
        top8a = sb("top8a", [P, 2, CH, 8])
        top8b = sb("top8b", [P, 2, CH, 8])
        left_a = sb("left_a", [P, 2, CH, NC])
        left_b = sb("left_b", [P, 2, CH, NC])
        taken = sb("taken", [P, 2, CH, NC])
        E1 = sb("E1", [P, 2, CH, NC])
        OT = sb("OT", [P, NCH, P])
        rsum = sb("rsum", [P, H])
        ON = sb("ON", [P, P])
        ONT = sb("ONT", [P, P])
        Y = sb("Y", [P, P])
        G = sb("G", [P, 2, HID, P])
        SG = sb("SG", [P, 2, HID, P])
        NX = sb("NX", [P, NB, P])
        EV = sb("EV", [P, NB, P])
        V3 = sb("V3", [P, 2, P])
        sum3 = sb("sum3", [P, 2, 2])
        LG = sb("LG", [NE, P])
        LGT = sb("LGT", [P, NB, NE])
        PR = sb("PR", [P, NB, NE])
        rt = sb("rt", [P, 4, NB])
        HE = sb("HE", [P, 2, 7, P])
        YB = sb("YB", [P, 4, P])
        TH = sb("TH", [P, P])
        RT = sb("RT", [P, P])
        R3 = sb("R3", [P, P])
        PS = ctx.enter_context(nc.psum_tensor("PS", [P, 8, 512], fp32))

        BS, BT, BO, BA, BB, BC = 0, 2, 4, 5, 6, 7
        ident = CONST[:, C_ID:C_ID + P]

        def w(l, name, at=0, n=P):
            c = WCOL[l][name] + at
            return W[l][:, c:c + n]

        def vcol(l, name, j=0, rows=P):
            c = VCOL[l, name] + j
            return VEC[0:rows, c:c + 1]

        def bank(i, a, b, rows=P):
            return PS[0:rows, i, a:b]

        loaded = {n: sem("loaded_" + n) for n in ("x", "small", "w0", "w1", "w2", "w3", "masks", "rows")}
        silu_ready = sem("silu_ready")
        consts_ready = sem("consts_ready")
        ada_done = sem("ada_done")
        params_ready = sem("params_ready")
        stats_done = event("stats_done", heads=2, mlps=2, proto=2)
        rstd_done = event("rstd_done", heads=2, mlps=2, proto=2)
        xn_ready = event("xn_ready", heads=1, mlps=1, proto=1)
        xnT_done = event("xnT_done", heads=1, mlps=1, proto=1)
        h_ready = event("h_ready", heads=1, mlps=1, proto=1)
        ctx_ready = event("ctx_ready", ctx=1)
        v_proj = event("v_proj", heads=1, proto=1)
        v_ready = event("v_ready", heads=1, proto=1)
        qk_proj = event("qk_proj", heads=1, proto=1)
        qk_ready = event("qk_ready", self=1, cross=1, top=1, proto=1)
        rope_mults = event("rope_mults", rope=1)
        rope_ready = event("rope_ready", rope=1)
        km_ready = event("km_ready", heads=NCH)
        s_done = event("s_done", heads=NCH)
        max_done = event("max_done", self=NCH, cross=NCH, rope=NCH)
        sub_done = event("sub_done", self=NCH, cross=NCH, rope=NCH)
        top_a = event("top_a", top=NCH)
        left_a_ready = event("left_a_ready", top=NCH)
        top_b = event("top_b", top=NCH)
        left_b_ready = event("left_b_ready", top=NCH)
        negm_ready = event("negm_ready", top=NCH)
        exp1_done = event("exp1_done", top=NCH)
        taken_ready = event("taken_ready", top=NCH)
        sel_ready = event("sel_ready", top=NCH)
        exp_done = event("exp_done", self=NCH, cross=NCH, rope=NCH)
        t_done = event("t_done", heads=NCH)
        pt_ready = event("pt_ready", heads=NCH)
        pv_done = event("pv_done", heads=NCH)
        oT_copied = event("oT_copied", heads=1)
        otr_done = event("otr_done", heads=1)
        rsum_ready = event("rsum_ready", heads=1)
        on_ready = event("on_ready", heads=1)
        onT_done = event("onT_done", heads=1)
        onT_ready = event("onT_ready", heads=1)
        y_done = event("y_done", heads=1, mlps=1)
        y_gated = event("y_gated", heads=1, mlps=1)
        yT_done = event("yT_done", heads=1, mlps=1)
        x_updated = open_event("x_updated", heads=1, mlps=1)
        fc1_done = event("fc1_done", mlps=1)
        act_done = event("act_done", mlps=1)
        glu_ready = event("glu_ready", glu=1)
        ps_done = event("ps_done", proto=1)
        pmax_done = event("pmax_done", proto=1)
        psub_done = event("psub_done", proto=1)
        pexp_done = event("pexp_done", proto=1)
        prec_done = event("prec_done", proto=1)
        pw_ready = event("pw_ready", proto=1)
        pwT_done = event("pwT_done", proto=1)
        pwT_ready = event("pwT_ready", proto=1)
        ev_done = event("ev_done", proto=1)
        ev_ready = event("ev_ready", proto=1)
        lg_done = event("lg_done", proto=1)
        lg_ready = event("lg_ready", proto=1)
        lgT_done = event("lgT_done", proto=1)
        lgT_ready = open_event("lgT_ready", proto=1)
        router_done = sem("router_done")
        router_exp = sem("router_exp")
        eh_done = event("eh_done", experts=2)
        eh_ready = event("eh_ready", experts=2)
        ey_done = event("ey_done", experts=1)
        eb_ready = event("eb_ready", experts=1)
        tanh_ready = event("tanh_ready", experts=1)
        mix_done = event("mix_done", experts=3)
        rT_done = event("rT_done", experts=1)
        rT_ready = event("rT_ready", experts=1)
        r_done = event("r_done", experts=1)
        delta_done = open_event("delta_done", experts=2)
        x_final = event("x_final", experts=1)
        stored = sem("stored")

        passed_dve, passed_pe, passed_pool = (sem("passed_" + n) for n in ("dve", "pe", "pool"))

        def nk(kind):
            return NC if kind in CTX else P

        def hidden_banks(kind, par):
            if kind in (GLU, EXPERTS):
                return (BS, BS + 1) if par == 0 else (BT, BT + 1)
            return (BS + par,)

        def s_free(eng, p, b, c):
            kind = PHASES[p]
            ev = exp1_done if kind == TOP else sub_done
            if isinstance(b, int) and b == 0 and c < 2:
                banks_left(eng, p)
            else:
                wait(eng, ev, ev.count(p, b, c - 1))

        def banks_left(eng, p):
            if p == 0:
                return
            before = PHASES[p - 1]
            if before in (SELF, CROSS, ROPE):
                wait(eng, sub_done, sub_done.all_of(p - 1))
            if before == TOP:
                wait(eng, exp1_done, exp1_done.all_of(p - 1))
            if before in MLPS:
                ev = glu_ready if before == GLU else act_done
                wait(eng, ev, ev.all_of(p - 1))
            if before == PROTO:
                wait(eng, psub_done, psub_done.all_of(p - 1))

        block = ctx.enter_context(nc.Block())

        def run(step, setup):
            last = len(PHASES) - 1
            yield_steps = []
            for p in range(last + 1):
                before = (p - 1, NB - 1) if p else None
                after = (p + 1, 0) if p < last else None
                yield_steps.append((p, before, after))
            return yield_steps

        def phases(fori, step, layer_setup, prep_only, tail_only):
            layer_setup(0)
            prep_only(0, 0, 0)
            last = len(PHASES) - 1
            for p in range(last + 1):
                step(p, 0, 0, (p - 1, NB - 1) if p else None, (p, 1))
                with fori(0, 3) as i:
                    for side in range(2):
                        b = 2 * i + (1 + side)
                        par = (1 + side) % 2
                        step(p, b, par, (p, b - 1), (p, b + 1))
                if p < last and LAYER[p + 1] != LAYER[p]:
                    layer_setup(LAYER[p + 1])
                step(p, NB - 1, 1, (p, NB - 2), (p + 1, 0) if p < last else None)
            tail_only(last, NB - 1, 1)

        @block.sync
        def _(sp):
            sp.dma_start(VEC[:, :], vec).then_inc(loaded["small"], 16)
            sp.dma_start(CONST[:, :], consts).then_inc(loaded["small"], 16)
            sp.dma_start(condT[:, :], cond_t).then_inc(loaded["small"], 16)
            sp.dma_start(CT[:, :, :], ctx_t).then_inc(loaded["x"], 16)
            sp.dma_start(W[1][:, :], w_dram[1]).then_inc(loaded["w1"], 16)
            sp.dma_start(W[3][:, :], w_dram[3]).then_inc(loaded["w3"], 16)
            p = len(PHASES) - 1
            with sp.Fori(0, NB) as b:
                sp.wait_ge(x_final.sem, x_final.count(p, b, 1))
                sp.dma_start(out[b, :, :], X[:, b, :]).then_inc(stored, 16)
            sp.wait_ge(stored, 16 * NB)

        @block.gpsimd
        def _(pool):
            pool.memset(minus_half[:, :], -0.5).then_inc(consts_ready, 1)

            def layer_setup(l):
                pass

            def norm(p, b, par):
                wait_apart(pool, stats_done, stats_done.count(p, b, 2), passed_pool)
                pool.tensor_scalar(var_eps[:, par:par + 1], mean_var[:, par, 1:2], EPS[LAYER[p]], None,
                                   ALU.add).then_inc(rstd_done.sem, 1)
                wait(pool, rstd_done, rstd_done.count(p, b, 1))
                pool.tensor_tensor(rstd[:, par:par + 1], var_eps[:, par:par + 1], minus_half[:, :],
                                   ALU.pow).then_inc(rstd_done.sem, 1)

            def context(p, b, par):
                if not (isinstance(b, int) and b < 2):
                    wait(pool, qk_proj, qk_proj.count(p, b, -1))
                pool.tensor_copy(CS[:, par, :], CT[:, b, :]).then_inc(ctx_ready.sem, 1)

            def mask_heads(p, b, par, c):
                kind, n = PHASES[p], nk(PHASES[p])
                if c == 0:
                    if kind == ROPE:
                        wait(pool, rope_ready, rope_ready.count(p, b, 1))
                    else:
                        wait(pool, qk_ready, qk_ready.count(p, b, 1))
                    wait(pool, s_done, s_done.count(p, b, -NCH))
                pool.tensor_tensor(
                    KM[:, par, CH * c:CH * c + CH, 0:n],
                    QK[:, par, 1, 0:n].unsqueeze(1).broadcast_to([P, CH, n]),
                    CONST[:, C_HEAD + CH * c:C_HEAD + CH * c + CH].unsqueeze(2).broadcast_to([P, CH, n]),
                    ALU.mult).then_inc(km_ready.sem, 1)

            def rotate(p, b, par):
                wait(pool, rope_mults, rope_mults.count(p, b, 1))
                pool.tensor_tensor(QK[:, par, :, :], rope_prod[:, 0, :, :], rope_prod[:, 1, :, :],
                                   ALU.add).then_inc(rope_ready.sem, 1)

            def select(p, b, c):
                r = c % 2
                wait_apart(pool, left_b_ready, left_b_ready.count(p, b, c + 1), passed_pool)
                pool.tensor_scalar(taken[:, r, :, :], left_b[:, r, :, :], 0.5 * REPLACED, None,
                                   ALU.is_le).then_inc(taken_ready.sem, 1)
                wait(pool, exp1_done, exp1_done.count(p, b, c + 1))
                wait(pool, taken_ready, taken_ready.count(p, b, c + 1))
                wait(pool, t_done, t_done.count(p, b, c - 1))
                pool.tensor_tensor(E[:, r, :, 0:NC], E1[:, r, :, :], taken[:, r, :, :],
                                   ALU.mult).then_inc(sel_ready.sem, 1)

            def prep_only(p, b, par):
                pool.wait_ge(loaded["small"], 48)
                norm(p, b, par)
                for c in range(NCH):
                    mask_heads(p, b, par, c)

            def step(p, b, par, tail, prep):
                top_main = PHASES[p] == TOP
                pk = PHASES[prep[0]] if prep else None
                if tail and PHASES[tail[0]] == TOP:
                    select(*tail, 3)
                if pk in CTX:
                    context(*prep, 1 - par)
                if pk and pk != EXPERTS:
                    norm(*prep, 1 - par)
                if top_main:
                    select(p, b, 0)
                    select(p, b, 1)
                if pk == ROPE:
                    rotate(*prep, 1 - par)
                if pk in HEADS:
                    mask_heads(*prep, 1 - par, 0)
                    mask_heads(*prep, 1 - par, 1)
                if top_main:
                    select(p, b, 2)
                if pk in HEADS:
                    mask_heads(*prep, 1 - par, 2)
                    mask_heads(*prep, 1 - par, 3)

            def tail_only(p, b, par):
                pass

            pool.dma_start(W[2][:, :], w_dram[2]).then_inc(loaded["w2"], 16)
            pool.dma_start(rows_bc[:, :], rows.partition_broadcast(P)).then_inc(loaded["rows"], 16)
            pool.wait_ge(loaded["x"], 32)
            phases(pool.Fori, step, layer_setup, prep_only, tail_only)

        @block.scalar
        def _(act):
            act.sem_inc(lgT_ready.sem, 1)
            act.dma_start(X[:, :, :], x).then_inc(loaded["x"], 16)
            act.dma_start(W[0][:, :], w_dram[0]).then_inc(loaded["w0"], 16)
            act.dma_start(key_mask_u[:, 0, :], key_mask0).then_inc(loaded["masks"], 16)
            act.dma_start(key_mask_u[:, 1, :], key_mask2).then_inc(loaded["masks"], 16)
            act.dma_start(self_mask_u[:, :], self_mask).then_inc(loaded["masks"], 16)
            act.wait_ge(loaded["small"], 48)
            act.activation(silu_cond[:, :], condT[:, :], ACT.Silu).then_inc(silu_ready, 1)

            def layer_setup(l):
                act.wait_ge(params_ready, SETUP_DONE[l])

            def modulate(p, b, par):
                wait(act, xnT_done, xnT_done.count(p, b, 1))
                col = b if p < 9 else 0
                dst = HT[:, par, :] if PHASES[p] != PROTO else NX[:, b, :]
                act.activation(dst, bank(BA, 384, 512), ACT.Identity, scale=PRM[:, p, 0, col:col + 1] if isinstance(col, int) else PRM[:, p, 0, bass.ds(col, 1)],
                               bias=PRM[:, p, 1, col:col + 1] if isinstance(col, int) else PRM[:, p, 1, bass.ds(col, 1)]).then_inc(h_ready.sem, 1)

            def copy_qk(p, b, par):
                kind, l, n = PHASES[p], LAYER[p], nk(PHASES[p])
                if kind == ROPE:
                    return
                wait(act, qk_proj, qk_proj.count(p, b, 1))
                if kind == SELF:
                    act.activation(QK[:, par, 0, :], bank(BA, 128, 256), ACT.Identity, bias=vcol(l, "qkv", 0))
                    act.activation(QK[:, par, 1, :], bank(BA, 256, 384), ACT.Identity,
                                   bias=vcol(l, "qkv", 1)).then_inc(qk_ready.sem, 1)
                elif l in (0, 1):
                    act.activation(QK[:, par, 0, :], bank(BA, 128, 256), ACT.Identity, bias=vcol(l, "q"))
                    act.activation(QK[:, par, 1, 0:n], bank(BA, 256, 256 + n), ACT.Identity,
                                   bias=vcol(l, "kv", 0)).then_inc(qk_ready.sem, 1)
                else:
                    act.activation(QK[:, par, 0, :], bank(BA, 128, 256), ACT.Copy)
                    act.activation(QK[:, par, 1, 0:n], bank(BA, 256, 256 + n), ACT.Copy).then_inc(qk_ready.sem, 1)

            def exps(p, b, c):
                kind, n, r = PHASES[p], nk(PHASES[p]), c % 2
                if kind == TOP:
                    wait(act, negm_ready, negm_ready.count(p, b, c + 1))
                    wait(act, left_a_ready, left_a_ready.count(p, b, c + 1))
                    wait(act, sel_ready, sel_ready.count(p, b, c - 1))
                    for j in range(CH):
                        ins = act.activation(E1[:, r, j, :], bank(BS + r, j * n, j * n + n), ACT.Exp,
                                             scale=SCALE, bias=MX[:, r, j:j + 1])
                    ins.then_inc(exp1_done.sem, 1)
                    return
                wait(act, sub_done, sub_done.count(p, b, c + 1))
                wait(act, t_done, t_done.count(p, b, c - 1))
                act.activation(E[:, r, :, 0:n], D[:, r, :, 0:n], ACT.Exp,
                               scale=SCALE).then_inc(exp_done.sem, 1)

            def copy_pt(p, b, c):
                n, r = nk(PHASES[p]), c % 2
                wait(act, t_done, t_done.count(p, b, c + 1))
                wait(act, pv_done, pv_done.count(p, b, c - 1))
                act.activation(PT[0:n, r, :, :], bank(BT + r, 0, CH * P, n), ACT.Copy).then_inc(pt_ready.sem, 1)

            def copy_o(p, b):
                wait(act, pv_done, pv_done.count(p, b, NCH))
                act.activation(OT[:, :, :], bank(BO, 0, 512), ACT.Copy).then_inc(oT_copied.sem, 1)

            def copy_on(p, b):
                wait(act, onT_done, onT_done.count(p, b, 1))
                act.activation(ONT[:, :], bank(BC, 0, P), ACT.Copy).then_inc(onT_ready.sem, 1)

            def gate(p, b):
                wait(act, y_done, y_done.count(p, b, 1))
                act.activation(Y[:, :], bank(BC, 128, 256), ACT.Identity, scale=PRM[:, p, 2, bass.ds(b, 1)],
                               bias=PRM[:, p, 3, bass.ds(b, 1)]).then_inc(y_gated.sem, 1)

            def hidden(p, b, par, half):
                kind, l = PHASES[p], LAYER[p]
                if kind in MLPS:
                    wait(act, fc1_done, fc1_done.count(p, b, 1))
                    func = {GELU: ACT.Gelu, GELUT: ACT.Gelu_apprx_tanh, GLU: ACT.Silu}[kind]
                    dst = SG if kind == GLU else G
                    src = hidden_banks(kind, par)[0]
                    for j in range(HID):
                        ins = act.activation(dst[:, par, j, :], bank(src, j * P, j * P + P), func,
                                             bias=vcol(l, "m1", j))
                    ins.then_inc(act_done.sem, 1)
                if kind == EXPERTS:
                    wait(act, eh_done, eh_done.count(p, b, half + 1))
                    for j in range(4 * half, min(4 * half + 4, 7)):
                        src = hidden_banks(kind, par)[j // 4]
                        ins = act.activation(HE[:, par, j, :], bank(src, j % 4 * P, j % 4 * P + P), ACT.Silu,
                                             bias=expert_bias[:, j, bass.ds(b, 1)])
                    ins.then_inc(eh_ready.sem, 1)

            def proto_exp(p, b, par):
                wait(act, psub_done, psub_done.count(p, b, 1))
                act.activation(E[:, par, 0, 0:NC], D[:, par, 0, 0:NC], ACT.Exp, scale=SCALE3,
                               accum_out=sum3[:, par, 0:1]).then_inc(pexp_done.sem, 1)

            def copy_pwT(p, b, par):
                wait(act, pwT_done, pwT_done.count(p, b, 1))
                act.activation(PT[0:NC, par, 0, :], bank(BT + par, 0, P, NC), ACT.Copy).then_inc(pwT_ready.sem, 1)

            def copy_ev(p, b):
                wait(act, ev_done, ev_done.count(p, b, 1))
                act.activation(EV[:, b, :], bank(BO, 0, P), ACT.Copy).then_inc(ev_ready.sem, 1)

            def copy_logits(p, b):
                wait(act, lg_done, lg_done.count(p, b, 1))
                act.activation(LG[:, :], bank(BB, 0, P, NE), ACT.Identity,
                               bias=router_bias[:, bass.ds(b, 1)]).then_inc(lg_ready.sem, 1)
                wait(act, lgT_done, lgT_done.count(p, b, 1))
                act.activation(LGT[:, b, :], bank(BC, 0, NE), ACT.Copy).then_inc(lgT_ready.sem, 1)

            def prep_only(p, b, par):
                modulate(p, b, par)
                copy_qk(p, b, par)

            def step(p, b, par, tail, prep):
                tk = PHASES[tail[0]] if tail else None
                pk = PHASES[prep[0]] if prep else None
                kind = PHASES[p]
                if tk in HEADS:
                    copy_pt(*tail, 2)
                    if tk != TOP:
                        exps(*tail, 3)
                    copy_pt(*tail, 3)
                if tk == PROTO:
                    copy_pwT(*tail, 1 - par)
                if kind in HEADS:
                    exps(p, b, 0)
                if tk in HEADS:
                    copy_o(*tail)
                if pk and pk != EXPERTS:
                    modulate(*prep, 1 - par)
                if kind in MLPS or kind == EXPERTS:
                    hidden(p, b, par, 0)
                if kind == PROTO:
                    proto_exp(p, b, par)
                if tk == PROTO:
                    copy_ev(*tail)
                if kind in HEADS:
                    copy_pt(p, b, 0)
                    exps(p, b, 1)
                if pk in HEADS or pk == PROTO:
                    copy_qk(*prep, 1 - par)
                if kind in HEADS:
                    copy_pt(p, b, 1)
                if tk in HEADS:
                    copy_on(*tail)
                if kind in HEADS:
                    exps(p, b, 2)
                if tk in HEADS:
                    gate(*tail)
                if kind == TOP:
                    exps(p, b, 3)
                if tk == PROTO:
                    copy_logits(*tail)
                    if kind == EXPERTS:
                        act.wait_ge(router_done, 2)
                        act.activation(PR[:, :, :], PR[:, :, :], ACT.Exp).then_inc(router_exp, 1)
                if tk == EXPERTS:
                    expert_tail(*tail)
                if kind == EXPERTS:
                    hidden(p, b, par, 1)

            def expert_tail(p, b):
                wait(act, eb_ready, eb_ready.count(p, b, 1))
                act.activation(TH[:, :], YB[:, 3, :], ACT.Tanh, scale=0.5).then_inc(tanh_ready.sem, 1)
                wait(act, rT_done, rT_done.count(p, b, 1))
                act.activation(RT[:, :], bank(BC, 0, P), ACT.Copy).then_inc(rT_ready.sem, 1)

            def tail_only(p, b, par):
                expert_tail(p, b)

            phases(act.Fori, step, layer_setup, prep_only, tail_only)

        @block.tensor
        def _(pe):
            def layer_setup(l):
                pe.wait_ge(loaded[f"w{l}"], 16)
                if l == 0:
                    pe.wait_ge(loaded["small"], 48)
                    pe.wait_ge(loaded["x"], 32)
                    pe.wait_ge(consts_ready, CONSTS)
                    pe.wait_ge(silu_ready, 1)
                else:
                    wait(pe, on_ready, on_ready.base[LAYER.index(l)])
                src = silu_cond if l < 2 else condT
                if l < 3:
                    for j in range(6 if l == 0 else 9):
                        ins = pe.matmul(bank(BB, j * NB, j * NB + NB), w(l, "ada", j * P), src[:, :],
                                        start=True, stop=True)
                    if l < 2:
                        pe.matmul(bank(BB, 128, 129), w(l, "so"), vcol(l, "qkv", 2), start=True, stop=True)
                        ins = pe.matmul(bank(BB, 129, 130), w(l, "co"), vcol(l, "kv", 1), start=True, stop=True)
                    ins.then_inc(ada_done, 1)
                else:
                    for j in range(6):
                        pe.matmul(bank(BB, j * NB, j * NB + NB), w(3, "e1", (j * 3 + 2) * P), src[:, :],
                                  start=True, stop=True)
                    pe.matmul(bank(BB, 48, 56), w(3, "gate1", 2 * P), src[:, :], start=True, stop=True)
                    pe.matmul(bank(BB, 64, 72, NE), w(3, "router", 6, NE), src[:, :], start=True,
                              stop=True).then_inc(ada_done, 1)

            def xn_transpose(p, b, par):
                wait(pe, xn_ready, xn_ready.count(p, b, 1))
                q, kind = (p, b - 1) if not (isinstance(b, int) and b == 0) else (p - 1, NB - 1), None
                if q[0] >= 0:
                    kind = PHASES[q[0]]
                    ev = rope_mults if kind == ROPE else qk_ready if kind in HEADS or kind == PROTO else h_ready
                    wait(pe, ev, ev.count(*q, 1))
                pe.transpose(bank(BA, 384, 512), XN[:, par, :], ident).then_inc(xnT_done.sem, 1)

            def project_v(p, b, par, tail):
                kind, l, n = PHASES[p], LAYER[p], nk(PHASES[p])
                wait(pe, h_ready, h_ready.count(p, b, 1))
                if tail and PHASES[tail[0]] in HEADS:
                    wait(pe, x_updated, x_updated.count(*tail, 0))
                elif tail and PHASES[tail[0]] in MLPS:
                    wait(pe, x_updated, x_updated.count(*tail, 1))
                elif tail:
                    wait(pe, x_updated, x_updated.all_of(tail[0] - 1))
                    wait(pe, lgT_ready, lgT_ready.count(*tail, 0))
                if kind in CTX:
                    wait(pe, ctx_ready, ctx_ready.count(p, b, 1))
                    pe.matmul(bank(BC, 384, 512, n), CS[:, par, :], w(l, "kv", P), start=True,
                              stop=True).then_inc(v_proj.sem, 1)
                else:
                    pe.matmul(bank(BC, 384, 512), HT[:, par, :], w(l, "qkv", 2 * P), start=True,
                              stop=True).then_inc(v_proj.sem, 1)

            def project_qk(p, b, par):
                kind, l, n = PHASES[p], LAYER[p], nk(PHASES[p])
                if kind == ROPE:
                    for j, wt in enumerate((w(2, "qkv", 0), w(2, "qkv", P), rope_w[:, 0, :], rope_w[:, 1, :])):
                        ins = pe.matmul(bank(BA, j * P, j * P + P), wt, HT[:, par, :], start=True, stop=True)
                elif kind == SELF:
                    pe.matmul(bank(BA, 128, 256), w(l, "qkv", 0), HT[:, par, :], start=True, stop=True)
                    ins = pe.matmul(bank(BA, 256, 384), w(l, "qkv", P), HT[:, par, :], start=True, stop=True)
                else:
                    src = HT[:, par, :] if kind != PROTO else NX[:, b, :]
                    pe.matmul(bank(BA, 128, 256), w(l, "q"), src, start=True, stop=True)
                    ins = pe.matmul(bank(BA, 256, 256 + n), w(l, "kv", 0), CS[:, par, :], start=True, stop=True)
                ins.then_inc(qk_proj.sem, 1)

            def scores(p, b, par, c):
                kind, l, n = PHASES[p], LAYER[p], nk(PHASES[p])
                wait(pe, km_ready, km_ready.count(p, b, c + 1))
                s_free(pe, p, b, c)
                o = bank(BS + c % 2, 0, CH * n)
                masked = kind == ROPE or (kind == SELF and l == 1) or kind == CROSS
                ins = pe.matmul(o, QK[:, par, 0, :], KM[:, par, CH * c:CH * c + CH, 0:n], start=True,
                                stop=not masked)
                if kind == CROSS:
                    m = key_mask_b[0:1, 0 if l == 0 else 1, :].rearrange("p (b k) -> p b k", b=NB)
                    ins = pe.matmul(o, ones_b[:, :], m[:, b, :].unsqueeze(1).broadcast_to([1, CH, n]),
                                    start=False, stop=True)
                elif masked:
                    m = self_mask_b if kind == ROPE else window_b
                    ins = pe.matmul(o, ident_b[:, :], m[:, :].unsqueeze(1).broadcast_to([P, CH, P]),
                                    start=False, stop=True)
                ins.then_inc(s_done.sem, 1)

            def transposes(p, b, c):
                n, r = nk(PHASES[p]), c % 2
                if PHASES[p] == TOP:
                    wait(pe, sel_ready, sel_ready.count(p, b, c + 1))
                else:
                    wait(pe, exp_done, exp_done.count(p, b, c + 1))
                if isinstance(b, int) and b == 0 and c < 2 and p and PHASES[p - 1] == GLU:
                    wait(pe, glu_ready, glu_ready.all_of(p - 1))
                wait(pe, pt_ready, pt_ready.count(p, b, c - 1))
                for j in range(CH):
                    ins = pe.transpose(bank(BT + r, j * P, j * P + P, n), E[:, r, j, 0:n], ident)
                ins.then_inc(t_done.sem, 1)

            def values(p, b, par, c):
                n, r = nk(PHASES[p]), c % 2
                wait(pe, pt_ready, pt_ready.count(p, b, c + 1))
                if c == 0:
                    wait(pe, oT_copied, oT_copied.count(p, b, 0))
                    if isinstance(b, int) and b == 0 and p:
                        pass
                for j in range(CH):
                    ins = pe.matmul(PS[32 * j:32 * j + 32, BO, c * P:c * P + P], V[0:n, par, CH * c + j, :],
                                    PT[0:n, r, j, :], start=True, stop=True, skip_group_check=True)
                ins.then_inc(pv_done.sem, 1)

            def tail_transpose(p, b):
                wait(pe, oT_copied, oT_copied.count(p, b, 1))
                for c in range(NCH):
                    ins = pe.transpose(bank(BB, c * P, c * P + P), OT[:, c, :], ident)
                ins.then_inc(otr_done.sem, 1)

            def tail_on(p, b, prep):
                wait(pe, on_ready, on_ready.count(p, b, 1))
                wait(pe, x_updated, x_updated.count(p, b, 0))
                if PHASES[prep[0]] in HEADS:
                    wait(pe, v_ready, v_ready.count(*prep, 1))
                pe.transpose(bank(BC, 0, P), ON[:, :], ident).then_inc(onT_done.sem, 1)

            def tail_y(p, b):
                l = LAYER[p]
                wait(pe, onT_ready, onT_ready.count(p, b, 1))
                pe.matmul(bank(BC, 128, 256), w(l, "co" if PHASES[p] in CTX else "so"), ONT[:, :], start=True,
                          stop=True).then_inc(y_done.sem, 1)

            def fc1(p, b, par):
                kind, l = PHASES[p], LAYER[p]
                wait(pe, h_ready, h_ready.count(p, b, 1))
                if isinstance(b, int) and b == 0:
                    banks_left(pe, p)
                if kind == GLU and par == 1:
                    wait(pe, pt_ready, pt_ready.all_of(p - 1))
                for i, bk in enumerate(hidden_banks(kind, par)):
                    for j in range(HID):
                        ins = pe.matmul(bank(bk, j * P, j * P + P), w(l, "m1", (i * HID + j) * P), HT[:, par, :],
                                        start=True, stop=True)
                ins.then_inc(fc1_done.sem, 1)

            def fc2(p, b, par):
                kind, l = PHASES[p], LAYER[p]
                ev = glu_ready if kind == GLU else act_done
                wait(pe, ev, ev.count(p, b, 1))
                wait(pe, x_updated, x_updated.count(p, b, 0))
                if isinstance(b, int) and b == NB - 1 and PHASES[p + 1] in v_proj.rates:
                    wait(pe, v_ready, v_ready.count(p + 1, 0, 1))
                for j in range(HID):
                    ins = pe.matmul(bank(BC, 128, 256), w(l, "m2", j * P), G[:, par, j, :], start=(j == 0),
                                    stop=(j == HID - 1))
                ins.then_inc(y_done.sem, 1)

            def tail_yT(p, b):
                wait(pe, y_gated, y_gated.count(p, b, 1))
                pe.transpose(bank(BC, 256, 384), Y[:, :], ident).then_inc(yT_done.sem, 1)

            def proto_scores(p, b, par):
                wait(pe, qk_ready, qk_ready.count(p, b, 1))
                if isinstance(b, int) and b == 0:
                    banks_left(pe, p)
                pe.matmul(bank(BS + par, 0, NC), QK[:, par, 0, :], QK[:, par, 1, 0:NC], start=True,
                          stop=True).then_inc(ps_done.sem, 1)

            def proto_transpose(p, b, par):
                wait(pe, pw_ready, pw_ready.count(p, b, 1))
                pe.transpose(bank(BT + par, 0, P, NC), E[:, par, 0, 0:NC], ident).then_inc(pwT_done.sem, 1)

            def proto_evidence(p, b, par):
                wait(pe, pwT_ready, pwT_ready.count(p, b, 1))
                pe.matmul(bank(BO, 0, P), V3[0:NC, par, :], PT[0:NC, par, 0, :], start=True,
                          stop=True).then_inc(ev_done.sem, 1)

            def proto_logits(p, b, prep):
                wait(pe, ev_ready, ev_ready.count(p, b, 1))
                pe.matmul(bank(BB, 0, P, NE), w(3, "router", 0, NE), NX[:, b, :], start=True, stop=False)
                pe.matmul(bank(BB, 0, P, NE), w(3, "router", 3, NE), EV[:, b, :], start=False,
                          stop=True).then_inc(lg_done.sem, 1)
                if PHASES[prep[0]] == PROTO:
                    wait(pe, v_ready, v_ready.count(*prep, 1))
                wait(pe, lg_ready, lg_ready.count(p, b, 1))
                wait_apart(pe, lgT_ready, lgT_ready.count(p, b, 0), passed_pe)
                pe.transpose(bank(BC, 0, NE), LG[:, :], ident[0:NE, 0:NE]).then_inc(lgT_done.sem, 1)

            def expert_hidden(p, b, par, half):
                if isinstance(b, int) and b == 0:
                    banks_left(pe, p)
                    wait(pe, ev_ready, ev_ready.count(p - 1, 0, 1))
                if par == 1:
                    wait(pe, pwT_ready, pwT_ready.all_of(p - 1))
                    wait(pe, ev_ready, ev_ready.all_of(p - 1))
                for j in range(4 * half, min(4 * half + 4, 7)):
                    o = bank(hidden_banks(EXPERTS, par)[j // 4], j % 4 * P, j % 4 * P + P)
                    name, at = ("e1", j * 3 * P) if j < 6 else ("gate1", 0)
                    pe.matmul(o, w(3, name, at), NX[:, b, :], start=True, stop=False)
                    ins = pe.matmul(o, w(3, name, at + P), EV[:, b, :], start=False, stop=True)
                ins.then_inc(eh_done.sem, 1)

            def expert_out(p, b, par):
                wait(pe, eh_ready, eh_ready.count(p, b, 2))
                for e in range(NE):
                    for r in range(2):
                        pe.matmul(bank(BO, e * P, e * P + P), HE[:, par, 2 * e + r, :],
                                  w(3, "e2", (2 * e + r) * P), start=(r == 0), stop=(r == 1))
                pe.matmul(bank(BO, 384, 512), HE[:, par, 6, :], w(3, "gate2"), start=True,
                          stop=True).then_inc(ey_done.sem, 1)

            def expert_mix(p, b):
                wait(pe, mix_done, mix_done.count(p, b, 3))
                wait(pe, delta_done, delta_done.count(p, b, 0))
                pe.transpose(bank(BC, 0, P), R3[:, :], ident).then_inc(rT_done.sem, 1)
                wait(pe, rT_ready, rT_ready.count(p, b, 1))
                pe.matmul(bank(BC, 128, 256), RT[:, :], w(3, "out"), start=True, stop=True).then_inc(r_done.sem, 1)

            def prep_only(p, b, par):
                pe.wait_ge(params_ready, SETUP_DONE[0])
                xn_transpose(p, b, par)
                project_v(p, b, par, None)
                project_qk(p, b, par)

            def step(p, b, par, tail, prep):
                tk = PHASES[tail[0]] if tail else None
                pk = PHASES[prep[0]] if prep else None
                kind, other = PHASES[p], 1 - par
                if kind in HEADS:
                    scores(p, b, par, 0)
                if kind in MLPS:
                    fc1(p, b, par)
                if kind == PROTO:
                    proto_scores(p, b, par)
                if kind == EXPERTS:
                    expert_hidden(p, b, par, 0)
                if tk in HEADS:
                    values(*tail, other, 2)
                    transposes(*tail, 3)
                if tk == PROTO:
                    proto_transpose(*tail, other)
                if kind not in HEADS and pk and pk != EXPERTS:
                    xn_transpose(*prep, other)
                if tk in MLPS:
                    fc2(*tail, other)
                if kind in HEADS:
                    scores(p, b, par, 1)
                if tk in HEADS:
                    values(*tail, other, 3)
                if kind in HEADS:
                    xn_transpose(*prep, other)
                    transposes(p, b, 0)
                if tk in MLPS:
                    tail_yT(*tail)
                if tk == PROTO:
                    proto_evidence(*tail, other)
                if kind in HEADS:
                    scores(p, b, par, 2)
                if tk in HEADS:
                    tail_transpose(*tail)
                if pk in HEADS or pk == PROTO:
                    project_v(*prep, other, tail)
                    project_qk(*prep, other)
                if kind in HEADS:
                    values(p, b, par, 0)
                    transposes(p, b, 1)
                if tk in HEADS:
                    tail_on(*tail, prep)
                if kind in HEADS:
                    scores(p, b, par, 3)
                if tk in HEADS:
                    tail_y(*tail)
                if kind in HEADS:
                    values(p, b, par, 1)
                    transposes(p, b, 2)
                if tk in HEADS:
                    tail_yT(*tail)
                if tk == PROTO:
                    proto_logits(*tail, prep)
                if tk == EXPERTS:
                    expert_out(*tail, other)
                if kind == EXPERTS:
                    expert_hidden(p, b, par, 1)
                if tk == EXPERTS:
                    expert_mix(*tail)

            def tail_only(p, b, par):
                expert_out(p, b, par)
                expert_mix(p, b)

            phases(pe.Fori, step, layer_setup, prep_only, tail_only)

        @block.vector
        def _(dve):
            dve.sem_inc(x_updated.sem, 1)
            dve.sem_inc(delta_done.sem, 1)
            dve.memset(ones_b[:, :], 1.0).then_inc(consts_ready, 1)
            dve.memset(V[:, :, :, :], 0.0).then_inc(consts_ready, 1)
            dve.wait_ge(loaded["small"], 48)
            dve.tensor_copy(ident_b[:, :], CONST[:, C_ID:C_ID + P]).then_inc(consts_ready, 1)
            dve.tensor_copy(window_b[:, :], CONST[:, C_WIN:C_WIN + P]).then_inc(consts_ready, 1)
            dve.wait_ge(consts_ready, 5)
            dve.memset(V[:, :, :, HD:HD + 1], 1.0).then_inc(consts_ready, 1)
            dve.wait_ge(loaded["masks"], 48)
            dve.tensor_scalar(self_mask_b[:, :], self_mask_u[:, :], -NEG, NEG, ALU.mult,
                              ALU.add).then_inc(consts_ready, 1)
            dve.tensor_scalar(key_mask_b[:, 0, :], key_mask_u[:, 0, :], REPLACED, 10.0, ALU.mult,
                              ALU.mult).then_inc(consts_ready, 1)
            dve.tensor_scalar(key_mask_b[:, 1, :], key_mask_u[:, 1, :], -NEG, NEG, ALU.mult,
                              ALU.add).then_inc(consts_ready, 1)
            dve.wait_ge(loaded["x"], 32)

            setup_count = [0]

            def chained(ins):
                setup_count[0] += 1
                ins.then_inc(params_ready, 1)
                dve.wait_ge(params_ready, setup_count[0])

            def layer_setup(l):
                def ps(j):
                    return bank(BB, j * NB, j * NB + NB)

                if l == 3:
                    dve.wait_ge(loaded["rows"], 16)
                    dve.wait_ge(ada_done, 4)
                    for j in range(7):
                        chained(dve.tensor_scalar(expert_bias[:, j, :], ps(j),
                                                  vcol(3, "e1", j) if j < 6 else vcol(3, "gate1"), None, ALU.add))
                    chained(dve.tensor_scalar(router_bias[:, :], bank(BB, 64, 72, NE), vcol(3, "router", 0, NE),
                                              None, ALU.add))
                    chained(dve.tensor_copy(PRM[:, 9, 0, :], vcol(3, "gamma").broadcast_to([P, NB])))
                    chained(dve.tensor_copy(PRM[:, 9, 1, :], vcol(3, "beta").broadcast_to([P, NB])))
                    assert setup_count[0] == SETUP_DONE[3]
                    return
                dve.wait_ge(ada_done, l + 1)
                if l < 2:
                    chained(dve.tensor_tensor(eff_bias[:, 0:1], bank(BB, 128, 129), vcol(l, "so"), ALU.add))
                    chained(dve.tensor_tensor(eff_bias[:, 1:2], bank(BB, 129, 130), vcol(l, "co"), ALU.add))
                for s in range(3):
                    p = 3 * l + s
                    if l == 0 and s == 1:
                        chained(dve.memset(PRM[:, p, 0, :], 1.0))
                        chained(dve.memset(PRM[:, p, 1, :], 0.0))
                        chained(dve.memset(PRM[:, p, 2, :], 1.0))
                    else:
                        j = 3 * s if l else (0 if s == 0 else 3)
                        chained(dve.tensor_scalar(PRM[:, p, 1, :], ps(j), vcol(l, "ada", j), None, ALU.add))
                        chained(dve.tensor_scalar(PRM[:, p, 0, :], ps(j + 1), vcol(l, "ada", j + 1), 1.0,
                                                  ALU.add, ALU.add))
                        if l == 2:
                            chained(dve.tensor_scalar(PRM[:, p, 0, :], PRM[:, p, 0, :], vcol(2, "norm", s), None,
                                                      ALU.mult))
                        chained(dve.tensor_scalar(PRM[:, p, 2, :], ps(j + 2), vcol(l, "ada", j + 2), None, ALU.add))
                    if s == 2:
                        bias = vcol(l, "m2")
                    elif l < 2:
                        bias = eff_bias[:, s:s + 1]
                    else:
                        bias = None
                    if bias is None:
                        chained(dve.memset(PRM[:, p, 3, :], 0.0))
                    else:
                        chained(dve.tensor_scalar(PRM[:, p, 3, :], PRM[:, p, 2, :], bias, None, ALU.mult))
                if l == 2:
                    dve.wait_ge(loaded["w2"], 16)
                    for i in range(2):
                        src = w(2, "qkv", i * P).rearrange("p (h t d) -> p h t d", t=2, d=HD // 2)
                        dst = rope_w[:, i, :].rearrange("p (h t d) -> p h t d", t=2, d=HD // 2)
                        chained(dve.tensor_scalar(dst[:, :, 0, :], src[:, :, 1, :], -1.0, None, ALU.mult))
                        chained(dve.tensor_copy(dst[:, :, 1, :], src[:, :, 0, :]))
                assert setup_count[0] == SETUP_DONE[l]

            def statistics(p, b, par):
                wait(dve, stats_done, stats_done.count(p, b, 0))
                if p:
                    wait(dve, x_updated, x_updated.count(p - 1, b, 1))
                dve.bn_stats(stats[:, par, :], X[:, b, :]).then_inc(stats_done.sem, 1)
                wait_apart(dve, stats_done, stats_done.count(p, b, 1), passed_dve)
                dve.bn_aggr(mean_var[:, par, :], stats[:, par, :]).then_inc(stats_done.sem, 1)

            def normalise(p, b, par):
                wait(dve, rstd_done, rstd_done.count(p, b, 2))
                dve.tensor_scalar(XN[:, par, :], X[:, b, :], mean_var[:, par, 0:1], rstd[:, par:par + 1],
                                  ALU.subtract, ALU.mult).then_inc(xn_ready.sem, 1)

            def copy_v(p, b, par):
                n = nk(PHASES[p])
                wait(dve, v_proj, v_proj.count(p, b, 1))
                if PHASES[p] == PROTO:
                    wait(dve, ev_done, ev_done.count(p, b, -1))
                    dve.tensor_copy(V3[0:n, par, :], bank(BC, 384, 512, n)).then_inc(v_ready.sem, 1)
                else:
                    dve.tensor_copy(V[0:n, par, :, 0:HD],
                                    bank(BC, 384, 512, n).rearrange("p (h d) -> p h d", h=H)).then_inc(v_ready.sem, 1)

            def rope(p, b):
                wait(dve, qk_proj, qk_proj.count(p, b, 1))
                wait(dve, rope_ready, rope_ready.count(p, b, 0))
                for i, at in ((0, C_COS), (1, C_SIN)):
                    ins = dve.tensor_tensor(
                        rope_prod[:, i, :, :], bank(BA, 256 * i, 256 * i + 256).rearrange("p (t q) -> p t q", t=2),
                        CONST[:, at:at + P].unsqueeze(1).broadcast_to([P, 2, P]), ALU.mult)
                ins.then_inc(rope_mults.sem, 1)

            def maxima(p, b, c):
                n, r = nk(PHASES[p]), c % 2
                wait(dve, s_done, s_done.count(p, b, c + 1))
                dve.tensor_reduce(MX[:, r, :], bank(BS + r, 0, CH * n).rearrange("p (h k) -> p h k", h=CH), AX.X,
                                  ALU.max).then_inc(max_done.sem, 1)

            def subtract(p, b, c):
                n, r = nk(PHASES[p]), c % 2
                wait(dve, max_done, max_done.count(p, b, c + 1))
                wait(dve, exp_done, exp_done.count(p, b, c - 1))
                dve.tensor_tensor(D[:, r, :, 0:n], bank(BS + r, 0, CH * n).rearrange("p (h k) -> p h k", h=CH),
                                  MX[:, r, :].unsqueeze(2).broadcast_to([P, CH, n]),
                                  ALU.subtract).then_inc(sub_done.sem, 1)

            def top16(p, b, c):
                r = c % 2
                wait_apart(dve, s_done, s_done.count(p, b, c + 1), passed_dve)
                for j in range(CH):
                    ins = dve.max(top8a[:, r, j, :], bank(BS + r, j * NC, j * NC + NC))
                ins.then_inc(top_a.sem, 1)
                wait(dve, top_a, top_a.count(p, b, c + 1))
                wait(dve, exp1_done, exp1_done.count(p, b, c - 1))
                dve.tensor_scalar(MX[:, r, :], top8a[:, r, :, 0], -SCALE, None, ALU.mult).then_inc(negm_ready.sem, 1)
                for j in range(CH):
                    ins = dve.match_replace(out=left_a[:, r, j, :], in_to_replace=top8a[:, r, j, :],
                                            in_values=bank(BS + r, j * NC, j * NC + NC), imm_value=REPLACED)
                ins.then_inc(left_a_ready.sem, 1)
                wait_apart(dve, left_a_ready, left_a_ready.count(p, b, c + 1), passed_dve)
                for j in range(CH):
                    ins = dve.max(top8b[:, r, j, :], left_a[:, r, j, :])
                ins.then_inc(top_b.sem, 1)
                wait(dve, taken_ready, taken_ready.count(p, b, c - 1))
                wait_apart(dve, top_b, top_b.count(p, b, c + 1), passed_dve)
                for j in range(CH):
                    ins = dve.match_replace(out=left_b[:, r, j, :], in_to_replace=top8b[:, r, j, :],
                                            in_values=left_a[:, r, j, :], imm_value=REPLACED)
                ins.then_inc(left_b_ready.sem, 1)

            def norm_out(p, b):
                wait(dve, otr_done, otr_done.count(p, b, 1))
                o = bank(BB, 0, 512).rearrange("p (h e) -> p h e", e=32)
                dve.reciprocal(rsum[:, :], o[:, :, HD]).then_inc(rsum_ready.sem, 1)
                wait(dve, rsum_ready, rsum_ready.count(p, b, 1))
                dve.tensor_tensor(ON[:, :].rearrange("p (h d) -> p h d", d=HD), o[:, :, 0:HD],
                                  rsum[:, :].unsqueeze(2).broadcast_to([P, H, HD]),
                                  ALU.mult).then_inc(on_ready.sem, 1)

            def gate_dve(p, b):
                wait(dve, y_done, y_done.count(p, b, 1))
                dve.tensor_scalar(Y[:, :], bank(BC, 128, 256), PRM[:, p, 2, bass.ds(b, 1)],
                                  PRM[:, p, 3, bass.ds(b, 1)], ALU.mult, ALU.add).then_inc(y_gated.sem, 1)

            def residual(p, b):
                wait(dve, yT_done, yT_done.count(p, b, 1))
                dve.tensor_tensor(X[:, b, :], X[:, b, :], bank(BC, 256, 384), ALU.add).then_inc(x_updated.sem, 1)

            def glu(p, b, par):
                wait(dve, act_done, act_done.count(p, b, 1))
                src = hidden_banks(GLU, par)[1]
                for j in range(HID):
                    ins = dve.scalar_tensor_tensor(G[:, par, j, :], bank(src, j * P, j * P + P),
                                                   vcol(1, "m1", HID + j), SG[:, par, j, :], ALU.add, ALU.mult)
                ins.then_inc(glu_ready.sem, 1)

            def proto_softmax(p, b, par):
                wait(dve, ps_done, ps_done.count(p, b, 1))
                dve.tensor_reduce(MX[:, par, 0:1], bank(BS + par, 0, NC), AX.X, ALU.max).then_inc(pmax_done.sem, 1)
                wait(dve, pmax_done, pmax_done.count(p, b, 1))
                dve.tensor_scalar(D[:, par, 0, 0:NC], bank(BS + par, 0, NC), MX[:, par, 0:1], None,
                                  ALU.subtract).then_inc(psub_done.sem, 1)
                wait(dve, pexp_done, pexp_done.count(p, b, 1))
                dve.reciprocal(sum3[:, par, 1:2], sum3[:, par, 0:1]).then_inc(prec_done.sem, 1)
                wait(dve, prec_done, prec_done.count(p, b, 1))
                dve.tensor_scalar(E[:, par, 0, 0:NC], E[:, par, 0, 0:NC], sum3[:, par, 1:2], None,
                                  ALU.mult).then_inc(pw_ready.sem, 1)

            def router_softmax():
                p = PHASES.index(PROTO)
                wait(dve, lgT_ready, lgT_ready.all_of(p))
                dve.tensor_reduce(rt[:, 0, :], LGT[:, :, :], AX.X, ALU.max).then_inc(router_done, 1)
                dve.wait_ge(router_done, 1)
                dve.tensor_tensor(PR[:, :, :], LGT[:, :, :], rt[:, 0, :].unsqueeze(2).broadcast_to([P, NB, NE]),
                                  ALU.subtract).then_inc(router_done, 1)
                dve.wait_ge(router_exp, 1)
                dve.tensor_reduce(rt[:, 1, :], PR[:, :, :], AX.X, ALU.add).then_inc(router_done, 1)
                dve.wait_ge(router_done, 3)
                dve.reciprocal(rt[:, 2, :], rt[:, 1, :]).then_inc(router_done, 1)
                dve.wait_ge(router_done, 4)
                dve.tensor_tensor(PR[:, :, :], PR[:, :, :], rt[:, 2, :].unsqueeze(2).broadcast_to([P, NB, NE]),
                                  ALU.mult).then_inc(router_done, 1)
                dve.wait_ge(router_done, 5)

            def expert_tail(p, b):
                wait(dve, ey_done, ey_done.count(p, b, 1))
                dve.tensor_tensor(YB[:, :, :], bank(BO, 0, 512), rows_bc[:, 0:512],
                                  ALU.add).then_inc(eb_ready.sem, 1)
                wait(dve, eb_ready, eb_ready.count(p, b, 1))
                dve.tensor_scalar(R3[:, :], YB[:, 0, :], PR[:, b, 0:1], None, ALU.mult).then_inc(mix_done.sem, 1)
                for e in (1, 2):
                    wait(dve, mix_done, mix_done.count(p, b, e))
                    dve.scalar_tensor_tensor(R3[:, :], YB[:, e, :], PR[:, b, e:e + 1], R3[:, :], ALU.mult,
                                             ALU.add).then_inc(mix_done.sem, 1)
                wait(dve, r_done, r_done.count(p, b, 1))
                dve.tensor_tensor(R3[:, :], bank(BC, 128, 256), rows_bc[:, 512:640],
                                  ALU.add).then_inc(delta_done.sem, 1)
                wait(dve, tanh_ready, tanh_ready.count(p, b, 1))
                wait(dve, delta_done, delta_done.count(p, b, 1))
                dve.scalar_tensor_tensor(R3[:, :], TH[:, :], 1.0, R3[:, :], ALU.add,
                                         ALU.mult).then_inc(delta_done.sem, 1)
                wait(dve, delta_done, delta_done.count(p, b, 2))
                dve.scalar_tensor_tensor(X[:, b, :], R3[:, :], 0.5, X[:, b, :], ALU.mult,
                                         ALU.add).then_inc(x_final.sem, 1)

            def prep_only(p, b, par):
                statistics(p, b, par)
                normalise(p, b, par)
                copy_v(p, b, par)

            def step(p, b, par, tail, prep):
                tk = PHASES[tail[0]] if tail else None
                pk = PHASES[prep[0]] if prep else None
                kind, other = PHASES[p], 1 - par
                softmax = kind in (SELF, CROSS, ROPE)
                if pk and pk != EXPERTS:
                    statistics(*prep, other)
                if softmax:
                    maxima(p, b, 0)
                    subtract(p, b, 0)
                if kind == TOP:
                    top16(p, b, 0)
                if pk and pk != EXPERTS:
                    normalise(*prep, other)
                if tk in MLPS:
                    gate_dve(*tail)
                if softmax:
                    maxima(p, b, 1)
                    subtract(p, b, 1)
                if tk in MLPS:
                    residual(*tail)
                if kind == PROTO:
                    proto_softmax(p, b, par)
                if softmax:
                    maxima(p, b, 2)
                if kind == TOP:
                    top16(p, b, 1)
                if tk in HEADS:
                    norm_out(*tail)
                if softmax:
                    subtract(p, b, 2)
                if pk in HEADS or pk == PROTO:
                    copy_v(*prep, other)
                if kind == TOP:
                    top16(p, b, 2)
                if pk == ROPE:
                    rope(*prep)
                if softmax:
                    maxima(p, b, 3)
                    subtract(p, b, 3)
                if kind == TOP:
                    top16(p, b, 3)
                if kind == GLU:
                    glu(p, b, par)
                if tk in HEADS:
                    residual(*tail)
                if tk == PROTO and kind == EXPERTS:
                    router_softmax()
                if tk == EXPERTS:
                    expert_tail(*tail)

            def tail_only(p, b, par):
                expert_tail(p, b)

            phases(dve.Fori, step, layer_setup, prep_only, tail_only)


SETUP_DONE = [14, 28, 47, 57]
CONSTS = 9


def pack(inputs):
    def a(name):
        return np.asarray(inputs[name])

    def rows(m):
        k = m.shape[0] // P
        return m.reshape(k, P, -1).transpose(1, 0, 2).reshape(P, -1)

    L0, L1, L2, L3 = "L0_xcond_", "L1_xcond_", "L2_xcond_", "L3_xcond_"
    w0 = [a(L0 + n) for n in ("ada_w", "qkv_w", "sa_proj_w", "q_w", "kv_w", "ca_proj_w", "fc1_w")] + [
        rows(a(L0 + "fc2_w"))]
    w1 = [a(L1 + n) for n in ("w_ada", "w_qkv", "w_so", "w_q", "w_kv", "w_co", "w_m1")] + [rows(a(L1 + "w_m2"))]
    w2 = [a(L2 + n) for n in ("adaLN_W", "qkv_W", "attn_out_W", "cq_W", "ck_W", "cv_W", "co_W", "mlp_W1")] + [
        rows(a(L2 + "mlp_W2"))]
    e1 = a(L3 + "e_w1").reshape(NE, 3, P, 2, P).transpose(2, 0, 3, 1, 4).reshape(P, -1)
    e2 = a(L3 + "e_w2").reshape(NE * 2, P, P).transpose(1, 0, 2).reshape(P, -1)
    w3 = [a(L3 + n) for n in ("Wq", "Wk", "Wv")] + [rows(a(L3 + "router_W")), rows(a(L3 + "gate_w1")), e1, e2,
                                                     a(L3 + "gate_w2"), a(L3 + "out_w")]
    weights = [np.ascontiguousarray(np.concatenate(x, axis=1)) for x in (w0, w1, w2, w3)]
    names = {
        (0, "ada"): L0 + "ada_b", (0, "qkv"): L0 + "qkv_b", (0, "so"): L0 + "sa_proj_b", (0, "q"): L0 + "q_b",
        (0, "kv"): L0 + "kv_b", (0, "co"): L0 + "ca_proj_b", (0, "m1"): L0 + "fc1_b", (0, "m2"): L0 + "fc2_b",
        (1, "ada"): L1 + "b_ada", (1, "qkv"): L1 + "b_qkv", (1, "so"): L1 + "b_so", (1, "q"): L1 + "b_q",
        (1, "kv"): L1 + "b_kv", (1, "co"): L1 + "b_co", (1, "m1"): L1 + "b_m1", (1, "m2"): L1 + "b_m2",
        (2, "ada"): L2 + "adaLN_b", (2, "m1"): L2 + "mlp_b1", (2, "m2"): L2 + "mlp_b2",
        (3, "gamma"): L3 + "ln_gamma", (3, "beta"): L3 + "ln_beta", (3, "e1"): L3 + "e_b1",
        (3, "gate1"): L3 + "gate_b1"}
    cols = []
    for n, l, c in VECTORS:
        if (l, n) == (2, "norm"):
            v = np.concatenate([a(L2 + "norm1_w"), a(L2 + "normc_w"), a(L2 + "norm2_w")])
        elif (l, n) == (3, "router"):
            v = np.concatenate([a(L3 + "router_b"), np.zeros(P - NE, np.float32)])
        else:
            v = a(names[l, n]).reshape(-1)
        cols.append(v.reshape(c, P).T)
    vec = np.ascontiguousarray(np.concatenate(cols, axis=1))
    rows5 = np.ascontiguousarray(np.concatenate(
        [a(L3 + "e_b2").reshape(-1), a(L3 + "gate_b2"), a(L3 + "out_b")]))
    return dict(
        x=np.ascontiguousarray(a("x").transpose(1, 0, 2)),
        ctx=np.ascontiguousarray(a("ctx_1024").transpose(2, 0, 1)),
        cond=np.ascontiguousarray(a("cond_1024").T),
        vec=vec, consts=constants(), rows=rows5,
        key_mask0=np.ascontiguousarray(a("mask_BxS2_bf0")).reshape(1, -1),
        key_mask2=np.ascontiguousarray(a("mask_BxS2_bf1")).reshape(1, -1),
        self_mask=np.ascontiguousarray(a("mask_SxS_bk0")),
        w0=weights[0], w1=weights[1], w2=weights[2], w3=weights[3])


def constants():
    c = np.zeros((P, NCONST), np.float32)
    c[:, C_ID:C_ID + P] = np.eye(P, dtype=np.float32)
    c[np.arange(P), C_HEAD + np.arange(P) // HD] = 1.0
    inv_freq = 1.0 / 10000.0 ** (np.arange(0, HD, 2, dtype=np.float32) / HD)
    freqs = np.outer(np.arange(P // 2, dtype=np.float32), inv_freq)
    emb = np.concatenate([freqs, freqs], axis=-1)
    c[:, C_COS:C_COS + P] = np.tile(np.cos(emb).astype(np.float32).T, (H, 2))
    c[:, C_SIN:C_SIN + P] = np.tile(np.sin(emb).astype(np.float32).T, (H, 2))
    inner = (np.arange(P) >= 32) & (np.arange(P) < 96)
    c[:, C_WIN:C_WIN + P] = np.where(inner[:, None] == inner[None, :], 0.0, NEG)
    return c


def kernel(**inputs):
    import concourse.bacc as bacc
    from concourse.bass_utils import run_bass_kernel_spmd

    nc = bacc.Bacc("TRN2", target_bir_lowering=False, num_devices=1)
    arrays, aps = {}, {}
    for name, arr in pack(inputs).items():
        arrays["in_" + name] = arr
        aps[name] = nc.dram_tensor("in_" + name, arr.shape, mybir.dt.from_np(arr.dtype), kind="ExternalInput").ap()
    out = nc.dram_tensor("out", (NB, P, P), mybir.dt.float32, kind="ExternalOutput").ap()
    build(nc, aps["x"], aps["ctx"], aps["cond"], aps["vec"], aps["consts"], aps["rows"], aps["key_mask0"],
          aps["key_mask2"], aps["self_mask"], [aps[f"w{l}"] for l in range(4)], out)
    r = run_bass_kernel_spmd(nc, [arrays], core_ids=[0])
    return r.results[0]["out"]
```

```python
from contextlib import ExitStack

import numpy as np

import concourse.bass as bass
from concourse import mybir

P = 128
NB = 8
H, HD = 16, 8
NC = 77
CH = 4
NCH = H // CH
TOPK = 16
HID = 4
NE = 3
NEG = -float(2 ** 100)
REPLACED = -3.0e38
SCALE = float(HD) ** -0.5
SCALE3 = float(P) ** -0.5

SELF, CROSS, TOP, ROPE, GELU, GLU, GELUT, PROTO, EXPERTS = (
    "self", "cross", "top", "rope", "gelu", "glu", "gelut", "proto", "experts")
PHASES = [SELF, CROSS, GELU, SELF, TOP, GLU, ROPE, CROSS, GELUT, PROTO, EXPERTS]
LAYER = [0, 0, 0, 1, 1, 1, 2, 2, 2, 3, 3]
HEADS = (SELF, CROSS, TOP, ROPE)
MLPS = (GELU, GLU, GELUT)
CTX = (CROSS, TOP, PROTO)
EPS = [1e-6, 1e-6, 1e-5, 1e-5]

WEIGHTS = [
    [("ada", 768), ("qkv", 384), ("so", 128), ("q", 128), ("kv", 256), ("co", 128), ("m1", 512), ("m2", 512)],
    [("ada", 1152), ("qkv", 384), ("so", 128), ("q", 128), ("kv", 256), ("co", 128), ("m1", 1024), ("m2", 512)],
    [("ada", 1152), ("qkv", 384), ("so", 128), ("q", 128), ("kv", 256), ("co", 128), ("m1", 512), ("m2", 512)],
    [("q", 128), ("kv", 256), ("router", 9), ("gate1", 384), ("e1", 2304), ("e2", 768), ("gate2", 128),
     ("out", 128)],
]
WCOL, WSIZE = [], []
for _l in WEIGHTS:
    _at, _d = 0, {}
    for _n, _c in _l:
        _d[_n] = _at
        _at += _c
    WCOL.append(_d)
    WSIZE.append(_at)

VECTORS = [("ada", 0, 6), ("qkv", 0, 3), ("q", 0, 1), ("kv", 0, 2), ("so", 0, 1), ("co", 0, 1), ("m1", 0, 4),
           ("m2", 0, 1),
           ("ada", 1, 9), ("qkv", 1, 3), ("q", 1, 1), ("kv", 1, 2), ("so", 1, 1), ("co", 1, 1), ("m1", 1, 8),
           ("m2", 1, 1),
           ("ada", 2, 9), ("norm", 2, 3), ("m1", 2, 4), ("m2", 2, 1),
           ("beta", 3, 1), ("gamma", 3, 1), ("e1", 3, 6), ("gate1", 3, 1)]
VCOL, _at = {}, 0
for _n, _l, _c in VECTORS:
    VCOL[_l, _n] = _at
    _at += _c
NVEC = _at

C_ID, C_HEAD, C_COS, C_SIN, C_WIN, NCONST = 0, 128, 144, 272, 400, 528


def kinds(**rates):
    out = {}
    for names, rate in rates.items():
        for k in {"heads": HEADS, "mlps": MLPS, "ctx": CTX}.get(names, (names,)):
            out[k] = out.get(k, 0) + rate
    return out


class Event:

    def __init__(self, sem, rates, first=0):
        self.sem, self.rates, self.base = sem, rates, [first]
        for kind in PHASES:
            self.base.append(self.base[-1] + NB * rates.get(kind, 0))

    def count(self, p, b, k):
        return self.base[p] + self.rates[PHASES[p]] * b + k

    def all_of(self, p):
        return self.base[p + 1]


def wait(eng, event, count):
    if isinstance(count, int) and count <= 0:
        return
    eng.wait_ge(event.sem, count)


def wait_apart(eng, event, count, passed):
    if isinstance(count, int):
        wait(eng, event, count)
    else:
        eng.wait_ge(event.sem, count)
        eng.sem_inc(passed, 1)


def build(nc, x, ctx_t, cond_t, vec, consts, rows, key_mask0, key_mask2, self_mask, w_dram, out):
    fp32, bf16, u8 = mybir.dt.float32, mybir.dt.bfloat16, mybir.dt.uint8
    ALU, ACT, AX = mybir.AluOpType, mybir.ActivationFunctionType, mybir.AxisListType

    ctx = ExitStack()
    with ctx:
        def sb(name, shape, dt=fp32):
            return ctx.enter_context(nc.sbuf_tensor(name, shape, dt))

        def sem(name):
            return ctx.enter_context(nc.semaphore(name))

        def event(name, **rates):
            return Event(sem(name), kinds(**rates))

        def open_event(name, first=1, **rates):
            return Event(sem(name), kinds(**rates), first)

        X = sb("X", [P, NB, P])
        CT = sb("CT", [P, NB, NC])
        condT = sb("condT", [P, NB])
        silu_cond = sb("silu_cond", [P, NB])
        VEC = sb("VEC", [P, NVEC])
        CONST = sb("CONST", [P, NCONST])
        W = [sb(f"W{l}", [P, WSIZE[l]]) for l in range(4)]
        rope_w = sb("rope_w", [P, 2 * P])
        ident_b = sb("ident_b", [P, P], bf16)
        window_b = sb("window_b", [P, P], bf16)
        self_mask_u = sb("self_mask_u", [P, P], u8)
        self_mask_b = sb("self_mask_b", [P, P], bf16)
        key_mask_u = sb("key_mask_u", [1, 2, NB * NC], u8)
        key_mask_b = sb("key_mask_b", [1, 2, NB * NC], bf16)
        ones_b = sb("ones_b", [1, P], bf16)
        PRM = sb("PRM", [P, 10, 4, NB])
        eff_bias = sb("eff_bias", [P, 2])
        minus_half = sb("minus_half", [P, 1])
        expert_bias = sb("expert_bias", [P, 7, NB])
        rows_bc = sb("rows_bc", [P, 5 * P + NE])

        stats = sb("stats", [P, 2, 6])
        mean_var = sb("mean_var", [P, 2, 2])
        var_eps = sb("var_eps", [P, 2])
        mean = sb("mean", [P, NB])
        rstd = sb("rstd", [P, NB])
        XN = sb("XN", [P, 2, P])
        HT = sb("HT", [P, 2, P])
        CS = sb("CS", [P, 2, NC])
        QK = sb("QK", [P, 2, 2, P])
        rope_prod = sb("rope_prod", [P, 2, 2, P])
        V = sb("V", [P, 2, H, 32])
        KM = sb("KM", [P, 2, H, P])
        MX = sb("MX", [P, 2, CH])
        D = sb("D", [P, 2, CH, P])
        E = sb("E", [P, 2, CH, P])
        PT = sb("PT", [P, 2, CH, P])
        top8a = sb("top8a", [P, 2, CH, 8])
        top8b = sb("top8b", [P, 2, CH, 8])
        left_a = sb("left_a", [P, 2, CH, NC])
        left_b = sb("left_b", [P, 2, CH, NC])
        taken = sb("taken", [P, 2, CH, NC])
        E1 = sb("E1", [P, 2, CH, NC])
        OT = sb("OT", [P, NCH, P])
        rsum = sb("rsum", [P, H])
        ON = sb("ON", [P, P])
        ONT = sb("ONT", [P, P])
        Y = sb("Y", [P, P])
        G = sb("G", [P, 2, HID, P])
        SG = sb("SG", [P, 2, HID, P])
        NX = sb("NX", [P, NB, P])
        EV = sb("EV", [P, NB, P])
        V3 = sb("V3", [P, 2, P])
        sum3 = sb("sum3", [P, 2, 2])
        PR = sb("PR", [P, NB, NE])
        rt = sb("rt", [P, 4, NB])
        HE = sb("HE", [P, 2, 7, P])
        ES = sb("ES", [P, 2, P])
        router_bias = sb("router_bias", [P, NB, NE])
        BM = sb("BM", [P, 2, P])
        BE = sb("BE", [P, 2, NE, P])
        GB = sb("GB", [P, P])
        TH = sb("TH", [P, P])
        RT = sb("RT", [P, P])
        R3 = sb("R3", [P, 2, P])
        D3 = sb("D3", [P, 2, P])
        PS = ctx.enter_context(nc.psum_tensor("PS", [P, 8, 512], fp32))

        BS, BT, BO, BA, BB, BC = 0, 2, 4, 5, 6, 7
        ident = CONST[:, C_ID:C_ID + P]

        def w(l, name, at=0, n=P):
            c = WCOL[l][name] + at
            return W[l][:, c:c + n]

        def vcol(l, name, j=0, rows=P):
            c = VCOL[l, name] + j
            return VEC[0:rows, c:c + 1]

        def bank(i, a, b, rows=P):
            return PS[0:rows, i, a:b]

        loaded = {n: sem("loaded_" + n) for n in ("x", "small", "w0", "w1", "w2", "w3", "masks", "rows")}
        silu_ready = sem("silu_ready")
        consts_ready = sem("consts_ready")
        ada_done = sem("ada_done")
        params_ready = sem("params_ready")
        stats_done = event("stats_done", heads=2, mlps=2, proto=2)
        rstd_done = event("rstd_done", heads=3, mlps=3, proto=3)
        xn_ready = event("xn_ready", heads=1, mlps=1, proto=1)
        xnT_done = event("xnT_done", heads=1, mlps=1, proto=1)
        h_ready = event("h_ready", heads=1, mlps=1, proto=1)
        ctx_ready = event("ctx_ready", ctx=1)
        v_proj = event("v_proj", heads=1, proto=1)
        v_ready = event("v_ready", heads=1, proto=1)
        qk_proj = event("qk_proj", heads=1, proto=1)
        qk_ready = event("qk_ready", self=1, cross=1, top=1, proto=1)
        rope_mults = event("rope_mults", rope=1)
        rope_ready = event("rope_ready", rope=1)
        km_ready = event("km_ready", heads=NCH)
        s_done = event("s_done", heads=NCH)
        max_done = event("max_done", self=NCH, cross=NCH, rope=NCH)
        sub_done = event("sub_done", self=NCH, cross=NCH, rope=NCH)
        top_a = event("top_a", top=NCH)
        left_a_ready = event("left_a_ready", top=NCH)
        top_b = event("top_b", top=NCH)
        left_b_ready = event("left_b_ready", top=NCH)
        negm_ready = event("negm_ready", top=NCH)
        exp1_done = event("exp1_done", top=NCH)
        taken_ready = event("taken_ready", top=NCH)
        sel_ready = event("sel_ready", top=NCH)
        exp_done = event("exp_done", self=NCH, cross=NCH, rope=NCH)
        t_done = event("t_done", heads=NCH)
        pt_ready = event("pt_ready", heads=NCH)
        pv_done = event("pv_done", heads=NCH)
        oT_copied = event("oT_copied", heads=1)
        otr_done = event("otr_done", heads=1)
        rsum_ready = event("rsum_ready", heads=1)
        on_ready = event("on_ready", heads=1)
        onT_done = event("onT_done", heads=1)
        onT_ready = event("onT_ready", heads=1)
        y_done = event("y_done", heads=1, mlps=1)
        y_gated = event("y_gated", heads=1, mlps=1)
        yT_done = event("yT_done", heads=1, mlps=1)
        x_updated = open_event("x_updated", heads=1, mlps=1)
        fc1_done = event("fc1_done", mlps=2)
        act_done = event("act_done", gelu=2, gelut=2, glu=1)
        glu_ready = event("glu_ready", glu=1)
        ps_done = event("ps_done", proto=1)
        pmax_done = event("pmax_done", proto=1)
        psub_done = event("psub_done", proto=1)
        pexp_done = event("pexp_done", proto=1)
        prec_done = event("prec_done", proto=1)
        pw_ready = event("pw_ready", proto=1)
        pwT_done = event("pwT_done", proto=1)
        pwT_ready = event("pwT_ready", proto=1)
        ev_done = event("ev_done", proto=1)
        ev_ready = event("ev_ready", proto=1)
        nx_kept = event("nx_kept", proto=1)
        ev_kept = open_event("ev_kept", 2, proto=1)
        lx_done = event("lx_done", proto=1)
        lg_done = event("lg_done", proto=1)
        router_done = sem("router_done")
        router_exp = sem("router_exp")
        eh_done = event("eh_done", experts=2)
        eh_ready = event("eh_ready", experts=2)
        ey_done = event("ey_done", experts=1)
        be_ready = event("be_ready", experts=2)
        bm_ready = event("bm_ready", experts=1)
        gb_ready = open_event("gb_ready", experts=1)
        tanh_ready = event("tanh_ready", experts=1)
        mix_done = event("mix_done", experts=3)
        rT_done = event("rT_done", experts=1)
        rT_ready = event("rT_ready", experts=1)
        r_done = event("r_done", experts=1)
        delta_done = open_event("delta_done", experts=2)
        x_final = event("x_final", experts=1)
        stored = sem("stored")

        passed_dve, passed_pe, passed_pool = (sem("passed_" + n) for n in ("dve", "pe", "pool"))

        def nk(kind):
            return NC if kind in CTX else P

        def hidden_banks(par):
            return (BS, BS + 1) if par == 0 else (BT, BT + 1)

        def hidden_blocks(kind):
            return {GELU: (2, 2), GELUT: (2, 2), GLU: (4, 4), EXPERTS: (4, 3)}[kind]

        def s_free(eng, p, b, c):
            kind = PHASES[p]
            ev = exp1_done if kind == TOP else sub_done
            if isinstance(b, int) and b == 0 and c < 2:
                banks_left(eng, p)
            else:
                wait(eng, ev, ev.count(p, b, c - 1))

        def banks_left(eng, p):
            if p == 0:
                return
            before = PHASES[p - 1]
            if before in (SELF, CROSS, ROPE):
                wait(eng, sub_done, sub_done.all_of(p - 1))
            if before == TOP:
                wait(eng, exp1_done, exp1_done.all_of(p - 1))
            if before in MLPS:
                ev = glu_ready if before == GLU else act_done
                wait(eng, ev, ev.count(p - 1, NB - 1, 0))
            if before == PROTO:
                wait(eng, psub_done, psub_done.all_of(p - 1))

        block = ctx.enter_context(nc.Block())

        def run(step, setup):
            last = len(PHASES) - 1
            yield_steps = []
            for p in range(last + 1):
                before = (p - 1, NB - 1) if p else None
                after = (p + 1, 0) if p < last else None
                yield_steps.append((p, before, after))
            return yield_steps

        def phases(fori, step, layer_setup, prep_only, tail_only):
            layer_setup(0)
            prep_only(0, 0, 0)
            last = len(PHASES) - 1
            for p in range(last + 1):
                step(p, 0, 0, (p - 1, NB - 1) if p else None, (p, 1))
                with fori(0, 3) as i:
                    for side in range(2):
                        b = 2 * i + (1 + side)
                        par = (1 + side) % 2
                        step(p, b, par, (p, b - 1), (p, b + 1))
                for l in SETUP_IN.get(p, ()):
                    layer_setup(l)
                step(p, NB - 1, 1, (p, NB - 2), (p + 1, 0) if p < last else None)
            tail_only(last, NB - 1, 1)

        @block.sync
        def _(sp):
            sp.dma_start(VEC[:, :], vec).then_inc(loaded["small"], 16)
            sp.dma_start(CONST[:, :], consts).then_inc(loaded["small"], 16)
            sp.dma_start(condT[:, :], cond_t).then_inc(loaded["small"], 16)
            sp.dma_start(CT[:, :, :], ctx_t).then_inc(loaded["x"], 16)
            sp.dma_start(W[1][:, :], w_dram[1]).then_inc(loaded["w1"], 16)
            sp.dma_start(W[3][:, :], w_dram[3]).then_inc(loaded["w3"], 16)
            p = len(PHASES) - 1
            with sp.Fori(0, NB) as b:
                sp.wait_ge(x_final.sem, x_final.count(p, b, 1))
                sp.dma_start(out[b, :, :], X[:, b, :]).then_inc(stored, 16)
            sp.wait_ge(stored, 16 * NB)

        @block.gpsimd
        def _(pool):
            pool.sem_inc(ev_kept.sem, 2)
            pool.memset(minus_half[:, :], -0.5).then_inc(consts_ready, 1)

            def layer_setup(l):
                pass

            def norm(p, b, par):
                pool.wait_ge(stats_done.sem, stats_done.count(p, b, 2))
                pool.sem_inc(passed_pool, 1)
                pool.tensor_scalar(var_eps[:, par:par + 1], mean_var[:, par, 1:2], EPS[LAYER[p]], None,
                                   ALU.add).then_inc(rstd_done.sem, 1)
                pool.tensor_copy(mean[:, bass.ds(b, 1)], mean_var[:, par, 0:1]).then_inc(rstd_done.sem, 1)
                pool.wait_ge(rstd_done.sem, rstd_done.count(p, b, 1))
                pool.tensor_tensor(rstd[:, bass.ds(b, 1)], var_eps[:, par:par + 1], minus_half[:, :],
                                   ALU.pow).then_inc(rstd_done.sem, 1)

            def context(p, b, par):
                if not (isinstance(b, int) and b < 2):
                    wait(pool, qk_proj, qk_proj.count(p, b, -1))
                pool.tensor_copy(CS[:, par, :], CT[:, b, :]).then_inc(ctx_ready.sem, 1)

            def mask_heads(p, b, par, c):
                kind, n = PHASES[p], nk(PHASES[p])
                if c == 0:
                    if kind == ROPE:
                        pool.wait_ge(rope_ready.sem, rope_ready.count(p, b, 1))
                    else:
                        pool.wait_ge(qk_ready.sem, qk_ready.count(p, b, 1))
                    wait(pool, s_done, s_done.count(p, b, -NCH))
                pool.tensor_tensor(
                    KM[:, par, CH * c:CH * c + CH, 0:n],
                    QK[:, par, 1, 0:n].unsqueeze(1).broadcast_to([P, CH, n]),
                    CONST[:, C_HEAD + CH * c:C_HEAD + CH * c + CH].unsqueeze(2).broadcast_to([P, CH, n]),
                    ALU.mult).then_inc(km_ready.sem, 1)

            def rotate(p, b, par):
                pool.wait_ge(rope_mults.sem, rope_mults.count(p, b, 1))
                pool.tensor_tensor(QK[:, par, :, :], rope_prod[:, 0, :, :], rope_prod[:, 1, :, :],
                                   ALU.add).then_inc(rope_ready.sem, 1)

            def select(p, b, c):
                r = c % 2
                pool.wait_ge(exp1_done.sem, exp1_done.count(p, b, c + 1))
                pool.wait_ge(taken_ready.sem, taken_ready.count(p, b, c + 1))
                wait(pool, t_done, t_done.count(p, b, c - 1))
                pool.tensor_tensor(E[:, r, :, 0:NC], E1[:, r, :, :], taken[:, r, :, :],
                                   ALU.mult).then_inc(sel_ready.sem, 1)

            def keep_nx(p, b, par):
                pool.wait_ge(h_ready.sem, h_ready.count(p, b, 1))
                pool.tensor_copy(NX[:, b, :], HT[:, par, :]).then_inc(nx_kept.sem, 1)

            def keep_ev(p, b, par):
                pool.wait_ge(ev_ready.sem, ev_ready.count(p, b, 1))
                pool.tensor_copy(EV[:, b, :], ES[:, par, :]).then_inc(ev_kept.sem, 1)

            def routed_bias(p, b, par):
                if isinstance(b, int) and b == 0:
                    pool.wait_ge(router_done, 7)
                wait(pool, delta_done, delta_done.count(p, b, -2))
                pool.tensor_tensor(BE[:, par, :, :], rows_bc[:, 0:NE * P].rearrange("p (e q) -> p e q", e=NE),
                                   PR[:, b, :].unsqueeze(2).broadcast_to([P, NE, P]),
                                   ALU.mult).then_inc(be_ready.sem, 1)
                pool.wait_ge(be_ready.sem, be_ready.count(p, b, 1))
                pool.tensor_tensor(BE[:, par, 1, :], BE[:, par, 0, :], BE[:, par, 1, :], ALU.add).then_inc(be_ready.sem, 1)
                pool.wait_ge(be_ready.sem, be_ready.count(p, b, 2))
                pool.tensor_tensor(BM[:, par, :], BE[:, par, 1, :], BE[:, par, 2, :], ALU.add).then_inc(bm_ready.sem, 1)

            def prep_only(p, b, par):
                pool.wait_ge(loaded["small"], 48)
                for c in range(NCH):
                    mask_heads(p, b, par, c)

            def step(p, b, par, tail, prep):
                tk = PHASES[tail[0]] if tail else None
                pk = PHASES[prep[0]] if prep else None
                if tk == TOP:
                    select(*tail, 2)
                    select(*tail, 3)
                if pk in CTX:
                    context(*prep, 1 - par)
                if tk == PROTO:
                    keep_ev(*tail, 1 - par)
                if pk == PROTO:
                    keep_nx(*prep, 1 - par)
                if PHASES[p] == EXPERTS:
                    routed_bias(p, b, par)
                if PHASES[p] == TOP:
                    select(p, b, 0)
                    select(p, b, 1)
                if pk == ROPE:
                    rotate(*prep, 1 - par)
                if pk in HEADS:
                    for c in range(NCH):
                        mask_heads(*prep, 1 - par, c)
                if tk in HEADS + MLPS:
                    norm(tail[0] + 1, tail[1], 1 - par)

            def tail_only(p, b, par):
                pass

            pool.dma_start(W[2][:, :], w_dram[2]).then_inc(loaded["w2"], 16)
            pool.dma_start(rows_bc[:, :], rows.partition_broadcast(P)).then_inc(loaded["rows"], 16)
            pool.wait_ge(loaded["x"], 32)
            for b in range(NB):
                norm(0, b, b % 2)
            phases(pool.Fori, step, layer_setup, prep_only, tail_only)

        @block.scalar
        def _(act):
            act.dma_start(X[:, :, :], x).then_inc(loaded["x"], 16)
            act.dma_start(W[0][:, :], w_dram[0]).then_inc(loaded["w0"], 16)
            act.dma_start(key_mask_u[:, 0, :], key_mask0).then_inc(loaded["masks"], 16)
            act.dma_start(key_mask_u[:, 1, :], key_mask2).then_inc(loaded["masks"], 16)
            act.dma_start(self_mask_u[:, :], self_mask).then_inc(loaded["masks"], 16)
            act.wait_ge(loaded["small"], 48)
            act.activation(silu_cond[:, :], condT[:, :], ACT.Silu).then_inc(silu_ready, 1)

            def layer_setup(l):
                act.wait_ge(params_ready, SETUP_DONE[l])

            def modulate(p, b, par):
                act.wait_ge(xnT_done.sem, xnT_done.count(p, b, 1))
                if PHASES[p] == PROTO:
                    wait(act, nx_kept, nx_kept.count(p, b, -1))
                act.activation(HT[:, par, :], bank(BA, 384, 512), ACT.Identity, scale=PRM[:, p, 1, bass.ds(b, 1)],
                               bias=PRM[:, p, 0, bass.ds(b, 1)]).then_inc(h_ready.sem, 1)

            def copy_qk(p, b, par):
                kind, l, n = PHASES[p], LAYER[p], nk(PHASES[p])
                if kind == ROPE:
                    return
                act.wait_ge(qk_proj.sem, qk_proj.count(p, b, 1))
                if kind == SELF:
                    act.activation(QK[:, par, 0, :], bank(BA, 128, 256), ACT.Identity, bias=vcol(l, "qkv", 0))
                    act.activation(QK[:, par, 1, :], bank(BA, 256, 384), ACT.Identity,
                                   bias=vcol(l, "qkv", 1)).then_inc(qk_ready.sem, 1)
                elif l in (0, 1):
                    act.activation(QK[:, par, 0, :], bank(BA, 128, 256), ACT.Identity, bias=vcol(l, "q"))
                    act.activation(QK[:, par, 1, 0:n], bank(BA, 256, 256 + n), ACT.Identity,
                                   bias=vcol(l, "kv", 0)).then_inc(qk_ready.sem, 1)
                else:
                    act.activation(QK[:, par, 0, :], bank(BA, 128, 256), ACT.Copy)
                    act.activation(QK[:, par, 1, 0:n], bank(BA, 256, 256 + n), ACT.Copy).then_inc(qk_ready.sem, 1)

            def exps(p, b, c):
                kind, n, r = PHASES[p], nk(PHASES[p]), c % 2
                if kind == TOP:
                    act.wait_ge(negm_ready.sem, negm_ready.count(p, b, c + 1))
                    act.wait_ge(left_a_ready.sem, left_a_ready.count(p, b, c + 1))
                    wait(act, sel_ready, sel_ready.count(p, b, c - 1))
                    for j in range(CH):
                        ins = act.activation(E1[:, r, j, :], bank(BS + r, j * n, j * n + n), ACT.Exp,
                                             scale=SCALE, bias=MX[:, r, j:j + 1])
                    ins.then_inc(exp1_done.sem, 1)
                    return
                act.wait_ge(sub_done.sem, sub_done.count(p, b, c + 1))
                wait(act, t_done, t_done.count(p, b, c - 1))
                act.activation(E[:, r, :, 0:n], D[:, r, :, 0:n], ACT.Exp,
                               scale=SCALE).then_inc(exp_done.sem, 1)

            def copy_pt(p, b, c):
                n, r = nk(PHASES[p]), c % 2
                act.wait_ge(t_done.sem, t_done.count(p, b, c + 1))
                wait(act, pv_done, pv_done.count(p, b, c - 1))
                act.activation(PT[0:n, r, :, :], bank(BT + r, 0, CH * P, n), ACT.Copy).then_inc(pt_ready.sem, 1)

            def copy_o(p, b):
                act.wait_ge(pv_done.sem, pv_done.count(p, b, NCH))
                act.activation(OT[:, :, :], bank(BO, 0, 512), ACT.Copy).then_inc(oT_copied.sem, 1)

            def copy_on(p, b):
                act.wait_ge(onT_done.sem, onT_done.count(p, b, 1))
                act.activation(ONT[:, :], bank(BC, 0, P), ACT.Copy).then_inc(onT_ready.sem, 1)

            def gate(p, b):
                act.wait_ge(y_done.sem, y_done.count(p, b, 1))
                act.activation(Y[:, :], bank(BC, 128, 256), ACT.Identity, scale=PRM[:, p, 2, bass.ds(b, 1)],
                               bias=PRM[:, p, 3, bass.ds(b, 1)]).then_inc(y_gated.sem, 1)

            def hidden(p, b, par, half):
                kind, l = PHASES[p], LAYER[p]
                if kind == GLU and half == 1:
                    return
                done, ready = (eh_done, eh_ready) if kind == EXPERTS else (fc1_done, act_done)
                act.wait_ge(done.sem, done.count(p, b, half + 1))
                func = {GELU: ACT.Gelu, GELUT: ACT.Gelu_apprx_tanh, GLU: ACT.Silu, EXPERTS: ACT.Silu}[kind]
                dst = {GLU: SG, EXPERTS: HE}.get(kind, G)
                first = half * hidden_blocks(kind)[0]
                for j in range(hidden_blocks(kind)[half]):
                    bias = expert_bias[:, first + j, bass.ds(b, 1)] if kind == EXPERTS else vcol(l, "m1", first + j)
                    ins = act.activation(dst[:, par, first + j, :], bank(hidden_banks(par)[half], j * P, j * P + P),
                                         func, bias=bias)
                ins.then_inc(ready.sem, 1)

            def proto_exp(p, b, par):
                act.wait_ge(psub_done.sem, psub_done.count(p, b, 1))
                act.activation(E[:, par, 0, 0:NC], D[:, par, 0, 0:NC], ACT.Exp, scale=SCALE3,
                               accum_out=sum3[:, par, 0:1]).then_inc(pexp_done.sem, 1)

            def copy_pwT(p, b, par):
                act.wait_ge(pwT_done.sem, pwT_done.count(p, b, 1))
                act.activation(PT[0:NC, par, 0, :], bank(BT + par, 0, P, NC), ACT.Copy).then_inc(pwT_ready.sem, 1)

            def copy_ev(p, b, par):
                act.wait_ge(ev_done.sem, ev_done.count(p, b, 1))
                act.wait_ge(ev_kept.sem, ev_kept.count(p, b, -1))
                act.activation(ES[:, par, :], bank(BO, 0, P), ACT.Copy).then_inc(ev_ready.sem, 1)

            def prep_only(p, b, par):
                modulate(p, b, par)
                copy_qk(p, b, par)

            def step(p, b, par, tail, prep):
                tk = PHASES[tail[0]] if tail else None
                pk = PHASES[prep[0]] if prep else None
                kind = PHASES[p]
                if kind == TOP:
                    top_step(p, b, par, tail, prep)
                    return
                if tk in HEADS:
                    copy_pt(*tail, 2)
                    if tk != TOP:
                        exps(*tail, 3)
                    copy_pt(*tail, 3)
                if tk == PROTO:
                    copy_pwT(*tail, 1 - par)
                if kind in HEADS:
                    exps(p, b, 0)
                if tk in HEADS:
                    copy_o(*tail)
                if kind in MLPS + (EXPERTS,):
                    hidden(p, b, par, 0)
                if pk and pk != EXPERTS:
                    modulate(*prep, 1 - par)
                if kind == PROTO:
                    proto_exp(p, b, par)
                if tk == PROTO:
                    copy_ev(*tail, 1 - par)
                if kind in HEADS:
                    copy_pt(p, b, 0)
                    exps(p, b, 1)
                if kind in MLPS:
                    hidden(p, b, par, 1)
                if pk in HEADS or pk == PROTO:
                    copy_qk(*prep, 1 - par)
                if kind in HEADS:
                    copy_pt(p, b, 1)
                if tk in HEADS:
                    copy_on(*tail)
                if kind in HEADS:
                    exps(p, b, 2)
                if tk in HEADS:
                    gate(*tail)
                if tk == PROTO and kind == EXPERTS:
                    act.wait_ge(router_done, 4)
                    act.activation(PR[:, :, :], PR[:, :, :], ACT.Exp).then_inc(router_exp, 1)
                if tk == EXPERTS:
                    expert_tail(*tail)
                if kind == EXPERTS:
                    hidden(p, b, par, 1)

            def top_step(p, b, par, tail, prep):
                copy_pt(*tail, 2)
                if PHASES[tail[0]] == SELF:
                    exps(*tail, 3)
                modulate(*prep, 1 - par)
                exps(p, b, 0)
                copy_pt(*tail, 3)
                exps(p, b, 1)
                copy_o(*tail)
                if PHASES[prep[0]] in HEADS:
                    copy_qk(*prep, 1 - par)
                copy_pt(p, b, 0)
                copy_on(*tail)
                copy_pt(p, b, 1)
                gate(*tail)
                exps(p, b, 2)
                exps(p, b, 3)

            def expert_tail(p, b):
                act.wait_ge(gb_ready.sem, gb_ready.count(p, b, 1))
                act.activation(TH[:, :], GB[:, :], ACT.Tanh, scale=0.5).then_inc(tanh_ready.sem, 1)
                act.wait_ge(rT_done.sem, rT_done.count(p, b, 1))
                act.activation(RT[:, :], bank(BC, 0, P), ACT.Copy).then_inc(rT_ready.sem, 1)

            def tail_only(p, b, par):
                expert_tail(p, b)

            phases(act.Fori, step, layer_setup, prep_only, tail_only)

        @block.tensor
        def _(pe):
            def layer_setup(l):
                pe.wait_ge(loaded[f"w{l}"], 16)
                if l == 0:
                    pe.wait_ge(loaded["small"], 48)
                    pe.wait_ge(loaded["x"], 32)
                    pe.wait_ge(consts_ready, CONSTS)
                    pe.wait_ge(silu_ready, 1)
                else:
                    pe.wait_ge(params_ready, SETUP_DONE[l - 1])
                    p = [p for p in SETUP_IN if l in SETUP_IN[p]][0]
                    wait(pe, on_ready, on_ready.count(p, NB - 2, 0) if PHASES[p] in HEADS else on_ready.base[p])
                src = silu_cond if l < 2 else condT
                if l < 3:
                    for j in range(6 if l == 0 else 9):
                        ins = pe.matmul(bank(BB, j * NB, j * NB + NB), w(l, "ada", j * P), src[:, :],
                                        start=True, stop=True)
                    if l < 2:
                        pe.matmul(bank(BB, 128, 129), w(l, "so"), vcol(l, "qkv", 2), start=True, stop=True)
                        ins = pe.matmul(bank(BB, 129, 130), w(l, "co"), vcol(l, "kv", 1), start=True, stop=True)
                    ins.then_inc(ada_done, 1)
                else:
                    for j in range(6):
                        pe.matmul(bank(BB, j * NB, j * NB + NB), w(3, "e1", (j * 3 + 2) * P), src[:, :],
                                  start=True, stop=True)
                    pe.matmul(bank(BB, 48, 56), w(3, "gate1", 2 * P), src[:, :], start=True, stop=True)
                    for b in range(NB):
                        ins = pe.matmul(bank(BB, 64 + NE * b, 64 + NE * b + NE),
                                        condT[:, b:b + 1].broadcast_to([P, P]), w(3, "router", 2 * NE, NE),
                                        start=True, stop=True)
                    ins.then_inc(ada_done, 1)

            def xn_transpose(p, b, par):
                pe.wait_ge(xn_ready.sem, xn_ready.count(p, b, 1))
                q, kind = (p, b - 1) if not (isinstance(b, int) and b == 0) else (p - 1, NB - 1), None
                if q[0] >= 0:
                    kind = PHASES[q[0]]
                    ev = rope_mults if kind == ROPE else qk_ready if kind in HEADS or kind == PROTO else h_ready
                    pe.wait_ge(ev.sem, ev.count(*q, 1))
                pe.transpose(bank(BA, 384, 512), XN[:, par, :], ident).then_inc(xnT_done.sem, 1)

            def project_v(p, b, par, tail):
                kind, l, n = PHASES[p], LAYER[p], nk(PHASES[p])
                if tail and PHASES[tail[0]] in HEADS:
                    pe.wait_ge(x_updated.sem, x_updated.count(*tail, 0))
                elif tail and PHASES[tail[0]] in MLPS:
                    pe.wait_ge(x_updated.sem, x_updated.count(*tail, 1))
                elif tail:
                    pe.wait_ge(x_updated.sem, x_updated.all_of(tail[0] - 1))
                if kind in CTX:
                    pe.wait_ge(ctx_ready.sem, ctx_ready.count(p, b, 1))
                    pe.matmul(bank(BC, 384, 512, n), CS[:, par, :], w(l, "kv", P), start=True,
                              stop=True).then_inc(v_proj.sem, 1)
                else:
                    pe.wait_ge(h_ready.sem, h_ready.count(p, b, 1))
                    pe.matmul(bank(BC, 384, 512), HT[:, par, :], w(l, "qkv", 2 * P), start=True,
                              stop=True).then_inc(v_proj.sem, 1)

            def project_qk(p, b, par):
                kind, l, n = PHASES[p], LAYER[p], nk(PHASES[p])
                if kind == ROPE:
                    for j, wt in enumerate((w(2, "qkv", 0), w(2, "qkv", P), rope_w[:, 0:P], rope_w[:, P:2 * P])):
                        ins = pe.matmul(bank(BA, j * P, j * P + P), wt, HT[:, par, :], start=True, stop=True)
                elif kind == SELF:
                    pe.matmul(bank(BA, 128, 256), w(l, "qkv", 0), HT[:, par, :], start=True, stop=True)
                    ins = pe.matmul(bank(BA, 256, 384), w(l, "qkv", P), HT[:, par, :], start=True, stop=True)
                else:
                    pe.wait_ge(h_ready.sem, h_ready.count(p, b, 1))
                    pe.matmul(bank(BA, 128, 256), w(l, "q"), HT[:, par, :], start=True, stop=True)
                    ins = pe.matmul(bank(BA, 256, 256 + n), w(l, "kv", 0), CS[:, par, :], start=True, stop=True)
                ins.then_inc(qk_proj.sem, 1)

            def scores(p, b, par, c):
                kind, l, n = PHASES[p], LAYER[p], nk(PHASES[p])
                pe.wait_ge(km_ready.sem, km_ready.count(p, b, c + 1))
                s_free(pe, p, b, c)
                o = bank(BS + c % 2, 0, CH * n)
                masked = kind == ROPE or (kind == SELF and l == 1) or kind == CROSS
                ins = pe.matmul(o, QK[:, par, 0, :], KM[:, par, CH * c:CH * c + CH, 0:n], start=True,
                                stop=not masked)
                if kind == CROSS:
                    m = key_mask_b[0:1, 0 if l == 0 else 1, :].rearrange("p (b k) -> p b k", b=NB)
                    ins = pe.matmul(o, ones_b[:, :], m[:, b, :].unsqueeze(1).broadcast_to([1, CH, n]),
                                    start=False, stop=True)
                elif masked:
                    m = self_mask_b if kind == ROPE else window_b
                    ins = pe.matmul(o, ident_b[:, :], m[:, :].unsqueeze(1).broadcast_to([P, CH, P]),
                                    start=False, stop=True)
                ins.then_inc(s_done.sem, 1)

            def transposes(p, b, c):
                n, r = nk(PHASES[p]), c % 2
                if PHASES[p] == TOP:
                    pe.wait_ge(sel_ready.sem, sel_ready.count(p, b, c + 1))
                else:
                    pe.wait_ge(exp_done.sem, exp_done.count(p, b, c + 1))
                if isinstance(b, int) and b == 0 and c < 2 and p and PHASES[p - 1] in MLPS:
                    ev = glu_ready if PHASES[p - 1] == GLU else act_done
                    pe.wait_ge(ev.sem, ev.all_of(p - 1))
                wait(pe, pt_ready, pt_ready.count(p, b, c - 1))
                for j in range(CH):
                    ins = pe.transpose(bank(BT + r, j * P, j * P + P, n), E[:, r, j, 0:n], ident)
                ins.then_inc(t_done.sem, 1)

            def values(p, b, par, c):
                n, r = nk(PHASES[p]), c % 2
                pe.wait_ge(pt_ready.sem, pt_ready.count(p, b, c + 1))
                if c == 0:
                    wait(pe, oT_copied, oT_copied.count(p, b, 0))
                    if isinstance(b, int) and b == 0 and p:
                        pass
                for j in range(CH):
                    ins = pe.matmul(PS[32 * j:32 * j + 32, BO, c * P:c * P + P], V[0:n, par, CH * c + j, :],
                                    PT[0:n, r, j, :], start=True, stop=True, skip_group_check=True)
                ins.then_inc(pv_done.sem, 1)

            def tail_transpose(p, b):
                pe.wait_ge(oT_copied.sem, oT_copied.count(p, b, 1))
                for c in range(NCH):
                    ins = pe.transpose(bank(BB, c * P, c * P + P), OT[:, c, :], ident)
                ins.then_inc(otr_done.sem, 1)

            def tail_on(p, b, prep):
                pe.wait_ge(on_ready.sem, on_ready.count(p, b, 1))
                pe.wait_ge(x_updated.sem, x_updated.count(p, b, 0))
                if PHASES[prep[0]] in HEADS:
                    pe.wait_ge(v_ready.sem, v_ready.count(*prep, 1))
                pe.transpose(bank(BC, 0, P), ON[:, :], ident).then_inc(onT_done.sem, 1)

            def tail_y(p, b):
                l = LAYER[p]
                pe.wait_ge(onT_ready.sem, onT_ready.count(p, b, 1))
                pe.matmul(bank(BC, 128, 256), w(l, "co" if PHASES[p] in CTX else "so"), ONT[:, :], start=True,
                          stop=True).then_inc(y_done.sem, 1)

            def fc1(p, b, par, half):
                kind, l = PHASES[p], LAYER[p]
                pe.wait_ge(h_ready.sem, h_ready.count(p, b, 1))
                if isinstance(b, int) and b == 0:
                    banks_left(pe, p)
                if par == 1:
                    pe.wait_ge(pt_ready.sem, pt_ready.all_of(p - 1))
                first = half * hidden_blocks(kind)[0]
                for j in range(hidden_blocks(kind)[half]):
                    ins = pe.matmul(bank(hidden_banks(par)[half], j * P, j * P + P),
                                    w(l, "m1", (first + j) * P), HT[:, par, :], start=True, stop=True)
                ins.then_inc(fc1_done.sem, 1)

            def fc2(p, b, par):
                kind, l = PHASES[p], LAYER[p]
                if kind == GLU:
                    pe.wait_ge(glu_ready.sem, glu_ready.count(p, b, 1))
                else:
                    pe.wait_ge(act_done.sem, act_done.count(p, b, 2))
                pe.wait_ge(x_updated.sem, x_updated.count(p, b, 0))
                if isinstance(b, int) and b == NB - 1 and PHASES[p + 1] in v_proj.rates:
                    pe.wait_ge(v_ready.sem, v_ready.count(p + 1, 0, 1))
                for j in range(HID):
                    ins = pe.matmul(bank(BC, 128, 256), w(l, "m2", j * P), G[:, par, j, :], start=(j == 0),
                                    stop=(j == HID - 1))
                ins.then_inc(y_done.sem, 1)

            def tail_yT(p, b):
                pe.wait_ge(y_gated.sem, y_gated.count(p, b, 1))
                pe.transpose(bank(BC, 256, 384), Y[:, :], ident).then_inc(yT_done.sem, 1)

            def proto_scores(p, b, par):
                pe.wait_ge(qk_ready.sem, qk_ready.count(p, b, 1))
                if isinstance(b, int) and b == 0:
                    banks_left(pe, p)
                pe.matmul(bank(BS + par, 0, NC), QK[:, par, 0, :], QK[:, par, 1, 0:NC], start=True,
                          stop=True).then_inc(ps_done.sem, 1)
                pe.matmul(PS[:, BB, bass.ds(NE * b, NE)], HT[:, par, :], w(3, "router", 0, NE),
                          start=True, stop=True).then_inc(lx_done.sem, 1)

            def proto_transpose(p, b, par):
                pe.wait_ge(pw_ready.sem, pw_ready.count(p, b, 1))
                pe.transpose(bank(BT + par, 0, P, NC), E[:, par, 0, 0:NC], ident).then_inc(pwT_done.sem, 1)

            def proto_evidence(p, b, par):
                pe.wait_ge(pwT_ready.sem, pwT_ready.count(p, b, 1))
                pe.matmul(bank(BO, 0, P), V3[0:NC, par, :], PT[0:NC, par, 0, :], start=True,
                          stop=True).then_inc(ev_done.sem, 1)

            def proto_logits(p, b, par):
                pe.wait_ge(ev_ready.sem, ev_ready.count(p, b, 1))
                pe.matmul(PS[:, BB, bass.ds(NB * NE + NE * b, NE)], ES[:, par, :], w(3, "router", NE, NE),
                          start=True, stop=True).then_inc(lg_done.sem, 1)

            def expert_hidden(p, b, par, first, end):
                if isinstance(b, int) and b == 0:
                    banks_left(pe, p)
                    pe.wait_ge(ev_kept.sem, ev_kept.count(p - 1, 0, 1))
                    pe.wait_ge(nx_kept.sem, nx_kept.all_of(p - 1))
                if par == 1:
                    pe.wait_ge(pwT_ready.sem, pwT_ready.all_of(p - 1))
                    pe.wait_ge(ev_kept.sem, ev_kept.all_of(p - 1))
                for j in range(first, end):
                    o = bank(hidden_banks(par)[j // 4], j % 4 * P, j % 4 * P + P)
                    name, at = ("e1", j * 3 * P) if j < 6 else ("gate1", 0)
                    pe.matmul(o, w(3, name, at), NX[:, b, :], start=True, stop=False)
                    ins = pe.matmul(o, w(3, name, at + P), EV[:, b, :], start=False, stop=True)
                    if j in (3, 6):
                        ins.then_inc(eh_done.sem, 1)

            def expert_out(p, b, par):
                pe.wait_ge(eh_ready.sem, eh_ready.count(p, b, 2))
                pe.wait_ge(gb_ready.sem, gb_ready.count(p, b, 0))
                for e in range(NE):
                    for r in range(2):
                        pe.matmul(bank(BO, e * P, e * P + P), HE[:, par, 2 * e + r, :],
                                  w(3, "e2", (2 * e + r) * P), start=(r == 0), stop=(r == 1))
                pe.matmul(bank(BO, 384, 512), HE[:, par, 6, :], w(3, "gate2"), start=True,
                          stop=True).then_inc(ey_done.sem, 1)

            def mix_transpose(p, b, par):
                pe.wait_ge(mix_done.sem, mix_done.count(p, b, 3))
                pe.wait_ge(delta_done.sem, delta_done.count(p, b, 0))
                pe.transpose(bank(BC, 0, P), R3[:, par, :], ident).then_inc(rT_done.sem, 1)

            def mix_out(p, b):
                pe.wait_ge(rT_ready.sem, rT_ready.count(p, b, 1))
                pe.matmul(bank(BC, 128, 256), RT[:, :], w(3, "out"), start=True, stop=True).then_inc(r_done.sem, 1)

            def prep_only(p, b, par):
                pe.wait_ge(params_ready, SETUP_DONE[0])
                xn_transpose(p, b, par)
                project_v(p, b, par, None)
                project_qk(p, b, par)

            def step(p, b, par, tail, prep):
                tk = PHASES[tail[0]] if tail else None
                pk = PHASES[prep[0]] if prep else None
                kind, other = PHASES[p], 1 - par
                if kind == TOP:
                    top_step(p, b, par, tail, prep)
                    return
                if kind in HEADS:
                    scores(p, b, par, 0)
                if kind in MLPS:
                    fc1(p, b, par, 0)
                if kind == PROTO:
                    proto_scores(p, b, par)
                if kind == EXPERTS:
                    experts_step(p, b, par, tail)
                    return
                if tk == TOP:
                    transposes(*tail, 2)
                if tk in HEADS:
                    values(*tail, other, 2)
                    transposes(*tail, 3)
                if tk == PROTO:
                    proto_transpose(*tail, other)
                if tk in MLPS:
                    fc2(*tail, other)
                if kind not in HEADS and pk and pk != EXPERTS:
                    xn_transpose(*prep, other)
                if kind in MLPS:
                    fc1(p, b, par, 1)
                if kind in HEADS:
                    scores(p, b, par, 1)
                if tk in HEADS:
                    values(*tail, other, 3)
                if kind in HEADS:
                    xn_transpose(*prep, other)
                    transposes(p, b, 0)
                if tk in MLPS:
                    tail_yT(*tail)
                if tk == PROTO:
                    proto_evidence(*tail, other)
                if kind in HEADS:
                    scores(p, b, par, 2)
                if tk in HEADS:
                    tail_transpose(*tail)
                if pk in HEADS or pk == PROTO:
                    project_v(*prep, other, tail)
                    project_qk(*prep, other)
                if kind in HEADS:
                    values(p, b, par, 0)
                    transposes(p, b, 1)
                if tk in HEADS:
                    tail_on(*tail, prep)
                if kind in HEADS:
                    scores(p, b, par, 3)
                if tk in HEADS:
                    tail_y(*tail)
                if kind in HEADS:
                    values(p, b, par, 1)
                    transposes(p, b, 2)
                if tk in HEADS:
                    tail_yT(*tail)
                if tk == PROTO:
                    proto_logits(*tail, 1 - par)

            def experts_step(p, b, par, tail):
                if PHASES[tail[0]] == PROTO:
                    expert_hidden(p, b, par, 0, 4)
                    proto_transpose(*tail, 1 - par)
                    proto_evidence(*tail, 1 - par)
                    proto_logits(*tail, 1 - par)
                    expert_hidden(p, b, par, 4, 7)
                    return
                expert_hidden(p, b, par, 0, 2)
                expert_out(*tail, 1 - par)
                expert_hidden(p, b, par, 2, 6)
                mix_transpose(*tail, 1 - par)
                expert_hidden(p, b, par, 6, 7)
                mix_out(*tail)

            def top_step(p, b, par, tail, prep):
                tk, other = PHASES[tail[0]], 1 - par
                scores(p, b, par, 0)
                scores(p, b, par, 1)
                xn_transpose(*prep, other)
                if tk == TOP:
                    transposes(*tail, 2)
                if PHASES[prep[0]] in HEADS:
                    project_v(*prep, other, tail)
                transposes(*tail, 3)
                values(*tail, other, 2)
                if PHASES[prep[0]] in HEADS:
                    project_qk(*prep, other)
                scores(p, b, par, 2)
                values(*tail, other, 3)
                scores(p, b, par, 3)
                tail_transpose(*tail)
                transposes(p, b, 0)
                tail_on(*tail, prep)
                transposes(p, b, 1)
                tail_y(*tail)
                values(p, b, par, 0)
                tail_yT(*tail)
                values(p, b, par, 1)

            def tail_only(p, b, par):
                expert_out(p, b, par)
                mix_transpose(p, b, par)
                mix_out(p, b)

            phases(pe.Fori, step, layer_setup, prep_only, tail_only)

        @block.vector
        def _(dve):
            dve.sem_inc(x_updated.sem, 1)
            dve.sem_inc(delta_done.sem, 1)
            dve.sem_inc(gb_ready.sem, 1)
            dve.memset(ones_b[:, :], 1.0).then_inc(consts_ready, 1)
            dve.memset(V[:, :, :, :], 0.0).then_inc(consts_ready, 1)
            dve.memset(PRM[:, 1, 0, :], 0.0).then_inc(consts_ready, 1)
            dve.memset(PRM[:, 1, 1:3, :], 1.0).then_inc(consts_ready, 1)
            dve.wait_ge(loaded["small"], 48)
            dve.tensor_copy(ident_b[:, :], CONST[:, C_ID:C_ID + P]).then_inc(consts_ready, 1)
            dve.tensor_copy(window_b[:, :], CONST[:, C_WIN:C_WIN + P]).then_inc(consts_ready, 1)
            dve.wait_ge(consts_ready, 7)
            dve.memset(V[:, :, :, HD:HD + 1], 1.0).then_inc(consts_ready, 1)
            dve.wait_ge(loaded["masks"], 48)
            dve.tensor_scalar(self_mask_b[:, :], self_mask_u[:, :], -NEG, NEG, ALU.mult,
                              ALU.add).then_inc(consts_ready, 1)
            dve.tensor_scalar(key_mask_b[:, 0, :], key_mask_u[:, 0, :], REPLACED, 10.0, ALU.mult,
                              ALU.mult).then_inc(consts_ready, 1)
            dve.tensor_scalar(key_mask_b[:, 1, :], key_mask_u[:, 1, :], -NEG, NEG, ALU.mult,
                              ALU.add).then_inc(consts_ready, 1)
            dve.wait_ge(loaded["x"], 32)

            def layer_setup(l):
                done = SETUP_DONE[l - 1] if l else 0
                dve.wait_ge(ada_done, l + 1)
                if l == 3:
                    c = VCOL[3, "e1"]
                    dve.tensor_tensor(expert_bias[:, :, :], bank(BB, 0, 7 * NB).rearrange("p (j b) -> p j b", j=7),
                                      VEC[:, c:c + 7].unsqueeze(2).broadcast_to([P, 7, NB]),
                                      ALU.add).then_inc(params_ready, 1)
                    dve.wait_ge(loaded["rows"], 16)
                    dve.tensor_tensor(router_bias[:, :, :],
                                      bank(BB, 64, 64 + NB * NE).rearrange("p (b e) -> p b e", e=NE),
                                      rows_bc[:, 640:640 + NE].unsqueeze(1).broadcast_to([P, NB, NE]),
                                      ALU.add).then_inc(params_ready, 1)
                    c = VCOL[3, "beta"]
                    dve.tensor_copy(PRM[:, 9, 0:2, :],
                                    VEC[:, c:c + 2].unsqueeze(2).broadcast_to([P, 2, NB])).then_inc(params_ready, 1)
                    return
                n = 2 if l == 0 else 3
                mod = PRM[:, 0:3:2, :, :] if l == 0 else PRM[:, 3 * l:3 * l + 3, :, :]
                c = VCOL[l, "ada"]
                for s in range(n):
                    ins = dve.tensor_tensor(
                        mod[:, s, 0:3, :],
                        bank(BB, 3 * s * NB, 3 * s * NB + 3 * NB).rearrange("p (j b) -> p j b", j=3),
                        VEC[:, c + 3 * s:c + 3 * s + 3].unsqueeze(2).broadcast_to([P, 3, NB]), ALU.add)
                ins.then_inc(params_ready, 1)
                if l < 2:
                    c = VCOL[l, "so"]
                    dve.tensor_tensor(eff_bias[:, :], bank(BB, 128, 130), VEC[:, c:c + 2],
                                      ALU.add).then_inc(params_ready, 1)
                else:
                    dve.memset(PRM[:, 6:8, 3, :], 0.0).then_inc(params_ready, 1)
                dve.wait_ge(params_ready, done + 2)
                if l == 2:
                    c = VCOL[2, "norm"]
                    dve.scalar_tensor_tensor(mod[:, :, 1, :], mod[:, :, 1, :], 1.0,
                                             VEC[:, c:c + 3].unsqueeze(2).broadcast_to([P, 3, NB]), ALU.add,
                                             ALU.mult).then_inc(params_ready, 1)
                else:
                    dve.tensor_scalar(mod[:, :, 1, :], mod[:, :, 1, :], 1.0, None,
                                      ALU.add).then_inc(params_ready, 1)
                    dve.tensor_tensor(PRM[:, 3 * l:3 * l + 2, 3, :], PRM[:, 3 * l:3 * l + 2, 2, :],
                                      eff_bias[:, :].unsqueeze(2).broadcast_to([P, 2, NB]),
                                      ALU.mult).then_inc(params_ready, 1)
                dve.tensor_scalar(PRM[:, 3 * l + 2, 3, :], PRM[:, 3 * l + 2, 2, :], vcol(l, "m2"), None,
                                  ALU.mult).then_inc(params_ready, 1)
                if l == 2:
                    dve.wait_ge(loaded["w2"], 16)
                    src = w(2, "qkv", 0, 2 * P).rearrange("p (h t d) -> p h t d", t=2, d=HD // 2)
                    dst = rope_w[:, :].rearrange("p (h t d) -> p h t d", t=2, d=HD // 2)
                    dve.tensor_scalar(dst[:, :, 0, :], src[:, :, 1, :], -1.0, None,
                                      ALU.mult).then_inc(params_ready, 1)
                    dve.tensor_copy(dst[:, :, 1, :], src[:, :, 0, :]).then_inc(params_ready, 1)

            def statistics(p, b, par):
                if not (p == 0 and b < 2):
                    wait(dve, rstd_done, rstd_done.count(p, b, -3))
                if p:
                    dve.wait_ge(x_updated.sem, x_updated.count(p - 1, b, 1))
                    dve.sem_inc(passed_dve, 1)
                dve.bn_stats(stats[:, par, :], X[:, b, :]).then_inc(stats_done.sem, 1)
                dve.wait_ge(stats_done.sem, stats_done.count(p, b, 1))
                dve.sem_inc(passed_dve, 1)
                dve.bn_aggr(mean_var[:, par, :], stats[:, par, :]).then_inc(stats_done.sem, 1)

            def normalise(p, b, par):
                dve.wait_ge(rstd_done.sem, rstd_done.count(p, b, 3))
                dve.tensor_scalar(XN[:, par, :], X[:, b, :], mean[:, bass.ds(b, 1)], rstd[:, bass.ds(b, 1)],
                                  ALU.subtract, ALU.mult).then_inc(xn_ready.sem, 1)

            def copy_v(p, b, par):
                n = nk(PHASES[p])
                dve.wait_ge(v_proj.sem, v_proj.count(p, b, 1))
                if PHASES[p] == PROTO:
                    wait(dve, ev_done, ev_done.count(p, b, -1))
                    dve.tensor_copy(V3[0:n, par, :], bank(BC, 384, 512, n)).then_inc(v_ready.sem, 1)
                else:
                    dve.tensor_copy(V[0:n, par, :, 0:HD],
                                    bank(BC, 384, 512, n).rearrange("p (h d) -> p h d", h=H)).then_inc(v_ready.sem, 1)

            def rope(p, b):
                dve.wait_ge(qk_proj.sem, qk_proj.count(p, b, 1))
                wait(dve, rope_ready, rope_ready.count(p, b, 0))
                for i, at in ((0, C_COS), (1, C_SIN)):
                    ins = dve.tensor_tensor(
                        rope_prod[:, i, :, :], bank(BA, 256 * i, 256 * i + 256).rearrange("p (t q) -> p t q", t=2),
                        CONST[:, at:at + P].unsqueeze(1).broadcast_to([P, 2, P]), ALU.mult)
                ins.then_inc(rope_mults.sem, 1)

            def maxima(p, b, c):
                n, r = nk(PHASES[p]), c % 2
                dve.wait_ge(s_done.sem, s_done.count(p, b, c + 1))
                dve.tensor_reduce(MX[:, r, :], bank(BS + r, 0, CH * n).rearrange("p (h k) -> p h k", h=CH), AX.X,
                                  ALU.max).then_inc(max_done.sem, 1)

            def subtract(p, b, c):
                n, r = nk(PHASES[p]), c % 2
                dve.wait_ge(max_done.sem, max_done.count(p, b, c + 1))
                wait(dve, exp_done, exp_done.count(p, b, c - 1))
                dve.tensor_tensor(D[:, r, :, 0:n], bank(BS + r, 0, CH * n).rearrange("p (h k) -> p h k", h=CH),
                                  MX[:, r, :].unsqueeze(2).broadcast_to([P, CH, n]),
                                  ALU.subtract).then_inc(sub_done.sem, 1)

            def first_8(p, b, c):
                r = c % 2
                dve.wait_ge(s_done.sem, s_done.count(p, b, c + 1))
                dve.sem_inc(passed_dve, 1)
                for j in range(CH):
                    ins = dve.max(top8a[:, r, j, :], bank(BS + r, j * NC, j * NC + NC))
                ins.then_inc(top_a.sem, 1)

            def replace_first(p, b, c):
                r = c % 2
                dve.wait_ge(top_a.sem, top_a.count(p, b, c + 1))
                wait(dve, exp1_done, exp1_done.count(p, b, c - 1))
                dve.tensor_scalar(MX[:, r, :], top8a[:, r, :, 0], -SCALE, None, ALU.mult).then_inc(negm_ready.sem, 1)
                for j in range(CH):
                    ins = dve.match_replace(out=left_a[:, r, j, :], in_to_replace=top8a[:, r, j, :],
                                            in_values=bank(BS + r, j * NC, j * NC + NC), imm_value=REPLACED)
                ins.then_inc(left_a_ready.sem, 1)

            def next_8(p, b, c):
                r = c % 2
                dve.wait_ge(left_a_ready.sem, left_a_ready.count(p, b, c + 1))
                dve.sem_inc(passed_dve, 1)
                for j in range(CH):
                    ins = dve.max(top8b[:, r, j, :], left_a[:, r, j, :])
                ins.then_inc(top_b.sem, 1)

            def replace_next(p, b, c):
                r = c % 2
                dve.wait_ge(top_b.sem, top_b.count(p, b, c + 1))
                dve.sem_inc(passed_dve, 1)
                for j in range(CH):
                    ins = dve.match_replace(out=left_b[:, r, j, :], in_to_replace=top8b[:, r, j, :],
                                            in_values=left_a[:, r, j, :], imm_value=REPLACED)
                ins.then_inc(left_b_ready.sem, 1)

            def mark_taken(p, b, c):
                r = c % 2
                dve.wait_ge(left_b_ready.sem, left_b_ready.count(p, b, c + 1))
                wait(dve, sel_ready, sel_ready.count(p, b, c - 1))
                dve.tensor_scalar(taken[:, r, :, :], left_b[:, r, :, :], 0.5 * REPLACED, None,
                                  ALU.is_le).then_inc(taken_ready.sem, 1)

            def norm_out(p, b):
                dve.wait_ge(otr_done.sem, otr_done.count(p, b, 1))
                o = bank(BB, 0, 512).rearrange("p (h e) -> p h e", e=32)
                dve.reciprocal(rsum[:, :], o[:, :, HD]).then_inc(rsum_ready.sem, 1)
                dve.wait_ge(rsum_ready.sem, rsum_ready.count(p, b, 1))
                dve.tensor_tensor(ON[:, :].rearrange("p (h d) -> p h d", d=HD), o[:, :, 0:HD],
                                  rsum[:, :].unsqueeze(2).broadcast_to([P, H, HD]),
                                  ALU.mult).then_inc(on_ready.sem, 1)

            def gate_dve(p, b):
                dve.wait_ge(y_done.sem, y_done.count(p, b, 1))
                dve.tensor_scalar(Y[:, :], bank(BC, 128, 256), PRM[:, p, 2, bass.ds(b, 1)],
                                  PRM[:, p, 3, bass.ds(b, 1)], ALU.mult, ALU.add).then_inc(y_gated.sem, 1)

            def residual(p, b):
                dve.wait_ge(yT_done.sem, yT_done.count(p, b, 1))
                dve.tensor_tensor(X[:, b, :], X[:, b, :], bank(BC, 256, 384), ALU.add).then_inc(x_updated.sem, 1)

            def glu(p, b, par):
                dve.wait_ge(act_done.sem, act_done.count(p, b, 1))
                dve.wait_ge(fc1_done.sem, fc1_done.count(p, b, 2))
                src = hidden_banks(par)[1]
                for j in range(HID):
                    ins = dve.scalar_tensor_tensor(G[:, par, j, :], bank(src, j * P, j * P + P),
                                                   vcol(1, "m1", HID + j), SG[:, par, j, :], ALU.add, ALU.mult)
                ins.then_inc(glu_ready.sem, 1)

            def proto_softmax(p, b, par):
                dve.wait_ge(ps_done.sem, ps_done.count(p, b, 1))
                dve.tensor_reduce(MX[:, par, 0:1], bank(BS + par, 0, NC), AX.X, ALU.max).then_inc(pmax_done.sem, 1)
                dve.wait_ge(pmax_done.sem, pmax_done.count(p, b, 1))
                dve.tensor_scalar(D[:, par, 0, 0:NC], bank(BS + par, 0, NC), MX[:, par, 0:1], None,
                                  ALU.subtract).then_inc(psub_done.sem, 1)
                dve.wait_ge(pexp_done.sem, pexp_done.count(p, b, 1))
                dve.reciprocal(sum3[:, par, 1:2], sum3[:, par, 0:1]).then_inc(prec_done.sem, 1)
                dve.wait_ge(prec_done.sem, prec_done.count(p, b, 1))
                dve.tensor_scalar(E[:, par, 0, 0:NC], E[:, par, 0, 0:NC], sum3[:, par, 1:2], None,
                                  ALU.mult).then_inc(pw_ready.sem, 1)

            def router_softmax():
                p = PHASES.index(PROTO)
                dve.wait_ge(lx_done.sem, lx_done.all_of(p))
                dve.wait_ge(lg_done.sem, lg_done.all_of(p))
                dve.tensor_tensor(router_bias[:, :, :], bank(BB, 0, NB * NE).rearrange("p (b e) -> p b e", e=NE),
                                  router_bias[:, :, :], ALU.add).then_inc(router_done, 1)
                dve.wait_ge(router_done, 1)
                dve.tensor_tensor(PR[:, :, :], bank(BB, NB * NE, 2 * NB * NE).rearrange("p (b e) -> p b e", e=NE),
                                  router_bias[:, :, :], ALU.add).then_inc(router_done, 1)
                dve.wait_ge(router_done, 2)
                dve.tensor_reduce(rt[:, 0, :], PR[:, :, :], AX.X, ALU.max).then_inc(router_done, 1)
                dve.wait_ge(router_done, 3)
                dve.tensor_tensor(PR[:, :, :], PR[:, :, :], rt[:, 0, :].unsqueeze(2).broadcast_to([P, NB, NE]),
                                  ALU.subtract).then_inc(router_done, 1)
                dve.wait_ge(router_exp, 1)
                dve.tensor_reduce(rt[:, 1, :], PR[:, :, :], AX.X, ALU.add).then_inc(router_done, 1)
                dve.wait_ge(router_done, 5)
                dve.reciprocal(rt[:, 2, :], rt[:, 1, :]).then_inc(router_done, 1)
                dve.wait_ge(router_done, 6)
                dve.tensor_tensor(PR[:, :, :], PR[:, :, :], rt[:, 2, :].unsqueeze(2).broadcast_to([P, NB, NE]),
                                  ALU.mult).then_inc(router_done, 1)
                dve.wait_ge(router_done, 7)

            def expert_tail(p, b, par):
                dve.wait_ge(ey_done.sem, ey_done.count(p, b, 1))
                dve.wait_ge(bm_ready.sem, bm_ready.count(p, b, 1))
                dve.scalar_tensor_tensor(R3[:, par, :], bank(BO, 0, P), PR[:, b, 0:1], BM[:, par, :], ALU.mult,
                                         ALU.add).then_inc(mix_done.sem, 1)
                for e in (1, 2):
                    dve.wait_ge(mix_done.sem, mix_done.count(p, b, e))
                    dve.scalar_tensor_tensor(R3[:, par, :], bank(BO, e * P, e * P + P), PR[:, b, e:e + 1], R3[:, par, :],
                                             ALU.mult, ALU.add).then_inc(mix_done.sem, 1)
                dve.tensor_tensor(GB[:, :], bank(BO, 384, 512), rows_bc[:, 384:512], ALU.add).then_inc(gb_ready.sem, 1)
                dve.wait_ge(r_done.sem, r_done.count(p, b, 1))
                dve.tensor_tensor(D3[:, par, :], bank(BC, 128, 256), rows_bc[:, 512:640],
                                  ALU.add).then_inc(delta_done.sem, 1)
                dve.wait_ge(tanh_ready.sem, tanh_ready.count(p, b, 1))
                dve.wait_ge(delta_done.sem, delta_done.count(p, b, 1))
                dve.scalar_tensor_tensor(D3[:, par, :], TH[:, :], 1.0, D3[:, par, :], ALU.add,
                                         ALU.mult).then_inc(delta_done.sem, 1)
                dve.wait_ge(delta_done.sem, delta_done.count(p, b, 2))
                dve.scalar_tensor_tensor(X[:, b, :], D3[:, par, :], 0.5, X[:, b, :], ALU.mult,
                                         ALU.add).then_inc(x_final.sem, 1)

            def prep_only(p, b, par):
                normalise(p, b, par)
                copy_v(p, b, par)

            def step(p, b, par, tail, prep):
                tk = PHASES[tail[0]] if tail else None
                pk = PHASES[prep[0]] if prep else None
                kind, other = PHASES[p], 1 - par
                if kind == TOP:
                    top_step(p, b, par, tail, prep)
                    return
                softmax = kind in (SELF, CROSS, ROPE)
                if kind not in HEADS and pk and pk != EXPERTS:
                    normalise(*prep, other)
                if softmax:
                    maxima(p, b, 0)
                    subtract(p, b, 0)
                    normalise(*prep, other)
                if tk in MLPS:
                    gate_dve(*tail)
                if softmax:
                    maxima(p, b, 1)
                    subtract(p, b, 1)
                if tk in MLPS:
                    residual(*tail)
                if kind == GLU:
                    glu(p, b, par)
                if tk in MLPS:
                    statistics(tail[0] + 1, tail[1], other)
                if kind == PROTO:
                    proto_softmax(p, b, par)
                if softmax:
                    maxima(p, b, 2)
                if tk in HEADS:
                    norm_out(*tail)
                if softmax:
                    subtract(p, b, 2)
                if pk in HEADS or pk == PROTO:
                    copy_v(*prep, other)
                if pk == ROPE:
                    rope(*prep)
                if softmax:
                    maxima(p, b, 3)
                    subtract(p, b, 3)
                if tk in HEADS:
                    residual(*tail)
                    statistics(tail[0] + 1, tail[1], other)
                if tk == PROTO and kind == EXPERTS:
                    router_softmax()
                if tk == EXPERTS:
                    expert_tail(*tail, other)

            def top_step(p, b, par, tail, prep):
                first_8(p, b, 0)
                first_8(p, b, 1)
                normalise(*prep, 1 - par)
                replace_first(p, b, 0)
                replace_first(p, b, 1)
                next_8(p, b, 0)
                next_8(p, b, 1)
                replace_next(p, b, 0)
                replace_next(p, b, 1)
                mark_taken(p, b, 0)
                mark_taken(p, b, 1)
                first_8(p, b, 2)
                first_8(p, b, 3)
                norm_out(*tail)
                if PHASES[prep[0]] in HEADS:
                    copy_v(*prep, 1 - par)
                replace_first(p, b, 2)
                replace_first(p, b, 3)
                next_8(p, b, 2)
                next_8(p, b, 3)
                residual(*tail)
                replace_next(p, b, 2)
                statistics(tail[0] + 1, tail[1], 1 - par)
                replace_next(p, b, 3)
                mark_taken(p, b, 2)
                mark_taken(p, b, 3)

            def tail_only(p, b, par):
                expert_tail(p, b, par)

            for b in range(NB):
                statistics(0, b, b % 2)
            phases(dve.Fori, step, layer_setup, prep_only, tail_only)


SETUP_IN = {2: (1,), 5: (2,), 8: (3,)}
SETUP_DONE = [5, 10, 16, 19]
CONSTS = 11


def pack(inputs):
    def a(name):
        return np.asarray(inputs[name])

    def rows(m):
        k = m.shape[0] // P
        return m.reshape(k, P, -1).transpose(1, 0, 2).reshape(P, -1)

    L0, L1, L2, L3 = "L0_xcond_", "L1_xcond_", "L2_xcond_", "L3_xcond_"
    w0 = [a(L0 + n) for n in ("ada_w", "qkv_w", "sa_proj_w", "q_w", "kv_w", "ca_proj_w", "fc1_w")] + [
        rows(a(L0 + "fc2_w"))]
    w1 = [a(L1 + n) for n in ("w_ada", "w_qkv", "w_so", "w_q", "w_kv", "w_co", "w_m1")] + [rows(a(L1 + "w_m2"))]
    w2 = [a(L2 + n) for n in ("adaLN_W", "qkv_W", "attn_out_W", "cq_W", "ck_W", "cv_W", "co_W", "mlp_W1")] + [
        rows(a(L2 + "mlp_W2"))]
    e1 = a(L3 + "e_w1").reshape(NE, 3, P, 2, P).transpose(2, 0, 3, 1, 4).reshape(P, -1)
    e2 = a(L3 + "e_w2").reshape(NE * 2, P, P).transpose(1, 0, 2).reshape(P, -1)
    w3 = [a(L3 + n) for n in ("Wq", "Wk", "Wv")] + [rows(a(L3 + "router_W")), rows(a(L3 + "gate_w1")), e1, e2,
                                                     a(L3 + "gate_w2"), a(L3 + "out_w")]
    weights = [np.ascontiguousarray(np.concatenate(x, axis=1)) for x in (w0, w1, w2, w3)]
    names = {
        (0, "ada"): L0 + "ada_b", (0, "qkv"): L0 + "qkv_b", (0, "so"): L0 + "sa_proj_b", (0, "q"): L0 + "q_b",
        (0, "kv"): L0 + "kv_b", (0, "co"): L0 + "ca_proj_b", (0, "m1"): L0 + "fc1_b", (0, "m2"): L0 + "fc2_b",
        (1, "ada"): L1 + "b_ada", (1, "qkv"): L1 + "b_qkv", (1, "so"): L1 + "b_so", (1, "q"): L1 + "b_q",
        (1, "kv"): L1 + "b_kv", (1, "co"): L1 + "b_co", (1, "m1"): L1 + "b_m1", (1, "m2"): L1 + "b_m2",
        (2, "ada"): L2 + "adaLN_b", (2, "m1"): L2 + "mlp_b1", (2, "m2"): L2 + "mlp_b2",
        (3, "gamma"): L3 + "ln_gamma", (3, "beta"): L3 + "ln_beta", (3, "e1"): L3 + "e_b1",
        (3, "gate1"): L3 + "gate_b1"}
    cols = []
    for n, l, c in VECTORS:
        if (l, n) == (2, "norm"):
            v = np.concatenate([a(L2 + "norm1_w"), a(L2 + "normc_w"), a(L2 + "norm2_w")])
        else:
            v = a(names[l, n]).reshape(-1)
        cols.append(v.reshape(c, P).T)
    vec = np.ascontiguousarray(np.concatenate(cols, axis=1))
    rows5 = np.ascontiguousarray(np.concatenate(
        [a(L3 + "e_b2").reshape(-1), a(L3 + "gate_b2"), a(L3 + "out_b"), a(L3 + "router_b")]))
    return dict(
        x=np.ascontiguousarray(a("x").transpose(1, 0, 2)),
        ctx=np.ascontiguousarray(a("ctx_1024").transpose(2, 0, 1)),
        cond=np.ascontiguousarray(a("cond_1024").T),
        vec=vec, consts=constants(), rows=rows5,
        key_mask0=np.ascontiguousarray(a("mask_BxS2_bf0")).reshape(1, -1),
        key_mask2=np.ascontiguousarray(a("mask_BxS2_bf1")).reshape(1, -1),
        self_mask=np.ascontiguousarray(a("mask_SxS_bk0")),
        w0=weights[0], w1=weights[1], w2=weights[2], w3=weights[3])


def constants():
    c = np.zeros((P, NCONST), np.float32)
    c[:, C_ID:C_ID + P] = np.eye(P, dtype=np.float32)
    c[np.arange(P), C_HEAD + np.arange(P) // HD] = 1.0
    inv_freq = 1.0 / 10000.0 ** (np.arange(0, HD, 2, dtype=np.float32) / HD)
    freqs = np.outer(np.arange(P // 2, dtype=np.float32), inv_freq)
    emb = np.concatenate([freqs, freqs], axis=-1)
    c[:, C_COS:C_COS + P] = np.tile(np.cos(emb).astype(np.float32).T, (H, 2))
    c[:, C_SIN:C_SIN + P] = np.tile(np.sin(emb).astype(np.float32).T, (H, 2))
    inner = (np.arange(P) >= 32) & (np.arange(P) < 96)
    c[:, C_WIN:C_WIN + P] = np.where(inner[:, None] == inner[None, :], 0.0, NEG)
    return c


def kernel(**inputs):
    import concourse.bacc as bacc
    from concourse.bass_utils import run_bass_kernel_spmd

    nc = bacc.Bacc("TRN2", target_bir_lowering=False, num_devices=1)
    arrays, aps = {}, {}
    for name, arr in pack(inputs).items():
        arrays["in_" + name] = arr
        aps[name] = nc.dram_tensor("in_" + name, arr.shape, mybir.dt.from_np(arr.dtype), kind="ExternalInput").ap()
    out = nc.dram_tensor("out", (NB, P, P), mybir.dt.float32, kind="ExternalOutput").ap()
    build(nc, aps["x"], aps["ctx"], aps["cond"], aps["vec"], aps["consts"], aps["rows"], aps["key_mask0"],
          aps["key_mask2"], aps["self_mask"], [aps[f"w{l}"] for l in range(4)], out)
    r = run_bass_kernel_spmd(nc, [arrays], core_ids=[0])
    return r.results[0]["out"]
```

```python
from contextlib import ExitStack

import numpy as np

import concourse.bass as bass
from concourse import mybir

P = 128
NB = 8
H, HD = 16, 8
NC = 77
WIN = 64
SHIFT = 32
CH = 4
NCH = H // CH
HID = 4
NE = 3
NEG = -float(2 ** 100)
REPLACED = -3.0e38
SCALE = float(HD) ** -0.5
SCALE3 = float(P) ** -0.5

SELF, WINDOW, CROSS, TOP, ROPE, GELU, GLU, GELUT, PROTO, EXPERTS = (
    "self", "window", "cross", "top", "rope", "gelu", "glu", "gelut", "proto", "experts")
PHASES = [SELF, CROSS, GELU, WINDOW, TOP, GLU, ROPE, CROSS, GELUT, PROTO, EXPERTS]
LAYER = [0, 0, 0, 1, 1, 1, 2, 2, 2, 3, 3]
HEADS = (SELF, WINDOW, CROSS, TOP, ROPE)
SOFTMAX = (SELF, WINDOW, CROSS, ROPE)
MLPS = (GELU, GLU, GELUT)
CTX = (CROSS, TOP, PROTO)
EPS = [1e-6, 1e-6, 1e-5, 1e-5]

WEIGHTS = [
    [("ada", 768), ("qkv", 384), ("so", 128), ("q", 128), ("kv", 256), ("co", 128), ("m1", 512), ("m2", 512)],
    [("ada", 1152), ("qkv", 384), ("so", 128), ("q", 128), ("kv", 256), ("co", 128), ("m1", 1024), ("m2", 512)],
    [("ada", 1152), ("qkv", 384), ("so", 128), ("q", 128), ("kv", 256), ("co", 128), ("m1", 512), ("m2", 512)],
    [("q", 128), ("kv", 256), ("router", 9), ("gate1", 384), ("e1", 2304), ("e2", 768), ("gate2", 128),
     ("out", 128)],
]
WCOL, WSIZE = [], []
for _l in WEIGHTS:
    _at, _d = 0, {}
    for _n, _c in _l:
        _d[_n] = _at
        _at += _c
    WCOL.append(_d)
    WSIZE.append(_at)

VECTORS = [("ada", 0, 6), ("qkv", 0, 3), ("q", 0, 1), ("kv", 0, 2), ("so", 0, 1), ("co", 0, 1), ("m1", 0, 4),
           ("m2", 0, 1),
           ("ada", 1, 9), ("qkv", 1, 3), ("q", 1, 1), ("kv", 1, 2), ("so", 1, 1), ("co", 1, 1), ("m1", 1, 8),
           ("m2", 1, 1),
           ("ada", 2, 9), ("norm", 2, 3), ("m1", 2, 4), ("m2", 2, 1),
           ("beta", 3, 1), ("gamma", 3, 1), ("e1", 3, 6), ("gate1", 3, 1)]
VCOL, _at = {}, 0
for _n, _l, _c in VECTORS:
    VCOL[_l, _n] = _at
    _at += _c
NVEC = _at

C_ID, C_HEAD, C_COS, C_SIN, NCONST = 0, 128, 144, 272, 400


def kinds(**rates):
    out = {}
    for names, rate in rates.items():
        for k in {"heads": HEADS, "softmax": SOFTMAX, "mlps": MLPS, "ctx": CTX}.get(names, (names,)):
            out[k] = out.get(k, 0) + rate
    return out


class Event:

    def __init__(self, sem, rates, first=0):
        self.sem, self.rates, self.base = sem, rates, [first]
        for kind in PHASES:
            self.base.append(self.base[-1] + NB * rates.get(kind, 0))

    def count(self, p, b, k):
        return self.base[p] + self.rates[PHASES[p]] * b + k

    def all_of(self, p):
        return self.base[p + 1]


def wait(eng, event, count):
    if isinstance(count, int) and count <= 0:
        return
    eng.wait_ge(event.sem, count)


def build(nc, x, ctx_t, cond_t, vec, consts, rows, key_mask0, key_mask2, self_mask, w_dram, out):
    fp32, bf16, u8 = mybir.dt.float32, mybir.dt.bfloat16, mybir.dt.uint8
    ALU, ACT, AX = mybir.AluOpType, mybir.ActivationFunctionType, mybir.AxisListType

    ctx = ExitStack()
    with ctx:
        def sb(name, shape, dt=fp32):
            return ctx.enter_context(nc.sbuf_tensor(name, shape, dt))

        def sem(name):
            return ctx.enter_context(nc.semaphore(name))

        def event(name, **rates):
            return Event(sem(name), kinds(**rates))

        def open_event(name, first=1, **rates):
            return Event(sem(name), kinds(**rates), first)

        X = sb("X", [P, NB, P])
        CT = sb("CT", [P, NB, NC])
        condT = sb("condT", [P, NB])
        silu_cond = sb("silu_cond", [P, NB])
        VEC = sb("VEC", [P, NVEC])
        CONST = sb("CONST", [P, NCONST])
        W = [sb(f"W{l}", [P, WSIZE[l]]) for l in range(4)]
        rope_w = sb("rope_w", [P, 2 * P])
        ident_b = sb("ident_b", [P, P], bf16)
        self_mask_u = sb("self_mask_u", [P, P], u8)
        self_mask_b = sb("self_mask_b", [P, P], bf16)
        key_mask_u = sb("key_mask_u", [1, 2, NB * NC], u8)
        key_mask_b = sb("key_mask_b", [1, 2, NB * NC], bf16)
        ones_b = sb("ones_b", [1, P], bf16)
        PRM = sb("PRM", [P, 10, 4, NB])
        eff_bias = sb("eff_bias", [P, 2])
        minus_half = sb("minus_half", [P, 1])
        expert_bias = sb("expert_bias", [P, 7, NB])
        rows_bc = sb("rows_bc", [P, 5 * P + NE])

        stats = sb("stats", [P, 2, 6])
        mean_var = sb("mean_var", [P, 2, 2])
        var_eps = sb("var_eps", [P, 2])
        mean = sb("mean", [P, NB])
        rstd = sb("rstd", [P, NB])
        XN = sb("XN", [P, 2, P])
        HT = sb("HT", [P, 2, P])
        CS = sb("CS", [P, 2, NC])
        QK = sb("QK", [P, 2, 2, P])
        rope_prod = sb("rope_prod", [P, 2, 2, P])
        V = sb("V", [P, 2, H, 32])
        VW = sb("VW", [P, 2, 2, H // 2, 64])
        KM = sb("KM", [P, 2, H, P])
        MX = sb("MX", [P, 2, CH])
        D = sb("D", [P, 2, CH, P])
        E = sb("E", [P, 2, CH, P])
        PT = sb("PT", [P, 2, CH, P])
        top8a = sb("top8a", [P, 2, CH, 8])
        top8b = sb("top8b", [P, 2, CH, 8])
        left_a = sb("left_a", [P, 2, CH, NC])
        left_b = sb("left_b", [P, 2, CH, NC])
        taken = sb("taken", [P, 2, CH, NC])
        E1 = sb("E1", [P, 2, CH, NC])
        OT = sb("OT", [P, NCH, P])
        rsum = sb("rsum", [P, H])
        ON = sb("ON", [P, P])
        ONT = sb("ONT", [P, P])
        Y = sb("Y", [P, P])
        G = sb("G", [P, 2, HID, P])
        SG = sb("SG", [P, 2, HID, P])
        NX = sb("NX", [P, NB, P])
        EV = sb("EV", [P, NB, P])
        V3 = sb("V3", [P, 2, P])
        sum3 = sb("sum3", [P, 2, 2])
        PR = sb("PR", [P, NB, NE])
        rt = sb("rt", [P, 4, NB])
        HE = sb("HE", [P, 2, 7, P])
        ES = sb("ES", [P, 2, P])
        router_bias = sb("router_bias", [P, NB, NE])
        BM = sb("BM", [P, 2, P])
        BE = sb("BE", [P, 2, NE, P])
        GB = sb("GB", [P, P])
        TH = sb("TH", [P, P])
        RT = sb("RT", [P, P])
        R3 = sb("R3", [P, 2, P])
        D3 = sb("D3", [P, 2, P])
        PS = ctx.enter_context(nc.psum_tensor("PS", [P, 8, 512], fp32))

        BS, BT, BO, BA, BB, BC = 0, 2, 4, 5, 6, 7
        ident = CONST[:, C_ID:C_ID + P]

        def w(l, name, at=0, n=P):
            c = WCOL[l][name] + at
            return W[l][:, c:c + n]

        def vcol(l, name, j=0, rows=P):
            c = VCOL[l, name] + j
            return VEC[0:rows, c:c + 1]

        def bank(i, a, b, rows=P):
            return PS[0:rows, i, a:b]

        loaded = {n: sem("loaded_" + n) for n in (
            "condition", "vectors", "heads", "tables", "x", "x_rest", "context", "masks", "ada0", "w0", "w1", "w2",
            "w3", "rows")}
        silu_ready = sem("silu_ready")
        consts_ready = sem("consts_ready")
        window_zeros = sem("window_zeros")
        masks_ready = sem("masks_ready")
        ada_done = sem("ada_done")
        params_ready = sem("params_ready")
        stats_done = event("stats_done", heads=2, mlps=2, proto=2)
        rstd_done = event("rstd_done", heads=3, mlps=3, proto=3)
        xn_ready = event("xn_ready", heads=1, mlps=1, proto=1)
        xnT_done = event("xnT_done", heads=1, mlps=1, proto=1)
        h_ready = event("h_ready", heads=1, mlps=1, proto=1)
        ctx_ready = event("ctx_ready", ctx=1)
        v_proj = event("v_proj", heads=1, proto=1)
        v_ready = event("v_ready", heads=1, proto=1)
        qk_proj = event("qk_proj", heads=1, proto=1)
        qk_ready = event("qk_ready", self=1, window=1, cross=1, top=1, proto=1)
        rope_mults = event("rope_mults", rope=1)
        rope_ready = event("rope_ready", rope=1)
        km_ready = event("km_ready", heads=NCH)
        s_done = event("s_done", heads=NCH)
        max_done = event("max_done", softmax=NCH)
        sub_done = event("sub_done", softmax=NCH)
        top_a = event("top_a", top=NCH)
        left_a_ready = event("left_a_ready", top=NCH)
        top_b = event("top_b", top=NCH)
        left_b_ready = event("left_b_ready", top=NCH)
        negm_ready = event("negm_ready", top=NCH)
        exp1_done = event("exp1_done", top=NCH)
        taken_ready = event("taken_ready", top=NCH)
        sel_ready = event("sel_ready", top=NCH)
        exp_done = event("exp_done", softmax=NCH)
        t_done = event("t_done", heads=NCH)
        pt_ready = event("pt_ready", heads=NCH)
        pv_done = event("pv_done", heads=NCH)
        oT_copied = event("oT_copied", heads=1)
        otr_done = event("otr_done", heads=1)
        rsum_ready = event("rsum_ready", heads=1)
        on_ready = event("on_ready", heads=1)
        onT_done = event("onT_done", heads=1)
        onT_ready = event("onT_ready", heads=1)
        y_done = event("y_done", heads=1, mlps=1)
        y_gated = event("y_gated", heads=1, mlps=1)
        yT_done = event("yT_done", heads=1, mlps=1)
        x_updated = open_event("x_updated", heads=1, mlps=1)
        fc1_done = event("fc1_done", mlps=2)
        act_done = event("act_done", mlps=2)
        glu_ready = event("glu_ready", glu=2)
        ps_done = event("ps_done", proto=1)
        pmax_done = event("pmax_done", proto=1)
        psub_done = event("psub_done", proto=1)
        pexp_done = event("pexp_done", proto=1)
        prec_done = event("prec_done", proto=1)
        pw_ready = event("pw_ready", proto=1)
        pwT_done = event("pwT_done", proto=1)
        pwT_ready = event("pwT_ready", proto=1)
        ev_done = event("ev_done", proto=1)
        ev_ready = event("ev_ready", proto=1)
        nx_kept = event("nx_kept", proto=1)
        ev_kept = open_event("ev_kept", 2, proto=1)
        lx_done = event("lx_done", proto=1)
        lg_done = event("lg_done", proto=1)
        router_done = sem("router_done")
        router_exp = sem("router_exp")
        eh_done = event("eh_done", experts=2)
        eh_ready = event("eh_ready", experts=2)
        ey_done = event("ey_done", experts=1)
        be_ready = event("be_ready", experts=2)
        bm_ready = event("bm_ready", experts=1)
        gb_ready = open_event("gb_ready", experts=1)
        tanh_ready = event("tanh_ready", experts=1)
        mix_done = event("mix_done", experts=3)
        rT_done = event("rT_done", experts=1)
        rT_ready = event("rT_ready", experts=1)
        r_done = event("r_done", experts=1)
        delta_done = open_event("delta_done", experts=2)
        x_final = event("x_final", experts=1)
        stored = sem("stored")

        passed_dve, passed_pool = sem("passed_dve"), sem("passed_pool")

        def nk(kind):
            return NC if kind in CTX else WIN if kind == WINDOW else P

        def hidden_banks(par):
            return (BS, BS + 1) if par == 0 else (BT, BT + 1)

        def hidden_blocks(kind):
            return (4, 3) if kind == EXPERTS else (HID // 2, HID // 2)

        def s_free(eng, p, b, c):
            kind = PHASES[p]
            ev = exp1_done if kind == TOP else sub_done
            if isinstance(b, int) and b == 0 and c < 2:
                banks_left(eng, p)
            else:
                wait(eng, ev, ev.count(p, b, c - 1))

        def banks_left(eng, p):
            if p == 0:
                return
            before = PHASES[p - 1]
            if before in SOFTMAX:
                wait(eng, sub_done, sub_done.all_of(p - 1))
            if before == TOP:
                wait(eng, exp1_done, exp1_done.all_of(p - 1))
            if before in MLPS:
                ev = glu_ready if before == GLU else act_done
                wait(eng, ev, ev.count(p - 1, NB - 1, 0))
            if before == PROTO:
                wait(eng, psub_done, psub_done.all_of(p - 1))

        block = ctx.enter_context(nc.Block())

        def phases(fori, step, layer_setup, prep_only, tail_only):
            layer_setup(0)
            prep_only(0, 0, 0)
            last = len(PHASES) - 1
            for p in range(last + 1):
                step(p, 0, 0, (p - 1, NB - 1) if p else None, (p, 1))
                with fori(0, 3) as i:
                    for side in range(2):
                        b = 2 * i + (1 + side)
                        par = (1 + side) % 2
                        step(p, b, par, (p, b - 1), (p, b + 1))
                for l in SETUP_IN.get(p, ()):
                    layer_setup(l)
                step(p, NB - 1, 1, (p, NB - 2), (p + 1, 0) if p < last else None)
            tail_only(last, NB - 1, 1)

        @block.sync
        def _(sp):
            sp.dma_start(condT[:, :], cond_t).then_inc(loaded["condition"], 16)
            sp.dma_start(VEC[:, :], vec).then_inc(loaded["vectors"], 16)
            sp.dma_start(CONST[:, 0:C_COS], consts[:, 0:C_COS]).then_inc(loaded["heads"], 16)
            c = WCOL[0]["qkv"]
            sp.dma_start(W[0][:, c:], w_dram[0][:, c:]).then_inc(loaded["w0"], 16)
            sp.wait_ge(loaded["ada0"], 16)
            sp.wait_ge(loaded["x_rest"], 16)
            sp.dma_start(CT[:, :, :], ctx_t).then_inc(loaded["context"], 16)
            sp.dma_start(key_mask_u[:, 0, :], key_mask0).then_inc(loaded["masks"], 16)
            sp.dma_start(key_mask_u[:, 1, :], key_mask2).then_inc(loaded["masks"], 16)
            sp.dma_start(self_mask_u[:, :], self_mask).then_inc(loaded["masks"], 16)
            sp.wait_ge(loaded["w0"], 16)
            sp.dma_start(W[1][:, :], w_dram[1]).then_inc(loaded["w1"], 16)
            sp.dma_start(CONST[:, C_COS:], consts[:, C_COS:]).then_inc(loaded["tables"], 16)
            sp.dma_start(W[2][:, :], w_dram[2]).then_inc(loaded["w2"], 16)
            sp.dma_start(W[3][:, :], w_dram[3]).then_inc(loaded["w3"], 16)
            sp.dma_start(rows_bc[:, :], rows.partition_broadcast(P)).then_inc(loaded["rows"], 16)
            p = len(PHASES) - 1
            with sp.Fori(0, NB) as b:
                sp.wait_ge(x_final.sem, x_final.count(p, b, 1))
                sp.dma_start(out[b, :, :], X[:, b, :]).then_inc(stored, 16)
            sp.wait_ge(stored, 16 * NB)

        @block.gpsimd
        def _(pool):
            pool.sem_inc(ev_kept.sem, 2)
            pool.memset(minus_half[:, :], -0.5).then_inc(consts_ready, 1)
            pool.memset(VW[:, :, :, :, :], 0.0).then_inc(window_zeros, 1)

            def layer_setup(l):
                pass

            def norm(p, b, par):
                pool.wait_ge(stats_done.sem, stats_done.count(p, b, 2))
                pool.sem_inc(passed_pool, 1)
                pool.tensor_scalar(var_eps[:, par:par + 1], mean_var[:, par, 1:2], EPS[LAYER[p]], None,
                                   ALU.add).then_inc(rstd_done.sem, 1)
                pool.tensor_copy(mean[:, bass.ds(b, 1)], mean_var[:, par, 0:1]).then_inc(rstd_done.sem, 1)
                pool.wait_ge(rstd_done.sem, rstd_done.count(p, b, 1))
                pool.tensor_tensor(rstd[:, bass.ds(b, 1)], var_eps[:, par:par + 1], minus_half[:, :],
                                   ALU.pow).then_inc(rstd_done.sem, 1)

            def context(p, b, par):
                if not (isinstance(b, int) and b < 2):
                    wait(pool, qk_proj, qk_proj.count(p, b, -1))
                if isinstance(b, int) and b == 0:
                    pool.wait_ge(loaded["context"], 16)
                pool.tensor_copy(CS[:, par, :], CT[:, b, :]).then_inc(ctx_ready.sem, 1)

            def mask_heads(p, b, par, c):
                kind, n = PHASES[p], NC if PHASES[p] in CTX else P
                if c == 0:
                    if kind == ROPE:
                        pool.wait_ge(rope_ready.sem, rope_ready.count(p, b, 1))
                    else:
                        pool.wait_ge(qk_ready.sem, qk_ready.count(p, b, 1))
                    wait(pool, s_done, s_done.count(p, b, -NCH))
                pool.tensor_tensor(
                    KM[:, par, CH * c:CH * c + CH, 0:n],
                    QK[:, par, 1, 0:n].unsqueeze(1).broadcast_to([P, CH, n]),
                    CONST[:, C_HEAD + CH * c:C_HEAD + CH * c + CH].unsqueeze(2).broadcast_to([P, CH, n]),
                    ALU.mult).then_inc(km_ready.sem, 1)

            def rotate(p, b, par):
                pool.wait_ge(rope_mults.sem, rope_mults.count(p, b, 1))
                pool.tensor_tensor(QK[:, par, :, :], rope_prod[:, 0, :, :], rope_prod[:, 1, :, :],
                                   ALU.add).then_inc(rope_ready.sem, 1)

            def select(p, b, c):
                r = c % 2
                pool.wait_ge(exp1_done.sem, exp1_done.count(p, b, c + 1))
                pool.wait_ge(taken_ready.sem, taken_ready.count(p, b, c + 1))
                wait(pool, t_done, t_done.count(p, b, c - 1))
                pool.tensor_tensor(E[:, r, :, 0:NC], E1[:, r, :, :], taken[:, r, :, :],
                                   ALU.mult).then_inc(sel_ready.sem, 1)

            def keep_nx(p, b, par):
                pool.wait_ge(h_ready.sem, h_ready.count(p, b, 1))
                pool.tensor_copy(NX[:, b, :], HT[:, par, :]).then_inc(nx_kept.sem, 1)

            def keep_ev(p, b, par):
                pool.wait_ge(ev_ready.sem, ev_ready.count(p, b, 1))
                pool.tensor_copy(EV[:, b, :], ES[:, par, :]).then_inc(ev_kept.sem, 1)

            def routed_bias(p, b, par):
                if isinstance(b, int) and b == 0:
                    pool.wait_ge(router_done, 7)
                wait(pool, delta_done, delta_done.count(p, b, -2))
                pool.tensor_tensor(BE[:, par, :, :], rows_bc[:, 0:NE * P].rearrange("p (e q) -> p e q", e=NE),
                                   PR[:, b, :].unsqueeze(2).broadcast_to([P, NE, P]),
                                   ALU.mult).then_inc(be_ready.sem, 1)
                pool.wait_ge(be_ready.sem, be_ready.count(p, b, 1))
                pool.tensor_tensor(BE[:, par, 1, :], BE[:, par, 0, :], BE[:, par, 1, :],
                                   ALU.add).then_inc(be_ready.sem, 1)
                pool.wait_ge(be_ready.sem, be_ready.count(p, b, 2))
                pool.tensor_tensor(BM[:, par, :], BE[:, par, 1, :], BE[:, par, 2, :], ALU.add).then_inc(bm_ready.sem, 1)

            def prep_only(p, b, par):
                for i in range(NB // 2, NB):
                    norm(0, i, i % 2)
                pool.wait_ge(loaded["heads"], 16)
                for c in range(NCH):
                    mask_heads(p, b, par, c)

            def step(p, b, par, tail, prep):
                tk = PHASES[tail[0]] if tail else None
                pk = PHASES[prep[0]] if prep else None
                if tk == TOP:
                    select(*tail, 2)
                    select(*tail, 3)
                if pk in CTX:
                    context(*prep, 1 - par)
                if tk == PROTO:
                    keep_ev(*tail, 1 - par)
                if pk == PROTO:
                    keep_nx(*prep, 1 - par)
                if PHASES[p] == EXPERTS:
                    routed_bias(p, b, par)
                if PHASES[p] == TOP:
                    select(p, b, 0)
                    select(p, b, 1)
                if pk == ROPE:
                    rotate(*prep, 1 - par)
                if pk in HEADS:
                    for c in range(NCH):
                        mask_heads(*prep, 1 - par, c)
                if tk in HEADS + MLPS:
                    norm(tail[0] + 1, tail[1], 1 - par)

            def tail_only(p, b, par):
                pass

            for b in range(NB // 2):
                norm(0, b, b % 2)
            phases(pool.Fori, step, layer_setup, prep_only, tail_only)

        @block.scalar
        def _(act):
            act.dma_start(W[0][:, 0:WCOL[0]["qkv"]], w_dram[0][:, 0:WCOL[0]["qkv"]]).then_inc(loaded["ada0"], 16)
            act.dma_start(X[:, 0:NB // 2, :], x[:, 0:NB // 2, :]).then_inc(loaded["x"], 16)
            act.dma_start(X[:, NB // 2:, :], x[:, NB // 2:, :]).then_inc(loaded["x_rest"], 16)
            act.wait_ge(loaded["condition"], 16)
            act.activation(silu_cond[:, :], condT[:, :], ACT.Silu).then_inc(silu_ready, 1)

            def layer_setup(l):
                act.wait_ge(params_ready, SETUP_DONE[l])

            def modulate(p, b, par):
                act.wait_ge(xnT_done.sem, xnT_done.count(p, b, 1))
                if PHASES[p] == PROTO:
                    wait(act, nx_kept, nx_kept.count(p, b, -1))
                pieces = [(0, SHIFT, P - SHIFT), (P - SHIFT, 0, SHIFT)] if PHASES[p] == WINDOW else [(0, 0, P)]
                for to, at, n in pieces:
                    ins = act.activation(HT[:, par, to:to + n], bank(BA, 384 + at, 384 + at + n), ACT.Identity,
                                         scale=PRM[:, p, 1, bass.ds(b, 1)], bias=PRM[:, p, 0, bass.ds(b, 1)])
                ins.then_inc(h_ready.sem, 1)

            def copy_qk(p, b, par):
                kind, l, n = PHASES[p], LAYER[p], nk(PHASES[p])
                if kind == ROPE:
                    return
                act.wait_ge(qk_proj.sem, qk_proj.count(p, b, 1))
                if kind in (SELF, WINDOW):
                    act.activation(QK[:, par, 0, :], bank(BA, 128, 256), ACT.Identity, bias=vcol(l, "qkv", 0))
                    act.activation(QK[:, par, 1, :], bank(BA, 256, 384), ACT.Identity,
                                   bias=vcol(l, "qkv", 1)).then_inc(qk_ready.sem, 1)
                elif l in (0, 1):
                    act.activation(QK[:, par, 0, :], bank(BA, 128, 256), ACT.Identity, bias=vcol(l, "q"))
                    act.activation(QK[:, par, 1, 0:n], bank(BA, 256, 256 + n), ACT.Identity,
                                   bias=vcol(l, "kv", 0)).then_inc(qk_ready.sem, 1)
                else:
                    act.activation(QK[:, par, 0, :], bank(BA, 128, 256), ACT.Copy)
                    act.activation(QK[:, par, 1, 0:n], bank(BA, 256, 256 + n), ACT.Copy).then_inc(qk_ready.sem, 1)

            def exps(p, b, c):
                kind, n, r = PHASES[p], nk(PHASES[p]), c % 2
                if kind == TOP:
                    act.wait_ge(negm_ready.sem, negm_ready.count(p, b, c + 1))
                    act.wait_ge(left_a_ready.sem, left_a_ready.count(p, b, c + 1))
                    wait(act, sel_ready, sel_ready.count(p, b, c - 1))
                    for j in range(CH):
                        ins = act.activation(E1[:, r, j, :], bank(BS + r, j * n, j * n + n), ACT.Exp,
                                             scale=SCALE, bias=MX[:, r, j:j + 1])
                    ins.then_inc(exp1_done.sem, 1)
                    return
                act.wait_ge(sub_done.sem, sub_done.count(p, b, c + 1))
                wait(act, t_done, t_done.count(p, b, c - 1))
                dst = E[:, r, 0:CH // 2, :].rearrange("p i (h k) -> p (i h) k", h=2) if kind == WINDOW else (
                    E[:, r, :, 0:n])
                act.activation(dst, D[:, r, :, 0:n], ACT.Exp, scale=SCALE).then_inc(exp_done.sem, 1)

            def copy_pt(p, b, c):
                n, r = nk(PHASES[p]), c % 2
                act.wait_ge(t_done.sem, t_done.count(p, b, c + 1))
                wait(act, pv_done, pv_done.count(p, b, c - 1))
                if PHASES[p] == WINDOW:
                    act.activation(PT[:, r, 0:CH // 2, :], bank(BT + r, 0, CH // 2 * P),
                                   ACT.Copy).then_inc(pt_ready.sem, 1)
                    return
                act.activation(PT[0:n, r, :, :], bank(BT + r, 0, CH * P, n), ACT.Copy).then_inc(pt_ready.sem, 1)

            def copy_o(p, b):
                act.wait_ge(pv_done.sem, pv_done.count(p, b, NCH))
                act.activation(OT[:, :, :], bank(BO, 0, 512), ACT.Copy).then_inc(oT_copied.sem, 1)

            def copy_on(p, b):
                act.wait_ge(onT_done.sem, onT_done.count(p, b, 1))
                pieces = [(SHIFT, 0, P - SHIFT), (0, P - SHIFT, SHIFT)] if PHASES[p] == WINDOW else [(0, 0, P)]
                for to, at, n in pieces:
                    ins = act.activation(ONT[:, to:to + n], bank(BC, at, at + n), ACT.Copy)
                ins.then_inc(onT_ready.sem, 1)

            def gate(p, b):
                act.wait_ge(y_done.sem, y_done.count(p, b, 1))
                act.activation(Y[:, :], bank(BC, 128, 256), ACT.Identity, scale=PRM[:, p, 2, bass.ds(b, 1)],
                               bias=PRM[:, p, 3, bass.ds(b, 1)]).then_inc(y_gated.sem, 1)

            def hidden(p, b, par, half):
                kind, l = PHASES[p], LAYER[p]
                done, ready = (eh_done, eh_ready) if kind == EXPERTS else (fc1_done, act_done)
                act.wait_ge(done.sem, done.count(p, b, half + 1))
                func = {GELU: ACT.Gelu, GELUT: ACT.Gelu_apprx_tanh, GLU: ACT.Silu, EXPERTS: ACT.Silu}[kind]
                dst = {GLU: SG, EXPERTS: HE}.get(kind, G)
                first = half * hidden_blocks(kind)[0]
                for j in range(hidden_blocks(kind)[half]):
                    bias = expert_bias[:, first + j, bass.ds(b, 1)] if kind == EXPERTS else vcol(l, "m1", first + j)
                    ins = act.activation(dst[:, par, first + j, :], bank(hidden_banks(par)[half], j * P, j * P + P),
                                         func, bias=bias)
                ins.then_inc(ready.sem, 1)

            def proto_exp(p, b, par):
                act.wait_ge(psub_done.sem, psub_done.count(p, b, 1))
                act.activation(E[:, par, 0, 0:NC], D[:, par, 0, 0:NC], ACT.Exp, scale=SCALE3,
                               accum_out=sum3[:, par, 0:1]).then_inc(pexp_done.sem, 1)

            def copy_pwT(p, b, par):
                act.wait_ge(pwT_done.sem, pwT_done.count(p, b, 1))
                act.activation(PT[0:NC, par, 0, :], bank(BT + par, 0, P, NC), ACT.Copy).then_inc(pwT_ready.sem, 1)

            def copy_ev(p, b, par):
                act.wait_ge(ev_done.sem, ev_done.count(p, b, 1))
                act.wait_ge(ev_kept.sem, ev_kept.count(p, b, -1))
                act.activation(ES[:, par, :], bank(BO, 0, P), ACT.Copy).then_inc(ev_ready.sem, 1)

            def prep_only(p, b, par):
                modulate(p, b, par)
                copy_qk(p, b, par)

            def step(p, b, par, tail, prep):
                tk = PHASES[tail[0]] if tail else None
                pk = PHASES[prep[0]] if prep else None
                kind = PHASES[p]
                if kind == TOP:
                    top_step(p, b, par, tail, prep)
                    return
                if kind == PROTO:
                    proto_step(p, b, par, tail, prep)
                    return
                if tk in HEADS:
                    copy_pt(*tail, 2)
                    if tk != TOP:
                        exps(*tail, 3)
                    copy_pt(*tail, 3)
                if tk == PROTO:
                    copy_pwT(*tail, 1 - par)
                if kind in HEADS:
                    exps(p, b, 0)
                if tk in HEADS:
                    copy_o(*tail)
                if kind in MLPS + (EXPERTS,):
                    hidden(p, b, par, 0)
                if pk and pk != EXPERTS:
                    modulate(*prep, 1 - par)
                if tk == PROTO:
                    copy_ev(*tail, 1 - par)
                if kind in HEADS:
                    copy_pt(p, b, 0)
                    exps(p, b, 1)
                if kind in MLPS:
                    hidden(p, b, par, 1)
                if pk in HEADS or pk == PROTO:
                    copy_qk(*prep, 1 - par)
                if kind in HEADS:
                    copy_pt(p, b, 1)
                if tk in HEADS:
                    copy_on(*tail)
                if kind in HEADS:
                    exps(p, b, 2)
                if tk in HEADS:
                    gate(*tail)
                if tk == PROTO and kind == EXPERTS:
                    act.wait_ge(router_done, 4)
                    act.activation(PR[:, :, :], PR[:, :, :], ACT.Exp).then_inc(router_exp, 1)
                if tk == EXPERTS:
                    expert_tail(*tail)
                if kind == EXPERTS:
                    hidden(p, b, par, 1)

            def proto_step(p, b, par, tail, prep):
                if PHASES[prep[0]] == PROTO:
                    modulate(*prep, 1 - par)
                if PHASES[tail[0]] == PROTO:
                    copy_pwT(*tail, 1 - par)
                proto_exp(p, b, par)
                if PHASES[tail[0]] == PROTO:
                    copy_ev(*tail, 1 - par)
                if PHASES[prep[0]] == PROTO:
                    copy_qk(*prep, 1 - par)

            def top_step(p, b, par, tail, prep):
                copy_pt(*tail, 2)
                if PHASES[tail[0]] == WINDOW:
                    exps(*tail, 3)
                exps(p, b, 0)
                copy_pt(*tail, 3)
                exps(p, b, 1)
                copy_o(*tail)
                modulate(*prep, 1 - par)
                if PHASES[prep[0]] in HEADS:
                    copy_qk(*prep, 1 - par)
                copy_on(*tail)
                copy_pt(p, b, 0)
                gate(*tail)
                copy_pt(p, b, 1)
                exps(p, b, 2)
                exps(p, b, 3)

            def expert_tail(p, b):
                act.wait_ge(gb_ready.sem, gb_ready.count(p, b, 1))
                act.activation(TH[:, :], GB[:, :], ACT.Tanh, scale=0.5).then_inc(tanh_ready.sem, 1)
                act.wait_ge(rT_done.sem, rT_done.count(p, b, 1))
                act.activation(RT[:, :], bank(BC, 0, P), ACT.Copy).then_inc(rT_ready.sem, 1)

            def tail_only(p, b, par):
                expert_tail(p, b)

            phases(act.Fori, step, layer_setup, prep_only, tail_only)

        @block.tensor
        def _(pe):
            def layer_setup(l):
                pe.wait_ge(loaded[f"w{l}" if l else "ada0"], 16)
                if l == 0:
                    pe.wait_ge(loaded["vectors"], 16)
                    pe.wait_ge(silu_ready, 1)
                else:
                    pe.wait_ge(params_ready, SETUP_DONE[l - 1])
                    p = [p for p in SETUP_IN if l in SETUP_IN[p]][0]
                    wait(pe, on_ready, on_ready.count(p, NB - 2, 0) if PHASES[p] in HEADS else on_ready.base[p])
                src = silu_cond if l < 2 else condT
                if l < 3:
                    for j in range(6 if l == 0 else 9):
                        ins = pe.matmul(bank(BB, j * NB, j * NB + NB), w(l, "ada", j * P), src[:, :],
                                        start=True, stop=True)
                    if l == 0:
                        pe.wait_ge(loaded["w0"], 16)
                    if l < 2:
                        pe.matmul(bank(BB, 128, 129), w(l, "so"), vcol(l, "qkv", 2), start=True, stop=True)
                        ins = pe.matmul(bank(BB, 129, 130), w(l, "co"), vcol(l, "kv", 1), start=True, stop=True)
                    ins.then_inc(ada_done, 1)
                else:
                    for j in range(6):
                        pe.matmul(bank(BB, j * NB, j * NB + NB), w(3, "e1", (j * 3 + 2) * P), src[:, :],
                                  start=True, stop=True)
                    pe.matmul(bank(BB, 48, 56), w(3, "gate1", 2 * P), src[:, :], start=True, stop=True)
                    for b in range(NB):
                        ins = pe.matmul(bank(BB, 64 + NE * b, 64 + NE * b + NE),
                                        condT[:, b:b + 1].broadcast_to([P, P]), w(3, "router", 2 * NE, NE),
                                        start=True, stop=True)
                    ins.then_inc(ada_done, 1)

            def xn_transpose(p, b, par):
                pe.wait_ge(xn_ready.sem, xn_ready.count(p, b, 1))
                q, kind = (p, b - 1) if not (isinstance(b, int) and b == 0) else (p - 1, NB - 1), None
                if q[0] >= 0:
                    kind = PHASES[q[0]]
                    ev = rope_mults if kind == ROPE else qk_ready if kind in HEADS or kind == PROTO else h_ready
                    pe.wait_ge(ev.sem, ev.count(*q, 1))
                pe.transpose(bank(BA, 384, 512), XN[:, par, :], ident).then_inc(xnT_done.sem, 1)

            def project_v(p, b, par, tail):
                kind, l, n = PHASES[p], LAYER[p], nk(PHASES[p])
                if tail and PHASES[tail[0]] in HEADS:
                    pe.wait_ge(x_updated.sem, x_updated.count(*tail, 0))
                elif tail and PHASES[tail[0]] in MLPS:
                    pe.wait_ge(x_updated.sem, x_updated.count(*tail, 1))
                elif tail:
                    pe.wait_ge(x_updated.sem, x_updated.all_of(tail[0] - 1))
                if kind in CTX:
                    pe.wait_ge(ctx_ready.sem, ctx_ready.count(p, b, 1))
                    pe.matmul(bank(BC, 384, 512, n), CS[:, par, :], w(l, "kv", P), start=True,
                              stop=True).then_inc(v_proj.sem, 1)
                elif kind == WINDOW:
                    pe.wait_ge(h_ready.sem, h_ready.count(p, b, 1))
                    wv = w(l, "qkv", 2 * P).rearrange("p (i t d) -> p t i d", t=2, d=HD)
                    for t in range(2):
                        for win in range(2):
                            ins = pe.matmul(PS[WIN * t:WIN * t + WIN, BC, 384 + 64 * win:448 + 64 * win],
                                            HT[:, par, WIN * win:WIN * win + WIN], wv[:, t, :, :], start=True,
                                            stop=True, skip_group_check=True)
                    ins.then_inc(v_proj.sem, 1)
                else:
                    pe.wait_ge(h_ready.sem, h_ready.count(p, b, 1))
                    pe.matmul(bank(BC, 384, 512), HT[:, par, :], w(l, "qkv", 2 * P), start=True,
                              stop=True).then_inc(v_proj.sem, 1)

            def project_qk(p, b, par):
                kind, l, n = PHASES[p], LAYER[p], nk(PHASES[p])
                if kind == ROPE:
                    for j, wt in enumerate((w(2, "qkv", 0), w(2, "qkv", P), rope_w[:, 0:P], rope_w[:, P:2 * P])):
                        ins = pe.matmul(bank(BA, j * P, j * P + P), wt, HT[:, par, :], start=True, stop=True)
                elif kind in (SELF, WINDOW):
                    pe.matmul(bank(BA, 128, 256), w(l, "qkv", 0), HT[:, par, :], start=True, stop=True)
                    ins = pe.matmul(bank(BA, 256, 384), w(l, "qkv", P), HT[:, par, :], start=True, stop=True)
                else:
                    pe.wait_ge(h_ready.sem, h_ready.count(p, b, 1))
                    pe.matmul(bank(BA, 128, 256), w(l, "q"), HT[:, par, :], start=True, stop=True)
                    ins = pe.matmul(bank(BA, 256, 256 + n), w(l, "kv", 0), CS[:, par, :], start=True, stop=True)
                ins.then_inc(qk_proj.sem, 1)

            def scores(p, b, par, c):
                kind, l, n = PHASES[p], LAYER[p], nk(PHASES[p])
                pe.wait_ge(km_ready.sem, km_ready.count(p, b, c + 1))
                s_free(pe, p, b, c)
                o = bank(BS + c % 2, 0, CH * n)
                if kind == WINDOW:
                    for win in range(2):
                        at = WIN * win
                        ins = pe.matmul(PS[at:at + WIN, BS + c % 2, 0:CH * n], QK[:, par, 0, at:at + WIN],
                                        KM[:, par, CH * c:CH * c + CH, at:at + n], start=True, stop=True,
                                        skip_group_check=True)
                    ins.then_inc(s_done.sem, 1)
                    return
                masked = kind in (ROPE, CROSS)
                if isinstance(b, int) and b == 0 and c == 0 and masked:
                    pe.wait_ge(masks_ready, 2 if l == 0 else 4)
                ins = pe.matmul(o, QK[:, par, 0, :], KM[:, par, CH * c:CH * c + CH, 0:n], start=True,
                                stop=not masked)
                if kind == CROSS:
                    m = key_mask_b[0:1, 0 if l == 0 else 1, :].rearrange("p (b k) -> p b k", b=NB)
                    ins = pe.matmul(o, ones_b[:, :], m[:, b, :].unsqueeze(1).broadcast_to([1, CH, n]),
                                    start=False, stop=True)
                elif masked:
                    ins = pe.matmul(o, ident_b[:, :], self_mask_b[:, :].unsqueeze(1).broadcast_to([P, CH, P]),
                                    start=False, stop=True)
                ins.then_inc(s_done.sem, 1)

            def transposes(p, b, c):
                n, r = nk(PHASES[p]), c % 2
                if PHASES[p] == TOP:
                    pe.wait_ge(sel_ready.sem, sel_ready.count(p, b, c + 1))
                else:
                    pe.wait_ge(exp_done.sem, exp_done.count(p, b, c + 1))
                if isinstance(b, int) and b == 0 and c < 2 and p and PHASES[p - 1] in MLPS:
                    ev = glu_ready if PHASES[p - 1] == GLU else act_done
                    pe.wait_ge(ev.sem, ev.all_of(p - 1))
                wait(pe, pt_ready, pt_ready.count(p, b, c - 1))
                if PHASES[p] == WINDOW:
                    for i in range(CH // 2):
                        ins = pe.transpose(bank(BT + r, i * P, i * P + P), E[:, r, i, :], ident)
                    ins.then_inc(t_done.sem, 1)
                    return
                for j in range(CH):
                    ins = pe.transpose(bank(BT + r, j * P, j * P + P, n), E[:, r, j, 0:n], ident)
                ins.then_inc(t_done.sem, 1)

            def values(p, b, par, c):
                n, r = nk(PHASES[p]), c % 2
                pe.wait_ge(pt_ready.sem, pt_ready.count(p, b, c + 1))
                if c == 0:
                    wait(pe, oT_copied, oT_copied.count(p, b, 0))
                if PHASES[p] == WINDOW:
                    for i in range(CH // 2):
                        for win in range(2):
                            at = WIN * win
                            ins = pe.matmul(PS[64 * i:64 * i + 64, BO, c * P + at:c * P + at + WIN],
                                            VW[:, par, win, CH // 2 * c + i, :], PT[:, r, i, at:at + WIN],
                                            start=True, stop=True, skip_group_check=True)
                    ins.then_inc(pv_done.sem, 1)
                    return
                for j in range(CH):
                    ins = pe.matmul(PS[32 * j:32 * j + 32, BO, c * P:c * P + P], V[0:n, par, CH * c + j, :],
                                    PT[0:n, r, j, :], start=True, stop=True, skip_group_check=True)
                ins.then_inc(pv_done.sem, 1)

            def tail_transpose(p, b):
                pe.wait_ge(oT_copied.sem, oT_copied.count(p, b, 1))
                for c in range(NCH):
                    ins = pe.transpose(bank(BB, c * P, c * P + P), OT[:, c, :], ident)
                ins.then_inc(otr_done.sem, 1)

            def tail_on(p, b, prep):
                pe.wait_ge(on_ready.sem, on_ready.count(p, b, 1))
                pe.wait_ge(x_updated.sem, x_updated.count(p, b, 0))
                if PHASES[prep[0]] in HEADS:
                    pe.wait_ge(v_ready.sem, v_ready.count(*prep, 1))
                pe.transpose(bank(BC, 0, P), ON[:, :], ident).then_inc(onT_done.sem, 1)

            def tail_y(p, b):
                l = LAYER[p]
                pe.wait_ge(onT_ready.sem, onT_ready.count(p, b, 1))
                pe.matmul(bank(BC, 128, 256), w(l, "co" if PHASES[p] in CTX else "so"), ONT[:, :], start=True,
                          stop=True).then_inc(y_done.sem, 1)

            def fc1(p, b, par, half):
                kind, l = PHASES[p], LAYER[p]
                pe.wait_ge(h_ready.sem, h_ready.count(p, b, 1))
                if isinstance(b, int) and b == 0:
                    banks_left(pe, p)
                if par == 1:
                    pe.wait_ge(pt_ready.sem, pt_ready.all_of(p - 1))
                n = HID // 2
                blocks = [half * n + j for j in range(n)]
                if kind == GLU:
                    blocks += [HID + j for j in blocks]
                for i, j in enumerate(blocks):
                    ins = pe.matmul(bank(hidden_banks(par)[half], i * P, i * P + P), w(l, "m1", j * P),
                                    HT[:, par, :], start=True, stop=True)
                ins.then_inc(fc1_done.sem, 1)

            def fc2(p, b, par):
                kind, l = PHASES[p], LAYER[p]
                pe.wait_ge(x_updated.sem, x_updated.count(p, b, 0))
                if isinstance(b, int) and b == NB - 1 and PHASES[p + 1] in v_proj.rates:
                    pe.wait_ge(v_ready.sem, v_ready.count(p + 1, 0, 1))
                for j in range(HID):
                    if j % (HID // 2) == 0:
                        ready = glu_ready if kind == GLU else act_done
                        pe.wait_ge(ready.sem, ready.count(p, b, j // (HID // 2) + 1))
                    ins = pe.matmul(bank(BC, 128, 256), w(l, "m2", j * P), G[:, par, j, :], start=(j == 0),
                                    stop=(j == HID - 1))
                ins.then_inc(y_done.sem, 1)

            def tail_yT(p, b):
                pe.wait_ge(y_gated.sem, y_gated.count(p, b, 1))
                pe.transpose(bank(BC, 256, 384), Y[:, :], ident).then_inc(yT_done.sem, 1)

            def proto_scores(p, b, par):
                pe.wait_ge(qk_ready.sem, qk_ready.count(p, b, 1))
                if isinstance(b, int) and b == 0:
                    banks_left(pe, p)
                pe.matmul(bank(BS + par, 0, NC), QK[:, par, 0, :], QK[:, par, 1, 0:NC], start=True,
                          stop=True).then_inc(ps_done.sem, 1)
                pe.matmul(PS[:, BB, bass.ds(NE * b, NE)], HT[:, par, :], w(3, "router", 0, NE),
                          start=True, stop=True).then_inc(lx_done.sem, 1)

            def proto_transpose(p, b, par):
                pe.wait_ge(pw_ready.sem, pw_ready.count(p, b, 1))
                pe.transpose(bank(BT + par, 0, P, NC), E[:, par, 0, 0:NC], ident).then_inc(pwT_done.sem, 1)

            def proto_evidence(p, b, par):
                pe.wait_ge(pwT_ready.sem, pwT_ready.count(p, b, 1))
                pe.matmul(bank(BO, 0, P), V3[0:NC, par, :], PT[0:NC, par, 0, :], start=True,
                          stop=True).then_inc(ev_done.sem, 1)

            def proto_logits(p, b, par):
                pe.wait_ge(ev_ready.sem, ev_ready.count(p, b, 1))
                pe.matmul(PS[:, BB, bass.ds(NB * NE + NE * b, NE)], ES[:, par, :], w(3, "router", NE, NE),
                          start=True, stop=True).then_inc(lg_done.sem, 1)

            def expert_hidden(p, b, par, first, end):
                if isinstance(b, int) and b == 0:
                    banks_left(pe, p)
                    pe.wait_ge(ev_kept.sem, ev_kept.count(p - 1, 0, 1))
                    pe.wait_ge(nx_kept.sem, nx_kept.all_of(p - 1))
                if par == 1:
                    pe.wait_ge(pwT_ready.sem, pwT_ready.all_of(p - 1))
                    pe.wait_ge(ev_kept.sem, ev_kept.all_of(p - 1))
                for j in range(first, end):
                    o = bank(hidden_banks(par)[j // 4], j % 4 * P, j % 4 * P + P)
                    name, at = ("e1", j * 3 * P) if j < 6 else ("gate1", 0)
                    pe.matmul(o, w(3, name, at), NX[:, b, :], start=True, stop=False)
                    ins = pe.matmul(o, w(3, name, at + P), EV[:, b, :], start=False, stop=True)
                    if j in (3, 6):
                        ins.then_inc(eh_done.sem, 1)

            def expert_out(p, b, par):
                pe.wait_ge(eh_ready.sem, eh_ready.count(p, b, 2))
                pe.wait_ge(gb_ready.sem, gb_ready.count(p, b, 0))
                for e in range(NE):
                    for r in range(2):
                        pe.matmul(bank(BO, e * P, e * P + P), HE[:, par, 2 * e + r, :],
                                  w(3, "e2", (2 * e + r) * P), start=(r == 0), stop=(r == 1))
                pe.matmul(bank(BO, 384, 512), HE[:, par, 6, :], w(3, "gate2"), start=True,
                          stop=True).then_inc(ey_done.sem, 1)

            def mix_transpose(p, b, par):
                pe.wait_ge(mix_done.sem, mix_done.count(p, b, 3))
                pe.wait_ge(delta_done.sem, delta_done.count(p, b, 0))
                pe.transpose(bank(BC, 0, P), R3[:, par, :], ident).then_inc(rT_done.sem, 1)

            def mix_out(p, b):
                pe.wait_ge(rT_ready.sem, rT_ready.count(p, b, 1))
                pe.matmul(bank(BC, 128, 256), RT[:, :], w(3, "out"), start=True, stop=True).then_inc(r_done.sem, 1)

            def prep_only(p, b, par):
                pe.wait_ge(loaded["heads"], 16)
                pe.wait_ge(consts_ready, CONSTS)
                pe.wait_ge(params_ready, SETUP_DONE[0])
                xn_transpose(p, b, par)
                project_v(p, b, par, None)
                project_qk(p, b, par)
                scores(p, b, par, 0)

            def step(p, b, par, tail, prep):
                tk = PHASES[tail[0]] if tail else None
                pk = PHASES[prep[0]] if prep else None
                kind, other = PHASES[p], 1 - par
                if kind in MLPS:
                    mlp_step(p, b, par, tail, prep)
                    return
                if kind == TOP:
                    top_step(p, b, par, tail, prep)
                    return
                if kind == PROTO:
                    proto_step(p, b, par, tail, prep)
                    return
                if kind == EXPERTS:
                    experts_step(p, b, par, tail)
                    return
                if tk == TOP:
                    transposes(*tail, 2)
                if tk in HEADS:
                    values(*tail, other, 2)
                    transposes(*tail, 3)
                if tk in MLPS:
                    fc2(*tail, other)
                scores(p, b, par, 1)
                if tk in HEADS:
                    values(*tail, other, 3)
                scores(p, b, par, 2)
                xn_transpose(*prep, other)
                transposes(p, b, 0)
                if tk in MLPS:
                    tail_yT(*tail)
                if tk in HEADS:
                    tail_transpose(*tail)
                if pk in HEADS or pk == PROTO:
                    project_v(*prep, other, tail)
                    project_qk(*prep, other)
                values(p, b, par, 0)
                transposes(p, b, 1)
                scores(p, b, par, 3)
                if tk in HEADS:
                    tail_on(*tail, prep)
                values(p, b, par, 1)
                if tk in HEADS:
                    tail_y(*tail)
                transposes(p, b, 2)
                if pk in HEADS:
                    scores(*prep, other, 0)
                if tk in HEADS:
                    tail_yT(*tail)

            def mlp_step(p, b, par, tail, prep):
                tk, pk, other = PHASES[tail[0]], PHASES[prep[0]], 1 - par
                fc1(p, b, par, 0)
                if tk in MLPS:
                    fc2(*tail, other)
                    xn_transpose(*prep, other)
                    fc1(p, b, par, 1)
                    tail_yT(*tail)
                if tk in HEADS:
                    if tk == TOP:
                        transposes(*tail, 2)
                    values(*tail, other, 2)
                    transposes(*tail, 3)
                    xn_transpose(*prep, other)
                    fc1(p, b, par, 1)
                    values(*tail, other, 3)
                    tail_transpose(*tail)
                    tail_on(*tail, prep)
                    tail_y(*tail)
                    tail_yT(*tail)
                if pk in HEADS or pk == PROTO:
                    project_v(*prep, other, tail)
                    project_qk(*prep, other)
                if pk in HEADS:
                    scores(*prep, other, 0)

            def proto_step(p, b, par, tail, prep):
                tk, pk, other = PHASES[tail[0]], PHASES[prep[0]], 1 - par
                if pk == PROTO:
                    xn_transpose(*prep, other)
                proto_scores(p, b, par)
                if tk == PROTO:
                    proto_transpose(*tail, other)
                if tk in MLPS:
                    fc2(*tail, other)
                    tail_yT(*tail)
                if pk == PROTO:
                    project_v(*prep, other, tail)
                if tk == PROTO:
                    proto_evidence(*tail, other)
                if pk == PROTO:
                    project_qk(*prep, other)
                if tk == PROTO:
                    proto_logits(*tail, other)

            def experts_step(p, b, par, tail):
                if PHASES[tail[0]] == PROTO:
                    expert_hidden(p, b, par, 0, 4)
                    proto_transpose(*tail, 1 - par)
                    proto_evidence(*tail, 1 - par)
                    proto_logits(*tail, 1 - par)
                    expert_hidden(p, b, par, 4, 7)
                    return
                expert_hidden(p, b, par, 0, 2)
                expert_out(*tail, 1 - par)
                expert_hidden(p, b, par, 2, 6)
                mix_transpose(*tail, 1 - par)
                expert_hidden(p, b, par, 6, 7)
                mix_out(*tail)

            def top_step(p, b, par, tail, prep):
                pk, other = PHASES[prep[0]], 1 - par
                scores(p, b, par, 1)
                if PHASES[tail[0]] == TOP:
                    transposes(*tail, 2)
                transposes(*tail, 3)
                if pk in HEADS:
                    project_v(*prep, other, tail)
                xn_transpose(*prep, other)
                values(*tail, other, 2)
                scores(p, b, par, 2)
                values(*tail, other, 3)
                scores(p, b, par, 3)
                tail_transpose(*tail)
                if pk in HEADS:
                    project_qk(*prep, other)
                tail_on(*tail, prep)
                transposes(p, b, 0)
                tail_y(*tail)
                transposes(p, b, 1)
                tail_yT(*tail)
                values(p, b, par, 0)
                values(p, b, par, 1)
                if pk in HEADS:
                    scores(*prep, other, 0)

            def tail_only(p, b, par):
                expert_out(p, b, par)
                mix_transpose(p, b, par)
                mix_out(p, b)

            phases(pe.Fori, step, layer_setup, prep_only, tail_only)

        @block.vector
        def _(dve):
            dve.sem_inc(x_updated.sem, 1)
            dve.sem_inc(delta_done.sem, 1)
            dve.sem_inc(gb_ready.sem, 1)
            dve.memset(ones_b[:, :], 1.0).then_inc(consts_ready, 1)
            dve.memset(V[:, :, :, :], 0.0).then_inc(consts_ready, 1)
            dve.memset(PRM[:, 1, 0, :], 0.0).then_inc(consts_ready, 1)
            dve.memset(PRM[:, 1, 1:3, :], 1.0).then_inc(consts_ready, 1)
            dve.wait_ge(consts_ready, 5)
            dve.memset(V[:, :, :, HD:HD + 1], 1.0).then_inc(consts_ready, 1)
            dve.wait_ge(window_zeros, 1)
            for t in range(2):
                dve.memset(VW[WIN * t:WIN * t + WIN, :, :, :, 32 * t + HD:32 * t + HD + 1],
                           1.0).then_inc(window_zeros, 1)

            def convert_masks(l):
                dve.wait_ge(loaded["masks"], 48)
                if l == 0:
                    dve.tensor_scalar(key_mask_b[:, 0, :], key_mask_u[:, 0, :], REPLACED, 10.0, ALU.mult,
                                      ALU.mult).then_inc(masks_ready, 1)
                    dve.wait_ge(loaded["heads"], 16)
                    dve.tensor_copy(ident_b[:, :], ident).then_inc(masks_ready, 1)
                    return
                dve.tensor_scalar(key_mask_b[:, 1, :], key_mask_u[:, 1, :], -NEG, NEG, ALU.mult,
                                  ALU.add).then_inc(masks_ready, 1)
                dve.tensor_scalar(self_mask_b[:, :], self_mask_u[:, :], -NEG, NEG, ALU.mult,
                                  ALU.add).then_inc(masks_ready, 1)

            def layer_setup(l):
                done = SETUP_DONE[l - 1] if l else 0
                if l == 1:
                    convert_masks(1)
                    dve.wait_ge(window_zeros, 3)
                if l == 0:
                    dve.wait_ge(loaded["vectors"], 16)
                dve.wait_ge(ada_done, l + 1)
                if l == 3:
                    c = VCOL[3, "e1"]
                    dve.tensor_tensor(expert_bias[:, :, :], bank(BB, 0, 7 * NB).rearrange("p (j b) -> p j b", j=7),
                                      VEC[:, c:c + 7].unsqueeze(2).broadcast_to([P, 7, NB]),
                                      ALU.add).then_inc(params_ready, 1)
                    dve.wait_ge(loaded["rows"], 16)
                    dve.tensor_tensor(router_bias[:, :, :],
                                      bank(BB, 64, 64 + NB * NE).rearrange("p (b e) -> p b e", e=NE),
                                      rows_bc[:, 640:640 + NE].unsqueeze(1).broadcast_to([P, NB, NE]),
                                      ALU.add).then_inc(params_ready, 1)
                    c = VCOL[3, "beta"]
                    dve.tensor_copy(PRM[:, 9, 0:2, :],
                                    VEC[:, c:c + 2].unsqueeze(2).broadcast_to([P, 2, NB])).then_inc(params_ready, 1)
                    return
                n = 2 if l == 0 else 3
                mod = PRM[:, 0:3:2, :, :] if l == 0 else PRM[:, 3 * l:3 * l + 3, :, :]
                c = VCOL[l, "ada"]
                for s in range(n):
                    ins = dve.tensor_tensor(
                        mod[:, s, 0:3, :],
                        bank(BB, 3 * s * NB, 3 * s * NB + 3 * NB).rearrange("p (j b) -> p j b", j=3),
                        VEC[:, c + 3 * s:c + 3 * s + 3].unsqueeze(2).broadcast_to([P, 3, NB]), ALU.add)
                ins.then_inc(params_ready, 1)
                if l < 2:
                    c = VCOL[l, "so"]
                    dve.tensor_tensor(eff_bias[:, :], bank(BB, 128, 130), VEC[:, c:c + 2],
                                      ALU.add).then_inc(params_ready, 1)
                else:
                    dve.memset(PRM[:, 6:8, 3, :], 0.0).then_inc(params_ready, 1)
                dve.wait_ge(params_ready, done + 2)
                if l == 2:
                    c = VCOL[2, "norm"]
                    dve.scalar_tensor_tensor(mod[:, :, 1, :], mod[:, :, 1, :], 1.0,
                                             VEC[:, c:c + 3].unsqueeze(2).broadcast_to([P, 3, NB]), ALU.add,
                                             ALU.mult).then_inc(params_ready, 1)
                else:
                    dve.tensor_scalar(mod[:, :, 1, :], mod[:, :, 1, :], 1.0, None,
                                      ALU.add).then_inc(params_ready, 1)
                    dve.tensor_tensor(PRM[:, 3 * l:3 * l + 2, 3, :], PRM[:, 3 * l:3 * l + 2, 2, :],
                                      eff_bias[:, :].unsqueeze(2).broadcast_to([P, 2, NB]),
                                      ALU.mult).then_inc(params_ready, 1)
                dve.tensor_scalar(PRM[:, 3 * l + 2, 3, :], PRM[:, 3 * l + 2, 2, :], vcol(l, "m2"), None,
                                  ALU.mult).then_inc(params_ready, 1)
                if l == 2:
                    dve.wait_ge(loaded["tables"], 16)
                    dve.wait_ge(loaded["w2"], 16)
                    src = w(2, "qkv", 0, 2 * P).rearrange("p (h t d) -> p h t d", t=2, d=HD // 2)
                    dst = rope_w[:, :].rearrange("p (h t d) -> p h t d", t=2, d=HD // 2)
                    dve.tensor_scalar(dst[:, :, 0, :], src[:, :, 1, :], -1.0, None,
                                      ALU.mult).then_inc(params_ready, 1)
                    dve.tensor_copy(dst[:, :, 1, :], src[:, :, 0, :]).then_inc(params_ready, 1)

            def statistics(p, b, par):
                if not (p == 0 and b < 2):
                    wait(dve, rstd_done, rstd_done.count(p, b, -3))
                if p:
                    dve.wait_ge(x_updated.sem, x_updated.count(p - 1, b, 1))
                    dve.sem_inc(passed_dve, 1)
                dve.bn_stats(stats[:, par, :], X[:, b, :]).then_inc(stats_done.sem, 1)
                dve.wait_ge(stats_done.sem, stats_done.count(p, b, 1))
                dve.sem_inc(passed_dve, 1)
                dve.bn_aggr(mean_var[:, par, :], stats[:, par, :]).then_inc(stats_done.sem, 1)

            def normalise(p, b, par):
                dve.wait_ge(rstd_done.sem, rstd_done.count(p, b, 3))
                dve.tensor_scalar(XN[:, par, :], X[:, b, :], mean[:, bass.ds(b, 1)], rstd[:, bass.ds(b, 1)],
                                  ALU.subtract, ALU.mult).then_inc(xn_ready.sem, 1)

            def copy_v(p, b, par):
                n = nk(PHASES[p])
                dve.wait_ge(v_proj.sem, v_proj.count(p, b, 1))
                if PHASES[p] == PROTO:
                    wait(dve, ev_done, ev_done.count(p, b, -1))
                    dve.tensor_copy(V3[0:n, par, :], bank(BC, 384, 512, n)).then_inc(v_ready.sem, 1)
                elif PHASES[p] == WINDOW:
                    for t in range(2):
                        ins = dve.tensor_copy(
                            VW[WIN * t:WIN * t + WIN, par, :, :, 32 * t:32 * t + HD],
                            PS[WIN * t:WIN * t + WIN, BC, 384:512].rearrange("p (w i d) -> p w i d", w=2, d=HD))
                    ins.then_inc(v_ready.sem, 1)
                else:
                    dve.tensor_copy(V[0:n, par, :, 0:HD],
                                    bank(BC, 384, 512, n).rearrange("p (h d) -> p h d", h=H)).then_inc(v_ready.sem, 1)

            def rope(p, b):
                dve.wait_ge(qk_proj.sem, qk_proj.count(p, b, 1))
                wait(dve, rope_ready, rope_ready.count(p, b, 0))
                for i, at in ((0, C_COS), (1, C_SIN)):
                    ins = dve.tensor_tensor(
                        rope_prod[:, i, :, :], bank(BA, 256 * i, 256 * i + 256).rearrange("p (t q) -> p t q", t=2),
                        CONST[:, at:at + P].unsqueeze(1).broadcast_to([P, 2, P]), ALU.mult)
                ins.then_inc(rope_mults.sem, 1)

            def maxima(p, b, c):
                n, r = nk(PHASES[p]), c % 2
                dve.wait_ge(s_done.sem, s_done.count(p, b, c + 1))
                dve.tensor_reduce(MX[:, r, :], bank(BS + r, 0, CH * n).rearrange("p (h k) -> p h k", h=CH), AX.X,
                                  ALU.max).then_inc(max_done.sem, 1)

            def subtract(p, b, c):
                n, r = nk(PHASES[p]), c % 2
                dve.wait_ge(max_done.sem, max_done.count(p, b, c + 1))
                wait(dve, exp_done, exp_done.count(p, b, c - 1))
                dve.tensor_tensor(D[:, r, :, 0:n], bank(BS + r, 0, CH * n).rearrange("p (h k) -> p h k", h=CH),
                                  MX[:, r, :].unsqueeze(2).broadcast_to([P, CH, n]),
                                  ALU.subtract).then_inc(sub_done.sem, 1)

            def first_8(p, b, c):
                r = c % 2
                dve.wait_ge(s_done.sem, s_done.count(p, b, c + 1))
                dve.sem_inc(passed_dve, 1)
                for j in range(CH):
                    ins = dve.max(top8a[:, r, j, :], bank(BS + r, j * NC, j * NC + NC))
                ins.then_inc(top_a.sem, 1)

            def replace_first(p, b, c):
                r = c % 2
                dve.wait_ge(top_a.sem, top_a.count(p, b, c + 1))
                wait(dve, exp1_done, exp1_done.count(p, b, c - 1))
                dve.tensor_scalar(MX[:, r, :], top8a[:, r, :, 0], -SCALE, None, ALU.mult).then_inc(negm_ready.sem, 1)
                for j in range(CH):
                    ins = dve.match_replace(out=left_a[:, r, j, :], in_to_replace=top8a[:, r, j, :],
                                            in_values=bank(BS + r, j * NC, j * NC + NC), imm_value=REPLACED)
                ins.then_inc(left_a_ready.sem, 1)

            def next_8(p, b, c):
                r = c % 2
                dve.wait_ge(left_a_ready.sem, left_a_ready.count(p, b, c + 1))
                dve.sem_inc(passed_dve, 1)
                for j in range(CH):
                    ins = dve.max(top8b[:, r, j, :], left_a[:, r, j, :])
                ins.then_inc(top_b.sem, 1)

            def replace_next(p, b, c):
                r = c % 2
                dve.wait_ge(top_b.sem, top_b.count(p, b, c + 1))
                dve.sem_inc(passed_dve, 1)
                for j in range(CH):
                    ins = dve.match_replace(out=left_b[:, r, j, :], in_to_replace=top8b[:, r, j, :],
                                            in_values=left_a[:, r, j, :], imm_value=REPLACED)
                ins.then_inc(left_b_ready.sem, 1)

            def mark_taken(p, b, c):
                r = c % 2
                dve.wait_ge(left_b_ready.sem, left_b_ready.count(p, b, c + 1))
                wait(dve, sel_ready, sel_ready.count(p, b, c - 1))
                dve.tensor_scalar(taken[:, r, :, :], left_b[:, r, :, :], 0.5 * REPLACED, None,
                                  ALU.is_le).then_inc(taken_ready.sem, 1)

            def norm_out(p, b):
                dve.wait_ge(otr_done.sem, otr_done.count(p, b, 1))
                o = bank(BB, 0, 512).rearrange("p (h e) -> p h e", e=32)
                dve.reciprocal(rsum[:, :], o[:, :, HD]).then_inc(rsum_ready.sem, 1)
                dve.wait_ge(rsum_ready.sem, rsum_ready.count(p, b, 1))
                dve.tensor_tensor(ON[:, :].rearrange("p (h d) -> p h d", d=HD), o[:, :, 0:HD],
                                  rsum[:, :].unsqueeze(2).broadcast_to([P, H, HD]),
                                  ALU.mult).then_inc(on_ready.sem, 1)

            def gate_dve(p, b):
                dve.wait_ge(y_done.sem, y_done.count(p, b, 1))
                dve.tensor_scalar(Y[:, :], bank(BC, 128, 256), PRM[:, p, 2, bass.ds(b, 1)],
                                  PRM[:, p, 3, bass.ds(b, 1)], ALU.mult, ALU.add).then_inc(y_gated.sem, 1)

            def residual(p, b):
                dve.wait_ge(yT_done.sem, yT_done.count(p, b, 1))
                dve.tensor_tensor(X[:, b, :], X[:, b, :], bank(BC, 256, 384), ALU.add).then_inc(x_updated.sem, 1)

            def glu(p, b, par, half):
                dve.wait_ge(act_done.sem, act_done.count(p, b, half + 1))
                n = HID // 2
                for i in range(n):
                    j = half * n + i
                    ins = dve.scalar_tensor_tensor(
                        G[:, par, j, :], bank(hidden_banks(par)[half], (n + i) * P, (n + i) * P + P),
                        vcol(1, "m1", HID + j), SG[:, par, j, :], ALU.add, ALU.mult)
                ins.then_inc(glu_ready.sem, 1)

            def proto_softmax(p, b, par):
                dve.wait_ge(ps_done.sem, ps_done.count(p, b, 1))
                dve.tensor_reduce(MX[:, par, 0:1], bank(BS + par, 0, NC), AX.X, ALU.max).then_inc(pmax_done.sem, 1)
                dve.wait_ge(pmax_done.sem, pmax_done.count(p, b, 1))
                dve.tensor_scalar(D[:, par, 0, 0:NC], bank(BS + par, 0, NC), MX[:, par, 0:1], None,
                                  ALU.subtract).then_inc(psub_done.sem, 1)
                dve.wait_ge(pexp_done.sem, pexp_done.count(p, b, 1))
                dve.reciprocal(sum3[:, par, 1:2], sum3[:, par, 0:1]).then_inc(prec_done.sem, 1)
                dve.wait_ge(prec_done.sem, prec_done.count(p, b, 1))
                dve.tensor_scalar(E[:, par, 0, 0:NC], E[:, par, 0, 0:NC], sum3[:, par, 1:2], None,
                                  ALU.mult).then_inc(pw_ready.sem, 1)

            def router_softmax():
                p = PHASES.index(PROTO)
                dve.wait_ge(lx_done.sem, lx_done.all_of(p))
                dve.wait_ge(lg_done.sem, lg_done.all_of(p))
                dve.tensor_tensor(router_bias[:, :, :], bank(BB, 0, NB * NE).rearrange("p (b e) -> p b e", e=NE),
                                  router_bias[:, :, :], ALU.add).then_inc(router_done, 1)
                dve.wait_ge(router_done, 1)
                dve.tensor_tensor(PR[:, :, :], bank(BB, NB * NE, 2 * NB * NE).rearrange("p (b e) -> p b e", e=NE),
                                  router_bias[:, :, :], ALU.add).then_inc(router_done, 1)
                dve.wait_ge(router_done, 2)
                dve.tensor_reduce(rt[:, 0, :], PR[:, :, :], AX.X, ALU.max).then_inc(router_done, 1)
                dve.wait_ge(router_done, 3)
                dve.tensor_tensor(PR[:, :, :], PR[:, :, :], rt[:, 0, :].unsqueeze(2).broadcast_to([P, NB, NE]),
                                  ALU.subtract).then_inc(router_done, 1)
                dve.wait_ge(router_exp, 1)
                dve.tensor_reduce(rt[:, 1, :], PR[:, :, :], AX.X, ALU.add).then_inc(router_done, 1)
                dve.wait_ge(router_done, 5)
                dve.reciprocal(rt[:, 2, :], rt[:, 1, :]).then_inc(router_done, 1)
                dve.wait_ge(router_done, 6)
                dve.tensor_tensor(PR[:, :, :], PR[:, :, :], rt[:, 2, :].unsqueeze(2).broadcast_to([P, NB, NE]),
                                  ALU.mult).then_inc(router_done, 1)
                dve.wait_ge(router_done, 7)

            def expert_tail(p, b, par):
                dve.wait_ge(ey_done.sem, ey_done.count(p, b, 1))
                dve.wait_ge(bm_ready.sem, bm_ready.count(p, b, 1))
                dve.scalar_tensor_tensor(R3[:, par, :], bank(BO, 0, P), PR[:, b, 0:1], BM[:, par, :], ALU.mult,
                                         ALU.add).then_inc(mix_done.sem, 1)
                for e in (1, 2):
                    dve.wait_ge(mix_done.sem, mix_done.count(p, b, e))
                    dve.scalar_tensor_tensor(R3[:, par, :], bank(BO, e * P, e * P + P), PR[:, b, e:e + 1],
                                             R3[:, par, :], ALU.mult, ALU.add).then_inc(mix_done.sem, 1)
                dve.tensor_tensor(GB[:, :], bank(BO, 384, 512), rows_bc[:, 384:512], ALU.add).then_inc(gb_ready.sem, 1)
                dve.wait_ge(r_done.sem, r_done.count(p, b, 1))
                dve.tensor_tensor(D3[:, par, :], bank(BC, 128, 256), rows_bc[:, 512:640],
                                  ALU.add).then_inc(delta_done.sem, 1)
                dve.wait_ge(tanh_ready.sem, tanh_ready.count(p, b, 1))
                dve.wait_ge(delta_done.sem, delta_done.count(p, b, 1))
                dve.scalar_tensor_tensor(D3[:, par, :], TH[:, :], 1.0, D3[:, par, :], ALU.add,
                                         ALU.mult).then_inc(delta_done.sem, 1)
                dve.wait_ge(delta_done.sem, delta_done.count(p, b, 2))
                dve.scalar_tensor_tensor(X[:, b, :], D3[:, par, :], 0.5, X[:, b, :], ALU.mult,
                                         ALU.add).then_inc(x_final.sem, 1)

            def prep_only(p, b, par):
                normalise(p, b, par)
                dve.wait_ge(loaded["x_rest"], 16)
                for i in range(NB // 2, NB):
                    statistics(0, i, i % 2)
                convert_masks(0)
                copy_v(p, b, par)
                maxima(p, b, 0)
                subtract(p, b, 0)

            def step(p, b, par, tail, prep):
                tk = PHASES[tail[0]] if tail else None
                pk = PHASES[prep[0]] if prep else None
                kind, other = PHASES[p], 1 - par
                if kind == TOP:
                    top_step(p, b, par, tail, prep)
                    return
                if kind not in SOFTMAX:
                    other_step(p, b, par, tail, prep)
                    return
                normalise(*prep, other)
                maxima(p, b, 1)
                if tk in MLPS:
                    gate_dve(*tail)
                subtract(p, b, 1)
                if tk in MLPS:
                    residual(*tail)
                    statistics(tail[0] + 1, tail[1], other)
                maxima(p, b, 2)
                if tk in HEADS:
                    norm_out(*tail)
                subtract(p, b, 2)
                if pk in HEADS or pk == PROTO:
                    copy_v(*prep, other)
                if pk == ROPE:
                    rope(*prep)
                maxima(p, b, 3)
                subtract(p, b, 3)
                if pk in SOFTMAX:
                    maxima(*prep, 0)
                if tk in HEADS:
                    residual(*tail)
                if pk in SOFTMAX:
                    subtract(*prep, 0)
                if tk in HEADS:
                    statistics(tail[0] + 1, tail[1], other)

            def other_step(p, b, par, tail, prep):
                tk = PHASES[tail[0]] if tail else None
                pk = PHASES[prep[0]] if prep else None
                kind, other = PHASES[p], 1 - par
                if pk and pk != EXPERTS:
                    normalise(*prep, other)
                if kind == GLU:
                    glu(p, b, par, 0)
                if tk in MLPS:
                    gate_dve(*tail)
                    residual(*tail)
                if kind == GLU:
                    glu(p, b, par, 1)
                if tk in MLPS:
                    statistics(tail[0] + 1, tail[1], other)
                if kind == PROTO:
                    proto_softmax(p, b, par)
                if tk in HEADS:
                    norm_out(*tail)
                if pk in HEADS or pk == PROTO:
                    copy_v(*prep, other)
                if pk == ROPE:
                    rope(*prep)
                if tk in HEADS:
                    residual(*tail)
                    statistics(tail[0] + 1, tail[1], other)
                if pk in SOFTMAX:
                    maxima(*prep, 0)
                    subtract(*prep, 0)
                if tk == PROTO and kind == EXPERTS:
                    router_softmax()
                if tk == EXPERTS:
                    expert_tail(*tail, other)

            def top_step(p, b, par, tail, prep):
                first_8(p, b, 0)
                first_8(p, b, 1)
                normalise(*prep, 1 - par)
                replace_first(p, b, 0)
                replace_first(p, b, 1)
                next_8(p, b, 0)
                next_8(p, b, 1)
                replace_next(p, b, 0)
                replace_next(p, b, 1)
                mark_taken(p, b, 0)
                mark_taken(p, b, 1)
                first_8(p, b, 2)
                first_8(p, b, 3)
                norm_out(*tail)
                if PHASES[prep[0]] in HEADS:
                    copy_v(*prep, 1 - par)
                replace_first(p, b, 2)
                replace_first(p, b, 3)
                next_8(p, b, 2)
                next_8(p, b, 3)
                replace_next(p, b, 2)
                residual(*tail)
                replace_next(p, b, 3)
                mark_taken(p, b, 2)
                statistics(tail[0] + 1, tail[1], 1 - par)
                mark_taken(p, b, 3)

            def tail_only(p, b, par):
                expert_tail(p, b, par)

            dve.wait_ge(loaded["x"], 16)
            for b in range(NB // 2):
                statistics(0, b, b % 2)
            phases(dve.Fori, step, layer_setup, prep_only, tail_only)


SETUP_IN = {2: (1,), 5: (2,), 8: (3,)}
SETUP_DONE = [5, 10, 16, 19]
CONSTS = 6


def pack(inputs):
    def a(name):
        return np.asarray(inputs[name])

    def rows(m):
        k = m.shape[0] // P
        return m.reshape(k, P, -1).transpose(1, 0, 2).reshape(P, -1)

    L0, L1, L2, L3 = "L0_xcond_", "L1_xcond_", "L2_xcond_", "L3_xcond_"
    w0 = [a(L0 + n) for n in ("ada_w", "qkv_w", "sa_proj_w", "q_w", "kv_w", "ca_proj_w", "fc1_w")] + [
        rows(a(L0 + "fc2_w"))]
    w1 = [a(L1 + n) for n in ("w_ada", "w_qkv", "w_so", "w_q", "w_kv", "w_co", "w_m1")] + [rows(a(L1 + "w_m2"))]
    w2 = [a(L2 + n) for n in ("adaLN_W", "qkv_W", "attn_out_W", "cq_W", "ck_W", "cv_W", "co_W", "mlp_W1")] + [
        rows(a(L2 + "mlp_W2"))]
    e1 = a(L3 + "e_w1").reshape(NE, 3, P, 2, P).transpose(2, 0, 3, 1, 4).reshape(P, -1)
    e2 = a(L3 + "e_w2").reshape(NE * 2, P, P).transpose(1, 0, 2).reshape(P, -1)
    w3 = [a(L3 + n) for n in ("Wq", "Wk", "Wv")] + [rows(a(L3 + "router_W")), rows(a(L3 + "gate_w1")), e1, e2,
                                                     a(L3 + "gate_w2"), a(L3 + "out_w")]
    weights = [np.ascontiguousarray(np.concatenate(x, axis=1)) for x in (w0, w1, w2, w3)]
    names = {
        (0, "ada"): L0 + "ada_b", (0, "qkv"): L0 + "qkv_b", (0, "so"): L0 + "sa_proj_b", (0, "q"): L0 + "q_b",
        (0, "kv"): L0 + "kv_b", (0, "co"): L0 + "ca_proj_b", (0, "m1"): L0 + "fc1_b", (0, "m2"): L0 + "fc2_b",
        (1, "ada"): L1 + "b_ada", (1, "qkv"): L1 + "b_qkv", (1, "so"): L1 + "b_so", (1, "q"): L1 + "b_q",
        (1, "kv"): L1 + "b_kv", (1, "co"): L1 + "b_co", (1, "m1"): L1 + "b_m1", (1, "m2"): L1 + "b_m2",
        (2, "ada"): L2 + "adaLN_b", (2, "m1"): L2 + "mlp_b1", (2, "m2"): L2 + "mlp_b2",
        (3, "gamma"): L3 + "ln_gamma", (3, "beta"): L3 + "ln_beta", (3, "e1"): L3 + "e_b1",
        (3, "gate1"): L3 + "gate_b1"}
    cols = []
    for n, l, c in VECTORS:
        if (l, n) == (2, "norm"):
            v = np.concatenate([a(L2 + "norm1_w"), a(L2 + "normc_w"), a(L2 + "norm2_w")])
        else:
            v = a(names[l, n]).reshape(-1)
        cols.append(v.reshape(c, P).T)
    vec = np.ascontiguousarray(np.concatenate(cols, axis=1))
    rows5 = np.ascontiguousarray(np.concatenate(
        [a(L3 + "e_b2").reshape(-1), a(L3 + "gate_b2"), a(L3 + "out_b"), a(L3 + "router_b")]))
    return dict(
        x=np.ascontiguousarray(a("x").transpose(1, 0, 2)),
        ctx=np.ascontiguousarray(a("ctx_1024").transpose(2, 0, 1)),
        cond=np.ascontiguousarray(a("cond_1024").T),
        vec=vec, consts=constants(), rows=rows5,
        key_mask0=np.ascontiguousarray(a("mask_BxS2_bf0")).reshape(1, -1),
        key_mask2=np.ascontiguousarray(a("mask_BxS2_bf1")).reshape(1, -1),
        self_mask=np.ascontiguousarray(a("mask_SxS_bk0")),
        w0=weights[0], w1=weights[1], w2=weights[2], w3=weights[3])


def constants():
    c = np.zeros((P, NCONST), np.float32)
    c[:, C_ID:C_ID + P] = np.eye(P, dtype=np.float32)
    c[np.arange(P), C_HEAD + np.arange(P) // HD] = 1.0
    inv_freq = 1.0 / 10000.0 ** (np.arange(0, HD, 2, dtype=np.float32) / HD)
    freqs = np.outer(np.arange(P // 2, dtype=np.float32), inv_freq)
    emb = np.concatenate([freqs, freqs], axis=-1)
    c[:, C_COS:C_COS + P] = np.tile(np.cos(emb).astype(np.float32).T, (H, 2))
    c[:, C_SIN:C_SIN + P] = np.tile(np.sin(emb).astype(np.float32).T, (H, 2))
    return c


def kernel(**inputs):
    import concourse.bacc as bacc
    from concourse.bass_utils import run_bass_kernel_spmd

    nc = bacc.Bacc("TRN2", target_bir_lowering=False, num_devices=1)
    arrays, aps = {}, {}
    for name, arr in pack(inputs).items():
        arrays["in_" + name] = arr
        aps[name] = nc.dram_tensor("in_" + name, arr.shape, mybir.dt.from_np(arr.dtype), kind="ExternalInput").ap()
    out = nc.dram_tensor("out", (NB, P, P), mybir.dt.float32, kind="ExternalOutput").ap()
    build(nc, aps["x"], aps["ctx"], aps["cond"], aps["vec"], aps["consts"], aps["rows"], aps["key_mask0"],
          aps["key_mask2"], aps["self_mask"], [aps[f"w{l}"] for l in range(4)], out)
    r = run_bass_kernel_spmd(nc, [arrays], core_ids=[0])
    return r.results[0]["out"]
```
